# Optimizing a Trainium2 kernel written in Bass

```python
import numpy as np
import jax
import jax.numpy as jnp

def _softmax(x, axis=-1):
    return jax.nn.softmax(x, axis=axis)

def _gelu(x):
    return jax.nn.gelu(x, approximate=True)

def _silu(x):
    return jax.nn.silu(x)

def _sigmoid(x):
    return jax.nn.sigmoid(x)

def _layernorm(x, axis=-1, eps=1e-05):
    m = jnp.mean(x, axis=axis, keepdims=True)
    v = jnp.var(x, axis=axis, keepdims=True)
    return (x - m) / jnp.sqrt(v + eps)

def _scatter_add(tgt, idx, src, axis=0):
    return tgt.at[idx].add(src)

def _segment_sum(src, seg, n):
    return jax.ops.segment_sum(src, seg, n)
kernel_name = 'mk_gnn_ffn_d2_gnn_r8_078fe2'

def setup_inputs(seed: int=0):
    np.random.seed(seed)
    _w = jnp.asarray

    def _rec_inputs():
        import jax
        import jax.numpy as jnp
        _gk = jax.random.key(seed)
        x = -0.0006008 + 1.001 * jax.random.normal(jax.random.fold_in(_gk, 1), (6250, 256), jnp.float32)
        _s = jax.random.randint(jax.random.fold_in(_gk, 2), (50000,), 0, 6250, jnp.int32)
        _d = jax.random.randint(jax.random.fold_in(_gk, 3), (50000,), 0, 6250, jnp.int32)
        _loop = jnp.arange(6250, dtype=jnp.int32)
        src = jnp.concatenate([_s, _d, _loop])
        dst = jnp.concatenate([_d, _s, _loop])
        _o = jnp.argsort(dst, stable=True)
        src = src[_o]
        dst = dst[_o]
        edge_weight = jax.random.uniform(jax.random.fold_in(_gk, 12), (106250,), jnp.float32, 0.0, 1)
        edge_weight1 = jax.random.uniform(jax.random.fold_in(_gk, 13), (106250, 1), jnp.float32, 0.0, 0.999994)
        return (x, src, dst, edge_weight, edge_weight1)
    x, src, dst, edge_weight, edge_weight1 = _rec_inputs()

    def _L0_gnn_setup():
        import jax, jax.numpy as jnp
        import numpy as np
        N_NODES = 1250
        N_EDGES = 40000
        D_IN = 256
        D_OUT = 256
        key = jax.random.key(seed)
        k1, k2, k3, k4, k5, k6 = jax.random.split(key, 6)
        feat = jax.random.normal(k1, (N_NODES, D_IN), dtype=jnp.float32)
        eweight = jax.random.uniform(k2, (N_EDGES, 1), dtype=jnp.float32)
        W = jax.random.normal(k3, (D_OUT, 2 * D_IN), dtype=jnp.float32) / np.sqrt(2 * D_IN)
        b = jax.random.normal(k4, (D_OUT,), dtype=jnp.float32) * 0.01
        src = jax.random.randint(k5, (N_EDGES,), 0, N_NODES, dtype=jnp.int64)
        dst = jax.random.randint(k6, (N_EDGES,), 0, N_NODES, dtype=jnp.int64)
        return {'feat': feat, 'eweight': eweight, 'W': W, 'b': b, 'src': src, 'dst': dst}
    _L0_gnn_all = _L0_gnn_setup()
    _L0_gnn_in = {k: v for k, v in _L0_gnn_all.items() if k in ('W', 'b')}
    del _L0_gnn_all

    def _L0_ffn_setup():
        import jax, jax.numpy as jnp
        import numpy as np
        D_MODEL = 256
        EXPERT_DIM = 512
        NUM_EXPERTS = 8
        TOP_K = 2
        SEQ_LEN = 256
        BATCH = 2
        key = jax.random.key(seed)
        ks = jax.random.split(key, 8)
        s = 0.02
        x = jax.random.normal(ks[0], (SEQ_LEN, BATCH, D_MODEL), dtype=jnp.float32)
        Wg = jax.random.normal(ks[1], (D_MODEL, NUM_EXPERTS), dtype=jnp.float32) * s
        bg = jax.random.normal(ks[2], (NUM_EXPERTS,), dtype=jnp.float32) * s
        bias = jnp.zeros((NUM_EXPERTS,), dtype=jnp.float32)
        W1 = jax.random.normal(ks[3], (NUM_EXPERTS, D_MODEL, EXPERT_DIM), dtype=jnp.float32) * s
        b1 = jax.random.normal(ks[4], (NUM_EXPERTS, EXPERT_DIM), dtype=jnp.float32) * s
        W2 = jax.random.normal(ks[5], (NUM_EXPERTS, EXPERT_DIM, D_MODEL), dtype=jnp.float32) * s
        b2 = jax.random.normal(ks[6], (NUM_EXPERTS, D_MODEL), dtype=jnp.float32) * s
        return {'x': x, 'Wg': Wg, 'bg': bg, 'bias': bias, 'W1': W1, 'b1': b1, 'W2': W2, 'b2': b2}
    _L0_ffn_all = _L0_ffn_setup()
    _L0_ffn_in = {k: v for k, v in _L0_ffn_all.items() if k in ('Wg', 'bg', 'bias', 'W1', 'b1', 'W2', 'b2')}
    del _L0_ffn_all

    def _L1_gnn_setup():
        import jax, jax.numpy as jnp
        import numpy as np
        MU = 2.0
        key = jax.random.key(seed)
        ks = jax.random.split(key, 8)
        N, E, IN, P, OUT = (12500, 200000, 256, 128, 256)
        x = jax.random.normal(ks[0], (N, IN), dtype=jnp.float32)
        edge_vals = jnp.ones((E,), dtype=jnp.float32)
        Wp = jax.random.normal(ks[1], (P, IN), dtype=jnp.float32) * (1.0 / np.sqrt(IN))
        bp = jnp.zeros((P,), dtype=jnp.float32)
        W1 = jax.random.normal(ks[2], (OUT, P), dtype=jnp.float32) * (1.0 / np.sqrt(P))
        b1 = jnp.zeros((OUT,), dtype=jnp.float32)
        W2 = jax.random.normal(ks[3], (OUT, P), dtype=jnp.float32) * (1.0 / np.sqrt(P))
        b2 = jnp.zeros((OUT,), dtype=jnp.float32)
        src = jax.random.randint(ks[4], (E,), 0, N, dtype=jnp.int32)
        dst = jax.random.randint(ks[5], (E,), 0, N, dtype=jnp.int32)
        return {'x': x, 'edge_vals': edge_vals, 'Wp': Wp, 'bp': bp, 'W1': W1, 'b1': b1, 'W2': W2, 'b2': b2, 'src': src, 'dst': dst}
    _L1_gnn_all = _L1_gnn_setup()
    _L1_gnn_in = {k: v for k, v in _L1_gnn_all.items() if k in ('Wp', 'bp', 'W1', 'b1', 'W2', 'b2')}
    del _L1_gnn_all

    def _L1_ffn_setup():
        import jax, jax.numpy as jnp
        import numpy as np
        NUM_EXPERTS = 8
        TOP_K = 2
        B, S, D = (8, 1024, 256)

        def _moe(tokens, router_w, w1, b1, w2, b2):
            N = tokens.shape[0]
            E = router_w.shape[0]
            logits = tokens.astype(jnp.float32) @ router_w.astype(jnp.float32).T
            probs = jax.nn.softmax(logits, axis=-1)
            rw, re = jax.lax.top_k(probs, TOP_K)
            if TOP_K > 1:
                rw = rw / jnp.maximum(rw.sum(-1, keepdims=True), 1e-12)
            rw = rw.astype(tokens.dtype)
            combine = jnp.zeros((N, E), tokens.dtype).at[jnp.arange(N)[:, None], re].set(rw)
            out = tokens
            for e in range(E):
                h = jax.nn.gelu(tokens @ w1[e] + b1[e], approximate=False)
                y = h @ w2[e] + b2[e]
                out = out + combine[:, e:e + 1] * y
            return out
        key = jax.random.key(seed)
        ks = jax.random.split(key, 4)
        scale = 1.0 / np.sqrt(D).astype(np.float32)
        return {'input_embeddings': jax.random.normal(ks[0], (B, S, D), jnp.float32), 'router_w': jax.random.normal(ks[1], (NUM_EXPERTS, D), jnp.float32) * scale, 'w1': jax.random.normal(ks[2], (NUM_EXPERTS, D, D), jnp.float32) * scale, 'b1': jnp.zeros((NUM_EXPERTS, D), jnp.float32), 'w2': jax.random.normal(ks[3], (NUM_EXPERTS, D, D), jnp.float32) * scale, 'b2': jnp.zeros((NUM_EXPERTS, D), jnp.float32)}
    _L1_ffn_all = _L1_ffn_setup()
    _L1_ffn_in = {k: v for k, v in _L1_ffn_all.items() if k in ('router_w', 'w1', 'b1', 'w2', 'b2')}
    del _L1_ffn_all
    return {'x': x, 'src': src, 'dst': dst, 'edge_weight': edge_weight, 'edge_weight1': edge_weight1, 'L0_gnn_W': _L0_gnn_in['W'], 'L0_gnn_b': _L0_gnn_in['b'], 'L0_ffn_Wg': _L0_ffn_in['Wg'], 'L0_ffn_bg': _L0_ffn_in['bg'], 'L0_ffn_bias': _L0_ffn_in['bias'], 'L0_ffn_W1': _L0_ffn_in['W1'], 'L0_ffn_b1': _L0_ffn_in['b1'], 'L0_ffn_W2': _L0_ffn_in['W2'], 'L0_ffn_b2': _L0_ffn_in['b2'], 'L1_gnn_Wp': _L1_gnn_in['Wp'], 'L1_gnn_bp': _L1_gnn_in['bp'], 'L1_gnn_W1': _L1_gnn_in['W1'], 'L1_gnn_b1': _L1_gnn_in['b1'], 'L1_gnn_W2': _L1_gnn_in['W2'], 'L1_gnn_b2': _L1_gnn_in['b2'], 'L1_ffn_router_w': _L1_ffn_in['router_w'], 'L1_ffn_w1': _L1_ffn_in['w1'], 'L1_ffn_b1': _L1_ffn_in['b1'], 'L1_ffn_w2': _L1_ffn_in['w2'], 'L1_ffn_b2': _L1_ffn_in['b2']}

def reference(x, src, dst, edge_weight, edge_weight1, L0_gnn_W, L0_gnn_b, L0_ffn_Wg, L0_ffn_bg, L0_ffn_bias, L0_ffn_W1, L0_ffn_b1, L0_ffn_W2, L0_ffn_b2, L1_gnn_Wp, L1_gnn_bp, L1_gnn_W1, L1_gnn_b1, L1_gnn_W2, L1_gnn_b2, L1_ffn_router_w, L1_ffn_w1, L1_ffn_b1, L1_ffn_w2, L1_ffn_b2):
    import jax
    import jax.numpy as jnp

    def _L0_gnn_ref(feat, eweight, W, b, src, dst):
        import jax, jax.numpy as jnp
        import numpy as np
        N_NODES = 1250
        N_EDGES = 40000
        D_IN = 256
        D_OUT = 256
        n = feat.shape[0]
        msg = feat[src] * eweight
        agg = jax.ops.segment_sum(msg, dst, num_segments=n)
        deg = jax.ops.segment_sum(jnp.ones((src.shape[0],), dtype=feat.dtype), dst, num_segments=n)
        h_neigh = agg / jnp.maximum(deg, 1.0)[:, None]
        h = jnp.concatenate([h_neigh, feat], axis=-1)
        return h @ W.T + b

    def _L0_ffn_ref(x, Wg, bg, bias, W1, b1, W2, b2):
        import jax, jax.numpy as jnp
        import numpy as np
        D_MODEL = 256
        EXPERT_DIM = 512
        NUM_EXPERTS = 8
        TOP_K = 2
        SEQ_LEN = 256
        BATCH = 2
        x_flat = x.reshape(-1, D_MODEL)
        gate_logits = x_flat @ Wg + bg + bias
        topk_vals, topk_idx = jax.lax.top_k(gate_logits, TOP_K)
        topk_w = jax.nn.softmax(topk_vals, axis=-1)
        combine = (jax.nn.one_hot(topk_idx, NUM_EXPERTS, dtype=x.dtype) * topk_w[..., None]).sum(axis=1)
        h = jax.nn.relu(jnp.einsum('td,edh->teh', x_flat, W1) + b1)
        y = jnp.einsum('teh,ehd->ted', h, W2) + b2
        out = jnp.einsum('ted,te->td', y, combine)
        return out.reshape(x.shape)

    def _L1_gnn_ref(x, edge_vals, Wp, bp, W1, b1, W2, b2, src, dst):
        import jax, jax.numpy as jnp
        import numpy as np
        MU = 2.0
        N = x.shape[0]
        h = jax.nn.relu(x @ Wp.T + bp)
        hp = h ** MU
        msgs = edge_vals[:, None] * hp[src]
        agg = jax.ops.segment_sum(msgs, dst, num_segments=N)
        agg = agg ** (1.0 / MU)
        return h @ W1.T + b1 + agg @ W2.T + b2

    def _L1_ffn_ref(input_embeddings, router_w, w1, b1, w2, b2):
        import jax, jax.numpy as jnp
        import numpy as np
        NUM_EXPERTS = 8
        TOP_K = 2
        B, S, D = (8, 1024, 256)

        def _moe(tokens, router_w, w1, b1, w2, b2):
            N = tokens.shape[0]
            E = router_w.shape[0]
            logits = tokens.astype(jnp.float32) @ router_w.astype(jnp.float32).T
            probs = jax.nn.softmax(logits, axis=-1)
            rw, re = jax.lax.top_k(probs, TOP_K)
            if TOP_K > 1:
                rw = rw / jnp.maximum(rw.sum(-1, keepdims=True), 1e-12)
            rw = rw.astype(tokens.dtype)
            combine = jnp.zeros((N, E), tokens.dtype).at[jnp.arange(N)[:, None], re].set(rw)
            out = tokens
            for e in range(E):
                h = jax.nn.gelu(tokens @ w1[e] + b1[e], approximate=False)
                y = h @ w2[e] + b2[e]
                out = out + combine[:, e:e + 1] * y
            return out
        b, s, d = input_embeddings.shape
        tokens = input_embeddings.reshape(b * s, d)
        return _moe(tokens, router_w, w1, b1, w2, b2).reshape(b, s, d)
    x = x + _L0_gnn_ref(_layernorm(x, axis=-1), edge_weight1, L0_gnn_W, L0_gnn_b, src, dst)
    x = x + _L0_ffn_ref(_layernorm(x, axis=-1)[None], L0_ffn_Wg, L0_ffn_bg, L0_ffn_bias, L0_ffn_W1, L0_ffn_b1, L0_ffn_W2, L0_ffn_b2)[0]
    x = x + _L1_gnn_ref(_layernorm(x, axis=-1), edge_weight, L1_gnn_Wp, L1_gnn_bp, L1_gnn_W1, L1_gnn_b1, L1_gnn_W2, L1_gnn_b2, src, dst)
    x = x + _L1_ffn_ref(_layernorm(x, axis=-1)[None], L1_ffn_router_w, L1_ffn_w1, L1_ffn_b1, L1_ffn_w2, L1_ffn_b2)[0]
    return x

_drawn_inputs = setup_inputs


def setup_inputs(seed=0):
    import zlib

    import numpy as np

    out = dict(_drawn_inputs(seed))
    spreads = {'L0_ffn_bias': (0.0, 0.1),
     'L1_gnn_bp': (0.0, 0.1),
     'L1_gnn_b1': (0.0, 0.1),
     'L1_gnn_b2': (0.0, 0.1),
     'L1_ffn_b1': (0.0, 0.531),
     'L1_ffn_b2': (0.0, 0.386)}
    factors = {'L0_gnn_b': 4.962, 'L0_ffn_bg': 6.085, 'L0_ffn_b1': 8.0, 'L0_ffn_b2': 4.575}
    for name, (base, spread) in spreads.items():
        noise = np.random.default_rng([zlib.crc32(name.encode()), seed]).standard_normal(out[name].shape)
        drawn = base * np.exp(spread * noise) if base else spread * noise
        out[name] = jnp.asarray(drawn.astype(out[name].dtype))
    for name, factor in factors.items():
        out[name] = (out[name] * factor).astype(out[name].dtype)
    return out
```

```python
import numpy as np
import concourse.bass as bass
from concourse import mybir
from contextlib import ExitStack

F32 = mybir.dt.float32
BF16 = mybir.dt.bfloat16
I32 = mybir.dt.int32
ALU = mybir.AluOpType
ACT = mybir.ActivationFunctionType
AX = mybir.AxisListType.X
RMAX = bass.bass_isa.ReduceOp.max

P = 128
D = 256
KD = D // P
NX = 8
SUB = 4
PT = 121
T = SUB * PT
GE = SUB * P
W = 64
GPT = 16
LAG = 2
WACC = T + 256
HC0, HC1 = 4, 2
CP = 9
EPS = 1e-5


def shapes(n, e):
    tiles = -(-n // T)
    groups = GPT * tiles + LAG
    assert tiles % 2 == 1 and groups * GE >= e and tiles >= 5
    return tiles, groups


def build_program(nc, a, n_nodes, n_edges):
    NT, NG = shapes(n_nodes, n_edges)
    NPAD = NT * T
    ET = NG * SUB

    table0 = nc.dram_tensor("table0", (NPAD, D), F32, kind="Internal").ap()
    table1 = nc.dram_tensor("table1", (NPAD, P), F32, kind="Internal").ap()
    x2_d = nc.dram_tensor("x2_d", (NPAD, D), F32, kind="Internal").ap()
    hT_d = nc.dram_tensor("hT_d", (NT, P, T), F32, kind="Internal").ap()
    seed0_d = nc.dram_tensor("seed0_d", (NT, P, 3 * T), F32, kind="Internal").ap()
    seed1_d = nc.dram_tensor("seed1_d", (NT, P, T), F32, kind="Internal").ap()

    def rows(dram, t):
        return dram[bass.ds(t * T, T), :].rearrange("(p s) d -> p (s d)", s=SUB)

    ctx = ExitStack()

    def sb(name, shape, dt=F32):
        return ctx.enter_context(nc.sbuf_tensor(name, shape, dt))

    def sem(name):
        return ctx.enter_context(nc.semaphore(name))

    def rep(x, axis, n):
        x = x.unsqueeze(axis)
        return x.broadcast_to([n if k == axis else d for k, d in enumerate(x.shape)])

    def wait(eng, s, value):
        if isinstance(value, int) and value <= 0:
            return
        eng.wait_ge(s, value)

    def hold(eng):
        eng.nop(nofuse=True)

    class Chain:

        def __init__(self, eng, s):
            self.eng, self.sem, self.base, self.n = eng, s, 0, 0

        def link(self, ins):
            self.n += 1
            ins.then_inc(self.sem, 1)
            self.eng.wait_ge(self.sem, self.base + self.n)

        def loop(self, i, per):
            self.start, self.per = self.base + self.n, per
            self.base, self.n = self.start + i * per, 0

        def looped(self, count):
            assert self.n == self.per, (self.n, self.per)
            self.base, self.n = self.start + count * self.per, 0

    with ctx:
        ident = sb("ident", [P, P])
        ident_b = sb("ident_b", [P, P], BF16)
        ones_b = sb("ones_b", [P, P], BF16)
        iota = sb("iota", [P, T])
        lower = sb("lower", [P, NX * NX])
        eps_t = sb("eps_t", [P, 1])
        spread = sb("spread", [3 * NX, NX, P], BF16)
        partmask = sb("partmask", [CP * NX, 3])
        gnn0_w = sb("gnn0_w", [P, 2 * KD, D])
        gnn0_b = sb("gnn0_b", [P, D])
        wg0 = sb("wg0", [P, KD, NX])
        gb0 = sb("gb0", [P, 2, NX])
        w1_0 = sb("w1_0", [P, NX, KD, HC0 * P])
        w2_0 = sb("w2_0", [P, NX, HC0, D])
        b1_0 = sb("b1_0", [P, NX, HC0])
        wp = sb("wp", [P, KD, P])
        bp = sb("bp", [P, 1])
        gnn1_w = sb("gnn1_w", [P, 2, D])
        gnn1_b = sb("gnn1_b", [P, 2, D])
        wg1 = sb("wg1", [P, KD, NX])
        w1_1 = w1_0[:, :, :, :].rearrange("p e k n -> p (e k n)")[:, 0:NX * KD * HC1 * P].rearrange(
            "p (e k n) -> p e k n", e=NX, k=KD)
        w2_1 = w2_0[:, :, :, :].rearrange("p e k n -> p (e k n)")[:, 0:NX * HC1 * D].rearrange(
            "p (e k n) -> p e k n", e=NX, k=HC1)
        b1_1 = sb("b1_1", [P, NX, HC1])
        b2s = [sb(f"b2s{i}", [CP * NX, D], BF16) for i in range(2)]

        src_s = sb("src_s", [P, ET], I32)
        w_s = [sb(f"w_s{i}", [P, ET]) for i in range(2)]
        dst_f = sb("dst_f", [P, NG, SUB])
        drel = sb("drel", [P, NG, SUB])
        floor_s = sb("floor_s", [P, NG])
        rel = sb("rel", [P, NG])
        base_i = sb("base_i", [P, NG + 2], I32)
        flag_f = sb("flag_f", [P, 2])
        flag_i = sb("flag_i", [1, 1], I32)
        RING = [4, 8]
        ring = sb("ring", [P, RING[0] * SUB * D])
        ringv = [ring[:, :].rearrange("p (r k d) -> p r k d", r=RING[0], k=SUB),
                 ring[:, :].rearrange("p (r k d) -> p r k d", r=RING[1], k=SUB)]
        idx = sb("idx", [P, 8, SUB], I32)
        oh = sb("oh", [P, 2, SUB, W], BF16)
        ohw = sb("ohw", [P, 2, SUB, W])
        acc = sb("acc", [P, 3, WACC])
        cnt = sb("cnt", [P, 2, T])
        aggs = sb("aggs", [P, KD, T])

        xin = sb("xin", [PT, SUB, D])
        feat = sb("feat", [PT, SUB, D])
        featT = sb("featT", [P, KD, T])
        res = [sb(f"res{i}", [PT, SUB, D]) for i in range(2)]
        xn = sb("xn", [PT, SUB, D])
        xnT = [sb(f"xnT{i}", [P, KD, T]) for i in range(2)]
        hid = [sb(f"hid{i}", [P, T]) for i in range(2)]
        hsc = [sb(f"hsc{i}", [P, T]) for i in range(2)]
        yT = sb("yT", [P, KD, T])
        x2 = sb("x2", [PT, SUB, D])
        x2T = sb("x2T", [P, KD, T])
        hT = sb("hT", [P, T])
        hp = sb("hp", [PT, SUB, P])
        stats = [sb(f"stats{i}", [PT, SUB, 6]) for i in range(2)]
        mv = [sb(f"mv{i}", [PT, SUB, 2]) for i in range(2)]
        sd = [sb(f"sd{i}", [PT, SUB]) for i in range(2)]
        rs = [sb(f"rs{i}", [PT, SUB]) for i in range(2)]
        lg = sb("lg", [PT, SUB, NX])
        lgd = sb("lgd", [PT, SUB, NX])
        ex = sb("ex", [PT, SUB, NX])
        pr = sb("pr", [PT, SUB, NX])
        m4 = sb("m4", [PT, 4, SUB])
        gt = sb("gt", [PT, SUB, NX, NX])
        eq = sb("eq", [PT, SUB, NX, NX])
        mask = sb("mask", [PT, SUB, NX])
        comb = sb("comb", [PT, SUB, NX])
        crem = sb("crem", [PT, SUB, NX])
        c72 = sb("c72", [PT, SUB, CP * NX], BF16)
        xn2 = sb("xn2", [PT, SUB, D])
        hTl = featT[:, 0, :]
        spread_f = x2[0:3 * NX, :, :].rearrange("p s d -> p (s d)")
        dst_s = ring[:, 0:ET].bitcast(I32)
        ext = x2T[:, :, :].rearrange("p k n -> p (k n)")[:, 0:2 * NG]
        extr = yT[:, :, :].rearrange("p k n -> p (k n)")[:, 0:2 * NG]
        chk = aggs[:, :, :].rearrange("p k n -> p (k n)")[:, 0:3 * NG].rearrange("p (a g) -> p a g", a=3)
        b2f = [cnt[0:CP * NX, i, 0:D] for i in range(2)]
        seed = sb("seed", [P, 3, T])
        fb_oh = sb("fb_oh", [P, T], BF16)
        fb_d = sb("fb_d", [P, 1])
        fb_off = sb("fb_off", [P, 1])
        cT = [sb(f"cT{i}", [CP * NX, T], BF16) for i in range(2)]

        psH = [ctx.enter_context(nc.psum_tensor(f"psH{i}", [P, 512], F32)) for i in range(2)]
        psY = [ctx.enter_context(nc.psum_tensor(f"psY{i}", [P, 512], F32)) for i in range(2)]
        psC = ctx.enter_context(nc.psum_tensor("psC", [P, 512], F32))
        psE = ctx.enter_context(nc.psum_tensor("psE", [P, 512], F32))
        psM = [ctx.enter_context(nc.psum_tensor(f"psM{i}", [P, 512], F32)) for i in range(2)]

        cps = psM[1][:, :].bitcast(BF16).rearrange("p (s n) -> p s n", s=2 * SUB)

        s_const = sem("const_loaded")
        s_edge = sem("edges_loaded")
        s_wl = sem("weights_loaded")
        s_wl1 = sem("layer1_experts_loaded")
        s_ext = sem("extremes_ready")
        s_extr = sem("extremes_reduced")
        s_flag = sem("flag_ready")
        s_ready = sem("constants_made")
        s_dve = sem("dve_chain")
        s_act = sem("act_chain")
        s_idx = [sem(f"idx_staged{i}") for i in range(2)]
        s_t0x = [sem(f"t0_x_loaded{i}") for i in range(2)]
        s_t0m = sem("t0_stats")
        s_t0s = sem("t0_sd")
        s_t0n = sem("t0_normed")
        s_t0w = [sem(f"t0_stored{i}") for i in range(2)]

        class Layer:

            def __init__(self, i):
                def s(name):
                    return sem(f"l{i}_{name}")

                self.onehot_ready = s("onehot_ready")
                self.group_summed = s("group_summed")
                self.window_added = s("window_added")
                self.agg_ready = s("agg_ready")
                self.agg_root = s("agg_root")
                self.feat_loaded = s("feat_loaded")
                self.xin_loaded = s("xin_loaded")
                self.featT_summed = s("featT_summed")
                self.featT_copied = s("featT_copied")
                self.lin_summed = s("lin_summed")
                self.res_ready = s("res_ready")
                self.ln_stats = s("ln_stats")
                self.ln_sd = s("ln_sd")
                self.xn_ready = s("xn_ready")
                self.xnT_summed = s("xnT_summed")
                self.xnT_copied = s("xnT_copied")
                self.logits_summed = s("logits_summed")
                self.logits_taken = s("logits_taken")
                self.exp_done = s("exp_done")
                self.comb_split = s("comb_split")
                self.combT_summed = s("combT_summed")
                self.comb_ready = s("comb_ready")
                self.spread_ready = s("spread_ready")
                self.hid_summed = s("hid_summed")
                self.hid_active = s("hid_active")
                self.hid_scaled = s("hid_scaled")
                self.hid_used = s("hid_used")
                self.ffn_summed = s("ffn_summed")
                self.y_copied = s("y_copied")
                self.ytok_summed = s("ytok_summed")
                self.out_ready = s("out_ready")
                self.out_stored = s("out_stored")
                self.fb_idx = s("fb_idx")
                self.fb_gathered = s("fb_gathered")
                self.fb_onehot = s("fb_onehot")
                self.fb_summed = s("fb_summed")
                self.fb_used = s("fb_used")
                self.fb_chain = s("fb_chain")
                self.fb_tile = s("fb_tile")
                self.fb_stored = s("fb_stored")
                self.seed_loaded = s("seed_loaded")
                self.seed_used = s("seed_used")
                self.i, self.HC = i, (HC0, HC1)[i]
                self.M = NX * self.HC
                self.R = RING[i]
                self.ring = ringv[i]
                self.gathered = [s(f"gathered{r}") for r in range(self.R)]
                self.w1, self.w2, self.b1 = (w1_0, w1_1)[i], (w2_0, w2_1)[i], (b1_0, b1_1)[i]
                self.wg, self.w = (wg0, wg1)[i], w_s[i]
                self.table, self.seed_d = (table0, table1)[i], (seed0_d, seed1_d)[i]
                self.parts = (3, 1)[i]
                self.at_take, self.at_feat, self.at_lin, self.at_norm, self.at_gate = (
                    (16, 14, 18, 21, 26), (12, 0, 13, 14, 15))[i]

        L = [Layer(0), Layer(1)]
        s_ln2m, s_ln2s, s_x2n = sem("ln2_stats"), sem("ln2_sd"), sem("x2n_ready")
        s_x2Ts, s_x2T = sem("x2T_summed"), sem("x2T_copied")
        s_hraw, s_hT = sem("hT_summed"), sem("hT_ready")
        s_hps, s_hp = sem("hp_summed"), sem("hp_ready")
        s_hTw, s_hpw = sem("hT_stored"), sem("hp_stored")

        block = ctx.enter_context(nc.Block())

        LASTG = LAG + GPT

        def stage_groups(u):
            if isinstance(u, int) and u == 0:
                return list(range(LASTG))
            return list(range(LAG, LASTG))

        def stage_place(l, n):
            if l.i == 0:
                return [LAG + n] if n < GPT else []
            lead = GPT - 12
            if n < lead:
                return [LAG + 2 * n, LAG + 2 * n + 1]
            return [LAG + lead + n] if n < 12 else []

        def iteration(l, emit, chain, per):
            emit(0, 0, True, False)
            emit(1, 1, False, False)
            with chain.eng.Fori(0, (NT - 3) // 2) as i:
                chain.loop(i, per)
                emit(2 * i + 2, 0, False, False)
                emit(2 * i + 3, 1, False, False)
            chain.looped((NT - 3) // 2)
            emit(NT - 1, 0, False, True)

        @block.sync
        def _(sp):
            for dst, s in ((ident, "ident"), (iota, "iota"), (lower, "lower"),
                           (partmask, "partmask"), (x2, "spread"), (floor_s, "floor")):
                dst = spread_f if s == "spread" else dst[:, :]
                sp.dma_start(dst, a[s]).then_inc(s_const, 16)
            for dst, s in ((src_s, "src"), (None, "dst"), (w_s[0], "w0"), (w_s[1], "w1")):
                sp.dma_start(dst_s if s == "dst" else dst[:, :], a[s]).then_inc(s_edge, 16)

            def t0_load(t, q):
                if not isinstance(t, int) or t >= 2:
                    sp.wait_ge(s_t0n, t - 1)
                sp.dma_start((xin, feat)[q][:, :, :].rearrange("p s d -> p (s d)"),
                             rows(a["x"], t)).then_inc(s_t0x[q], 16)

            def t0_store(t, q):
                sp.wait_ge(s_t0n, t + 1)
                sp.dma_start(rows(table0, t),
                             res[q][:, :, :].rearrange("p s d -> p (s d)")).then_inc(s_t0w[q], 16)

            t0_load(0, 0)
            t0_load(1, 1)
            with sp.Fori(0, (NT - 3) // 2) as i:
                t0_store(2 * i, 0)
                t0_load(2 * i + 2, 0)
                t0_store(2 * i + 1, 1)
                t0_load(2 * i + 3, 1)
            t0_store(NT - 3, 0)
            t0_load(NT - 1, 0)
            t0_store(NT - 2, 1)
            t0_store(NT - 1, 0)

            for dst, s in (
                (gnn0_w, "gnn0_w"), (wg0, "wg0"), (w1_0, "w1_0"), (w2_0, "w2_0"), (b1_0, "b1_0"),
                (wp, "wp"), (gnn1_w, "gnn1_w"), (wg1, "wg1"),
                (b1_1, "b1_1"),
            ):
                v = dst[:, :, :] if len(dst.shape) == 3 else dst[:, :, :, :]
                sp.dma_start(v, a[s]).then_inc(s_wl, 16)
            sp.dma_start(bp[:, :], a["bp"]).then_inc(s_wl, 16)
            sp.dma_start(gnn0_b[:, :], a["gnn0_b"].broadcast_to((P, a["gnn0_b"].shape[1]))).then_inc(s_wl, 16)
            sp.dma_start(gnn1_b[:, 0, :], a["gnn1_b1"].broadcast_to((P, a["gnn1_b1"].shape[1]))).then_inc(s_wl, 16)
            sp.dma_start(gnn1_b[:, 1, :], a["gnn1_b2"].broadcast_to((P, a["gnn1_b2"].shape[1]))).then_inc(s_wl, 16)
            sp.dma_start(gb0[:, 0, :], a["bg"].broadcast_to((P, a["bg"].shape[1]))).then_inc(s_wl, 16)
            sp.dma_start(gb0[:, 1, :], a["bias"].broadcast_to((P, a["bias"].shape[1]))).then_inc(s_wl, 16)
            for k in range(CP):
                for i in range(2):
                    sp.dma_start(cnt[k * NX:(k + 1) * NX, i, 0:D], a[("b2_0", "b2_1")[i]])\
                      .then_inc(s_wl, 16)

            sp.wait_ge(s_flag, 1)
            flag = sp.value_load(flag_i[0:1, 0:1], min_val=0, max_val=1)

            def general_store(l):
                with sp.If(flag):
                    with sp.Fori(0, NT) as u:
                        sp.wait_ge(l.fb_tile, u + 1)
                        sp.dma_start(l.seed_d[bass.ds(u, 1), :, :].rearrange(
                            "o p (k n) -> (o p) k n", k=l.parts),
                            acc[:, 0:l.parts, 0:T]).then_inc(l.fb_stored, 16)

            def seed_load(l, u):
                with sp.If(flag):
                    wait(sp, l.seed_used, u)
                    sp.dma_start(seed[:, 0:l.parts, :], l.seed_d[bass.ds(u, 1), :, :].rearrange(
                        "o p (k n) -> (o p) k n", k=l.parts)).then_inc(l.seed_loaded, 16)

            def inputs(l, u):
                if l.i == 0:
                    wait(sp, l.featT_summed, 2 * u)
                    sp.dma_start(feat[:, :, :].rearrange("p s d -> p (s d)"), rows(table0, u))\
                      .then_inc(l.feat_loaded, 16)
                    src = a["x"]
                else:
                    wait(sp, l.lin_summed, 2 * u)
                    sp.dma_start(hTl, hT_d[bass.ds(u, 1), :, :].rearrange(
                        "o p n -> (o p) n")).then_inc(l.feat_loaded, 16)
                    src = x2_d
                wait(sp, l.res_ready, u)
                sp.dma_start(xin[:, :, :].rearrange("p s d -> p (s d)"), rows(src, u))\
                  .then_inc(l.xin_loaded, 16)

            def results0(tt):
                sp.wait_ge(L[0].out_ready, 2 * tt + 2)
                sp.dma_start(rows(x2_d, tt), x2[:, :, :].rearrange("p s d -> p (s d)"))\
                  .then_inc(L[0].out_stored, 16)
                sp.wait_ge(s_hT, tt + 1)
                sp.dma_start(hT_d[bass.ds(tt, 1), :, :].rearrange("o p n -> (o p) n"), hT[:, :])\
                  .then_inc(s_hTw, 16)
                sp.wait_ge(s_hp, tt + 1)
                sp.dma_start(rows(table1, tt), hp[:, :, :].rearrange("p s d -> p (s d)"))\
                  .then_inc(s_hpw, 16)

            def results1(tt, last=False):
                sp.wait_ge(L[1].out_ready, 2 * tt + 2)
                if not last:
                    sp.dma_start(rows(a["out"], tt), x2[:, :, :].rearrange("p s d -> p (s d)"))\
                      .then_inc(L[1].out_stored, 16)
                    return
                left = n_nodes - tt * T
                full, rest = left // SUB, left % SUB
                sp.dma_start(a["out"][tt * T:tt * T + full * SUB, :].rearrange(
                    "(p s) d -> p (s d)", s=SUB),
                    x2[0:full, :, :].rearrange("p s d -> p (s d)")).then_inc(L[1].out_stored, 16)
                if rest:
                    sp.dma_start(a["out"][tt * T + full * SUB:n_nodes, :].rearrange(
                        "(o s) d -> o (s d)", o=1),
                        x2[full:full + 1, 0:rest, :].rearrange("p s d -> p (s d)"))\
                      .then_inc(L[1].out_stored, 16)

            for q in range(2):
                sp.wait_ge(s_t0w[q], 16 * ((NT + 1 - q) // 2))
            general_store(L[0])
            ends = Chain(sp, s_act)
            for l, results in ((L[0], results0), (L[1], results1)):
                if l.i == 1:
                    sp.wait_ge(L[0].hid_used, L[0].M * NT)
                    sp.dma_start(w1_1, a["w1_1"]).then_inc(s_wl1, 16)
                    sp.dma_start(w2_1, a["w2_1"]).then_inc(s_wl1, 16)
                    general_store(l)
                    sp.wait_ge(L[0].out_stored, 16 * NT)
                    sp.wait_ge(s_hTw, 16 * NT)
                inputs(l, 0)
                seed_load(l, 0)

                def tile(t, q, first, last):
                    if not first:
                        results(t - 1)
                    if not last:
                        inputs(l, t + 1)
                        seed_load(l, t + 1)

                iteration(l, tile, ends, 0)
                if l.i == 0:
                    results(NT - 1)
                else:
                    results(NT - 1, last=True)
            stores = NT + (1 if (n_nodes - (NT - 1) * T) % SUB else 0)
            sp.wait_ge(L[1].out_stored, 16 * stores)
            sp.wait_ge(s_hpw, 16 * NT)

        @block.gpsimd
        def _(pool):
            pool.wait_ge(s_ext, 1)
            pool.partition_all_reduce(extr, ext, P, RMAX).then_inc(s_extr, 1)
            pool.wait_ge(s_edge, 64)
            pool.wait_ge(s_flag, 1)
            flag = pool.value_load(flag_i[0:1, 0:1], min_val=0, max_val=1)

            def general_gather(l):
                with pool.If(flag):
                    with pool.Fori(0, NT) as u:
                        with pool.Fori(0, ET) as j:
                            n = u * ET + j
                            pool.wait_ge(l.fb_used, n + 1)
                            pool.tensor_copy(idx[:, 0, 0:1], src_s[:, bass.ds(j, 1)])\
                                .then_inc(l.fb_idx, 1)
                            pool.wait_ge(l.fb_idx, n + 1)
                            hold(pool)
                            pool.indirect_dma_start(
                                out=l.ring[:, 0, 0, :], out_offset=None, in_=l.table,
                                in_offset=bass.IndirectOffsetOnAxis(ap=idx[:, 0, 0:1], axis=0))\
                                .then_inc(l.fb_gathered, 16)
                    pool.wait_ge(l.fb_used, NT * ET + 1)

            def gather_group(l, it, g8):
                g = 8 * it + g8
                wait(pool, l.group_summed, g - l.R + 1)
                pool.tensor_copy(idx[:, g8, :], src_s[:, bass.ds(g * SUB, SUB)])\
                    .then_inc(s_idx[l.i], 1)
                pool.wait_ge(s_idx[l.i], g + 1)
                hold(pool)
                for k in range(SUB):
                    pool.indirect_dma_start(
                        out=l.ring[:, g8 % l.R, k, :], out_offset=None, in_=l.table,
                        in_offset=bass.IndirectOffsetOnAxis(ap=idx[:, g8, k:k + 1], axis=0))\
                        .then_inc(l.gathered[g8 % l.R], 16)

            for l in L:
                if l.i == 0:
                    for q in range(2):
                        pool.wait_ge(s_t0w[q], 16 * ((NT + 1 - q) // 2))
                else:
                    pool.wait_ge(L[0].group_summed, NG)
                    pool.wait_ge(s_hpw, 16 * NT)
                general_gather(l)
                for g8 in range(8):
                    gather_group(l, 0, g8)
                with pool.Fori(1, NG // 8) as it:
                    for g8 in range(8):
                        gather_group(l, it, g8)
                for g8 in range(NG % 8):
                    gather_group(l, NG // 8, g8)

        @block.tensor
        def _(pe):
            pe.wait_ge(s_ready, 1)
            pe.wait_ge(s_wl, 16 * (15 + 2 * CP))
            flag = pe.value_load(flag_i[0:1, 0:1], min_val=0, max_val=1)
            mm = pe.matmul

            def general_sums(l):
                with pe.If(flag):
                    with pe.Fori(0, NT) as u:
                        with pe.Fori(0, ET) as j:
                            n = u * ET + j
                            pe.wait_ge(l.fb_onehot, n + 1)
                            pe.wait_ge(l.fb_gathered, 16 * n + 16)
                            if l.i == 0:
                                mm(psH[0][:, 0:T], l.ring[:, 0, 0, 0:P], hsc[0][:, :], start=True, stop=True)
                                mm(psH[1][:, 0:T], l.ring[:, 0, 0, P:D], hsc[0][:, :], start=True, stop=True)
                                mm(psC[:, 0:T], ones_b[:, :], fb_oh[:, :], start=True, stop=True)\
                                    .then_inc(l.fb_summed, 1)
                            else:
                                mm(psC[:, 0:T], l.ring[:, 0, 0, :], hsc[0][:, :], start=True, stop=True)\
                                    .then_inc(l.fb_summed, 1)

            def sum_group(l, u, j):
                g, r, q = GPT * u + j, j % l.R, j % 2
                pe.wait_ge(l.onehot_ready, g + 1)
                pe.wait_ge(l.gathered[r], 16 * SUB * ((GPT // l.R) * u + j // l.R + 1))
                wait(pe, l.window_added, g)
                for h in range(KD if l.i == 0 else 1):
                    for k in range(SUB):
                        last = mm(psE[:, h * W:(h + 1) * W], l.ring[:, r, k, h * P:(h + 1) * P],
                                  ohw[:, q, k, :], start=(k == 0), stop=(k == SUB - 1))
                if l.i == 0:
                    for k in range(SUB):
                        last = mm(psE[:, 2 * W:3 * W], ones_b[:, :], oh[:, q, k, :],
                                  start=(k == 0), stop=(k == SUB - 1))
                last.then_inc(l.group_summed, 1)

            def up(l, t, q, n):
                e, c = n // l.HC, n % l.HC
                wait(pe, l.hid_active, l.M * t + n - 1)
                for k in range(KD):
                    last = mm(psH[n % 2][:, 0:T], l.w1[:, e, k, c * P:(c + 1) * P], xnT[q][:, k, :],
                              start=(k == 0), stop=(k == KD - 1))
                last.then_inc(l.hid_summed, 1)

            def spread_weights(l, t, q, e):
                wait(pe, l.hid_scaled, l.M * t + l.HC * e)
                mm(psC[:, 0:T], spread[:, e, :], cT[q][0:3 * NX, :], start=True, stop=True)\
                    .then_inc(l.spread_ready, 1)

            def down(l, t, q, n):
                e, c = n // l.HC, n % l.HC
                if n == 0:
                    wait(pe, l.y_copied, t)
                    for d in range(KD):
                        mm(psY[d][:, 0:T], b2s[l.i][:, d * P:(d + 1) * P], cT[q][:, :],
                           start=True, stop=False)
                pe.wait_ge(l.hid_scaled, l.M * t + n + 1)
                for d in range(KD):
                    last = mm(psY[d][:, 0:T], l.w2[:, e, c, d * P:(d + 1) * P], hsc[n % 2][:, :],
                              start=False, stop=(n == l.M - 1))
                last.then_inc(l.hid_used, 1)

            def back_to_tokens(l, tt):
                pe.wait_ge(l.y_copied, tt + 1)
                for b in range(2):
                    for s in (2 * b, 2 * b + 1):
                        for k in range(KD):
                            last = pe.transpose(psM[b][0:PT, (s % 2) * D + k * P:(s % 2) * D + (k + 1) * P],
                                                yT[:, k, s * PT:(s + 1) * PT], ident[:, :])
                    last.then_inc(l.ytok_summed, 1)

            def to_features(src, b, k, then):
                for s in range(SUB):
                    last = pe.transpose(psM[b][:, s * PT:(s + 1) * PT], src[:, s, k * P:(k + 1) * P],
                                        ident[0:PT, 0:PT])
                last.then_inc(then, 1)

            def project(tt):
                pe.wait_ge(s_x2T, 2 * tt + 2)
                for k in range(KD):
                    last = mm(psM[0][:, 0:T], wp[:, k, :], x2T[:, k, :], start=(k == 0), stop=(k == KD - 1))
                last.then_inc(s_hraw, 1)

            def project_tokens(tt):
                pe.wait_ge(s_hT, tt + 1)
                for s in range(SUB):
                    last = pe.transpose(psM[1][0:PT, s * P:(s + 1) * P], hT[:, s * PT:(s + 1) * PT],
                                        ident[:, :])
                last.then_inc(s_hps, 1)

            def feat_transposed(l, u):
                pe.wait_ge(l.feat_loaded, 16 * u + 16)
                wait(pe, s_hT, u - 1)
                wait(pe, l.logits_taken, u)
                to_features(feat, 0, 0, l.featT_summed)
                wait(pe, s_hp, u - 1)
                wait(pe, l.comb_ready, u)
                to_features(feat, 1, 1, l.featT_summed)

            def linear(l, u):
                if l.i == 0:
                    pe.wait_ge(l.featT_copied, 2 * u + 2)
                    pe.wait_ge(l.agg_ready, u + 1)
                    parts = [(aggs[:, k, :], gnn0_w[:, k, :]) for k in range(KD)]
                    parts += [(featT[:, k, :], gnn0_w[:, KD + k, :]) for k in range(KD)]
                else:
                    wait(pe, l.out_ready, 2 * u - 2)
                    wait(pe, l.logits_taken, u)
                    wait(pe, l.comb_ready, u)
                    pe.wait_ge(l.feat_loaded, 16 * u + 16)
                    pe.wait_ge(l.agg_root, u + 1)
                    parts = [(hTl, gnn1_w[:, 0, :]), (aggs[:, 1, :], gnn1_w[:, 1, :])]
                for b in range(2):
                    for s in (2 * b, 2 * b + 1):
                        for m, (x, w) in enumerate(parts):
                            last = mm(psM[b][0:PT, (s % 2) * D:(s % 2 + 1) * D],
                                      x[:, s * PT:(s + 1) * PT], w, start=(m == 0), stop=(m == len(parts) - 1))
                    last.then_inc(l.lin_summed, 1)

            def normed_transposed(l, u):
                pe.wait_ge(l.xn_ready, u + 1)
                for k in range(KD):
                    to_features(xn, k, k, l.xnT_summed)

            def logits(l, u, q):
                pe.wait_ge(l.xnT_copied, 2 * u + 2)
                for s in range(SUB):
                    for k in range(KD):
                        last = mm(psM[0][0:PT, s * NX:(s + 1) * NX], xnT[q][:, k, s * PT:(s + 1) * PT],
                                  l.wg[:, k, :], start=(k == 0), stop=(k == KD - 1))
                last.then_inc(l.logits_summed, 1)

            def weights_transposed(l, u):
                pe.wait_ge(l.comb_split, u + 1)
                for s in range(SUB):
                    last = pe.transpose(cps[0:CP * NX, s, 0:PT], c72[:, s, :], ident_b[0:PT, 0:PT])
                last.then_inc(l.combT_summed, 1)

            for l in L:
                general_sums(l)
                for j in stage_groups(0):
                    sum_group(l, 0, j)
                if l.i == 0:
                    feat_transposed(l, 0)
                linear(l, 0)
                normed_transposed(l, 0)
                logits(l, 0, 0)
                weights_transposed(l, 0)
                if l.i == 1:
                    pe.wait_ge(s_wl1, 32)

                def tile(t, q, first, last):
                    pe.wait_ge(l.comb_ready, t + 1)
                    up(l, t, q, 0)
                    spread_weights(l, t, q, 0)
                    for n in range(l.M):
                        if n + 1 < l.M:
                            up(l, t, q, n + 1)
                        down(l, t, q, n)
                        if n % l.HC == l.HC - 1 and n + 1 < l.M:
                            spread_weights(l, t, q, n // l.HC + 1)
                        if n == 1 and not first:
                            back_to_tokens(l, t - 1)
                        if l.i == 0 and not first:
                            if n == 6:
                                pe.wait_ge(s_x2n, t)
                                to_features(xn2, 0, 0, s_x2Ts)
                                to_features(xn2, 1, 1, s_x2Ts)
                            if n == 9:
                                project(t - 1)
                            if n == 11:
                                project_tokens(t - 1)
                        if last:
                            continue
                        for j in stage_place(l, n):
                            sum_group(l, t + 1, j)
                        if n == l.at_feat and l.i == 0:
                            feat_transposed(l, t + 1)
                        if n == l.at_lin:
                            linear(l, t + 1)
                        if n == l.at_norm:
                            normed_transposed(l, t + 1)
                        if n == l.at_gate:
                            logits(l, t + 1, 1 - q)
                        if n == min(l.at_gate + 3, l.M - 1):
                            weights_transposed(l, t + 1)

                iteration(l, tile, Chain(pe, s_act), 0)
                pe.wait_ge(s_hp, NT - 1) if l.i == 0 else pe.wait_ge(l.out_ready, 2 * NT - 2)
                back_to_tokens(l, NT - 1)
                if l.i == 0:
                    pe.wait_ge(s_x2n, NT)
                    to_features(xn2, 0, 0, s_x2Ts)
                    to_features(xn2, 1, 1, s_x2Ts)
                    project(NT - 1)
                    project_tokens(NT - 1)

        @block.vector
        def _(dve):
            c = Chain(dve, s_dve)
            link = c.link
            tt_, ts_ = dve.tensor_tensor, dve.tensor_scalar

            dve.wait_ge(s_const, 16 * 6)
            dve.memset(ones_b[:, :], 1.0)
            dve.memset(eps_t[:, :], EPS)
            dve.memset(acc[:, :, :], 0.0)
            dve.memset(base_i[:, :], 0)
            dve.tensor_copy(ident_b[:, :], ident[:, :])
            link(dve.tensor_copy(spread[:, :, :].rearrange("k e p -> k (e p)"), spread_f))

            dve.wait_ge(s_edge, 64)
            link(dve.tensor_copy(dst_f[:, :, :].rearrange("p g k -> p (g k)"), dst_s))
            link(ts_(drel[:, :, :], dst_f[:, :, :], -1.0, None, ALU.mult))
            dve.reduce_max(ext[:, 0:NG], dst_f[:, :, :], AX)
            dve.reduce_max(ext[:, NG:2 * NG], drel[:, :, :], AX).then_inc(s_ext, 1)
            dve.wait_ge(s_extr, 1)
            hi, neg = extr[:, 0:NG], extr[:, NG:2 * NG]
            link(tt_(rel[:, :], neg, floor_s[:, :], ALU.add))
            link(ts_(rel[:, :], rel[:, :], -1.0, None, ALU.mult))
            link(tt_(chk[:, 2, :], hi, neg, ALU.add))
            ts_(chk[:, 0, :], rel[:, :], 0.0, None, ALU.is_lt)
            ts_(chk[:, 1, :], rel[:, :], float(WACC - W), None, ALU.is_gt)
            link(ts_(chk[:, 2, :], chk[:, 2, :], float(W - 1), None, ALU.is_gt))
            link(dve.reduce_max(flag_f[:, 0:1], chk.rearrange("p a g -> p (a g)"), AX))
            link(ts_(flag_f[:, 1:2], flag_f[:, 0:1], -1.0, 1.0, ALU.mult, ALU.add))
            link(ts_(rel[:, :], rel[:, :], 0.0, float(WACC - W), ALU.max, ALU.min))
            dve.tensor_copy(base_i[:, 2:NG + 2], rel[:, :])
            link(tt_(drel[:, :, :], dst_f[:, :, :], rep(neg, 2, SUB), ALU.add))
            link(ts_(drel[:, :, :], drel[:, :, :], flag_f[:, 1:2], flag_f[:, 0:1], ALU.mult, ALU.subtract))
            link(dve.tensor_copy(flag_i[:, :], flag_f[0:1, 0:1]))
            dve.sem_inc(s_flag, 1)

            def ln_moments(x, i, then):
                for s in range(SUB):
                    last = dve.bn_stats(stats[i][:, s, :], x[:, s, :])
                link(last)
                hold(dve)
                for s in range(SUB):
                    last = dve.bn_aggr(mv[i][:, s, :], stats[i][:, s, :])
                last.then_inc(then, 1)

            def ln_apply(out, x, i, then):
                link(dve.reciprocal(rs[i][:, :], sd[i][:, :]))
                for s in range(SUB):
                    last = ts_(out[:, s, :], x[:, s, :], mv[i][:, s, 0:1], rs[i][:, s:s + 1],
                               ALU.subtract, ALU.mult)
                last.then_inc(then, 1)

            def table_tile(t, q, k):
                dve.wait_ge(s_t0x[q], 16 * k + 16)
                x = (xin, feat)[q]
                if not isinstance(t, int) or t >= 2:
                    dve.wait_ge(s_t0w[q], 16 * k)
                ln_moments(x, 0, s_t0m)
                dve.wait_ge(s_t0s, t + 1)
                ln_apply(res[q], x, 0, s_t0n)
                dve.wait_ge(s_t0n, t + 1)
                hold(dve)

            table_tile(0, 0, 0)
            table_tile(1, 1, 0)
            with dve.Fori(1, (NT - 1) // 2) as i:
                c.loop(i - 1, 4)
                table_tile(2 * i, 0, i)
                table_tile(2 * i + 1, 1, i)
            c.looped((NT - 1) // 2 - 1)
            table_tile(NT - 1, 0, (NT - 1) // 2)

            dve.wait_ge(s_wl, 16 * (15 + 2 * CP))
            for i in range(2):
                b, part = b2f[i], (hid[0], hid[1], hsc[0])
                n = CP * NX
                bb = b2s[i][:, :]
                for k in range(3):
                    link(dve.tensor_copy(bb, b))
                    link(dve.tensor_copy(part[k][0:n, 0:D], bb))
                    link(tt_(b, b, part[k][0:n, 0:D], ALU.subtract))
                link(ts_(part[0][0:n, 0:D], part[0][0:n, 0:D], partmask[:, 0:1], None, ALU.mult))
                link(dve.scalar_tensor_tensor(part[0][0:n, 0:D], part[1][0:n, 0:D], partmask[:, 1:2],
                                              part[0][0:n, 0:D], ALU.mult, ALU.add))
                link(dve.scalar_tensor_tensor(bb, part[2][0:n, 0:D], partmask[:, 2:3],
                                              part[0][0:n, 0:D], ALU.mult, ALU.add))
            dve.sem_inc(s_ready, 1)

            flag = dve.value_load(flag_i[0:1, 0:1], min_val=0, max_val=1)

            def general_windows(l):
                per = ET + 2
                d2 = dst_f[:, :, :].rearrange("p g k -> p (g k)")
                with dve.If(flag):
                    dve.memset(fb_off[:, :], 0.0).then_inc(l.fb_chain, 1)
                    dve.sem_inc(l.fb_used, 1)
                    with dve.Fori(0, NT) as u:
                        dve.wait_ge(l.fb_chain, u * per + 1)
                        dve.memset(acc[:, 0:l.parts, 0:T], 0.0).then_inc(l.fb_chain, 1)
                        with dve.Fori(0, ET) as j:
                            n = u * ET + j
                            dve.wait_ge(l.fb_chain, u * per + j + 2)
                            tt_(fb_d[:, :], d2[:, bass.ds(j, 1)], fb_off[:, :], ALU.subtract)\
                                .then_inc(l.fb_chain, 1)
                            dve.wait_ge(l.fb_chain, u * per + j + 3)
                            hold(dve)
                            ts_(fb_oh[:, :], iota[:, :], fb_d[:, 0:1], None, ALU.is_equal)
                            ts_(hsc[0][:, :], iota[:, :], fb_d[:, 0:1], l.w[:, bass.ds(j, 1)],
                                ALU.is_equal, ALU.mult).then_inc(l.fb_onehot, 1)
                            dve.wait_ge(l.fb_summed, n + 1)
                            for k in range(l.parts):
                                ps = (psH[0], psH[1], psC)[k] if l.i == 0 else psC
                                last = tt_(acc[:, k, 0:T], acc[:, k, 0:T], ps[:, 0:T], ALU.add)
                            last.then_inc(l.fb_used, 1)
                            dve.wait_ge(l.fb_used, n + 2)
                            hold(dve)
                        dve.wait_ge(l.fb_chain, u * per + ET + 2)
                        ts_(fb_off[:, :], fb_off[:, :], float(T), None, ALU.add).then_inc(l.fb_chain, 1)
                        dve.sem_inc(l.fb_tile, 1)
                        dve.wait_ge(l.fb_stored, 16 * u + 16)
                        hold(dve)
                    dve.memset(acc[:, :, :], 0.0).then_inc(l.fb_chain, 1)
                    dve.wait_ge(l.fb_chain, NT * per + 2)

            def onehots(l, u, j):
                g, q = GPT * u + j, j % 2
                wait(dve, l.group_summed, g - 1)
                ohw_e, oh_e = ohw[:, q, :, :], oh[:, q, :, :]
                d = rep(drel[:, bass.ds(g, 1), :].rearrange("p g k -> p (g k)"), 2, W)
                w = rep(l.w[:, bass.ds(g * SUB, SUB)], 2, W)
                i = rep(iota[:, 0:W], 1, SUB)
                link(tt_(oh_e, i, d, ALU.is_equal))
                tt_(ohw_e, oh_e, w, ALU.mult).then_inc(l.onehot_ready, 1)

            regs = {}

            def window_columns(l, u, j):
                n = 2 if j == 0 else 4
                cols = base_i[0:1, bass.ds(GPT * u + j + 2, n)]
                _, vals = nc.values_load_multi_w_load_instructions(
                    cols, engines=[mybir.EngineType.DVE], min_val=0, max_val=WACC - W,
                    skip_runtime_bounds_check_because="clamped to the range above")
                for k in range(n):
                    regs[j + k] = vals[k]

            def add_window(l, u, j):
                g = GPT * u + j
                if j == 0 or (j - LAG) % 4 == 0:
                    window_columns(l, u, j)
                dve.wait_ge(l.group_summed, g + 1)
                wait(dve, l.window_added, g)
                v = acc[:, 0:l.parts, bass.ds(regs[j], W)]
                ps = psE[:, 0:l.parts * W].rearrange("p (k n) -> p k n", k=l.parts)
                tt_(v, v, ps, ALU.add).then_inc(l.window_added, 1)

            def take(l, u):
                dve.wait_ge(l.window_added, GPT * u + LASTG)
                hold(dve)
                with dve.If(flag):
                    dve.wait_ge(l.seed_loaded, 16 * u + 16)
                    v = acc[:, 0:l.parts, 0:T]
                    tt_(v, v, seed[:, 0:l.parts, :], ALU.add).then_inc(l.seed_used, 1)
                    dve.wait_ge(l.seed_used, u + 1)
                    hold(dve)
                wait(dve, l.lin_summed, 2 * u)

                def perm(x):
                    return x.rearrange("c (q s) -> c q s", s=SUB)

                def placed(x):
                    return x.rearrange("c (s q) -> c q s", s=SUB)

                if l.i == 0:
                    link(ts_(cnt[:, 0, :], acc[:, 2, 0:T], 1.0, None, ALU.max))
                    link(dve.reciprocal(cnt[:, 1, :], cnt[:, 0, :]))
                    for k in range(KD):
                        last = tt_(placed(aggs[:, k, :]), perm(acc[:, k, 0:T]), perm(cnt[:, 1, :]), ALU.mult)
                    last.then_inc(l.agg_ready, 1)
                else:
                    dve.tensor_copy(placed(aggs[:, 0, :]), perm(acc[:, 0, 0:T])).then_inc(l.agg_ready, 1)
                dve.wait_ge(l.agg_ready, u + 1)
                link(dve.tensor_copy(acc[:, 0:l.parts, 0:WACC - T], acc[:, 0:l.parts, T:WACC]))
                link(dve.memset(acc[:, 0:l.parts, WACC - T:WACC], 0.0))

            def flat(x):
                return x.rearrange("p s d -> p (s d)")

            def residual(l, u, q):
                wait(dve, l.out_ready, 2 * u - 2)
                dve.wait_ge(l.xin_loaded, 16 * u + 16)
                for b in range(2):
                    dve.wait_ge(l.lin_summed, 2 * u + b + 1)
                    r = res[q][:, 2 * b:2 * b + 2, :]
                    p = psM[b][0:PT, :].rearrange("p (s d) -> p s d", s=2)
                    bias = rep((gnn0_b[0:PT, :] if l.i == 0 else gnn1_b[0:PT, 0, :]), 1, 2)
                    link(tt_(r, p, bias, ALU.add))
                    if l.i == 1:
                        bias2 = rep(gnn1_b[0:PT, 1, :], 1, 2)
                        link(tt_(r, r, bias2, ALU.add))
                    link(tt_(r, r, xin[:, 2 * b:2 * b + 2, :], ALU.add))
                dve.sem_inc(l.res_ready, 1)
                ln_moments(res[q], 0, l.ln_stats)

            def normed(l, u, q):
                dve.wait_ge(l.ln_sd, u + 1)
                wait(dve, l.xnT_summed, 2 * u)
                ln_apply(xn, res[q], 0, l.xn_ready)
                if l.i == 1:
                    dve.wait_ge(l.xn_ready, u + 1)
                    link(tt_(flat(res[q][:, :, :]), flat(res[q][:, :, :]), flat(xn[:, :, :]), ALU.add))

            def gate_max(l, u):
                dve.wait_ge(l.logits_summed, u + 1)
                ps = psM[0][0:PT, 0:SUB * NX].rearrange("p (s e) -> p s e", s=SUB)
                if l.i == 0:
                    link(tt_(lg[:, :, :], ps, rep(gb0[0:PT, 0, :], 1, SUB), ALU.add))
                    link(tt_(lg[:, :, :], lg[:, :, :], rep(gb0[0:PT, 1, :], 1, SUB), ALU.add))
                else:
                    link(dve.tensor_copy(lg[:, :, :], ps))
                link(dve.reduce_max(m4[:, 0, :], lg[:, :, :], AX))
                tt_(lgd[:, :, :], lg[:, :, :], rep(m4[:, 0, :], 2, NX), ALU.subtract)\
                    .then_inc(l.logits_taken, 1)

            def gate_weights(l, u):
                dve.wait_ge(l.exp_done, u + 1)
                if l.i == 0:
                    key = lg
                else:
                    key = pr
                    link(dve.reduce_sum(m4[:, 1, :], ex[:, :, :], AX))
                    link(dve.reciprocal(m4[:, 2, :], m4[:, 1, :]))
                    link(tt_(pr[:, :, :], ex[:, :, :], rep(m4[:, 2, :], 2, NX), ALU.mult))
                other = rep(key[:, :, :], 2, NX)
                own = rep(key[:, :, :], 3, NX)
                tt_(gt[:, :, :, :], other, own, ALU.is_gt)
                link(tt_(eq[:, :, :, :], other, own, ALU.is_equal))
                low = rep(lower[0:PT, :], 1, SUB)
                e3 = eq[:, :, :, :].rearrange("p s e j -> p s (e j)")
                link(tt_(e3, e3, low, ALU.mult))
                link(tt_(gt[:, :, :, :], gt[:, :, :, :], eq[:, :, :, :], ALU.add))
                link(dve.reduce_sum(mask[:, :, :], gt[:, :, :, :], AX))
                link(ts_(mask[:, :, :], mask[:, :, :], 1.5, None, ALU.is_lt))
                link(tt_(comb[:, :, :], mask[:, :, :], (ex if l.i == 0 else pr)[:, :, :], ALU.mult))
                link(dve.reduce_sum(m4[:, 1, :], comb[:, :, :], AX))
                if l.i == 1:
                    link(ts_(m4[:, 1, :], m4[:, 1, :], 1e-12, None, ALU.max))
                link(dve.reciprocal(m4[:, 2, :], m4[:, 1, :]))
                link(tt_(crem[:, :, :], comb[:, :, :], rep(m4[:, 2, :], 2, NX), ALU.mult))
                wait(dve, l.combT_summed, u)
                for k in range(3):
                    c4 = c72[:, :, :].rearrange("p s (j i e) -> p s j i e", j=3, i=3)
                    link(dve.tensor_copy(c4[:, :, :, k, :], rep(crem[:, :, :], 2, 3)))
                    if k < 2:
                        link(tt_(crem[:, :, :], crem[:, :, :], c4[:, :, 0, k, :], ALU.subtract))
                dve.sem_inc(l.comb_split, 1)

            def scale(l, t, n):
                dve.wait_ge(l.hid_active, l.M * t + n + 1)
                if n % l.HC == 0:
                    dve.wait_ge(l.spread_ready, NX * t + n // l.HC + 1)
                wait(dve, l.hid_used, l.M * t + n - 1)
                tt_(hsc[n % 2][:, :], hid[n % 2][:, :], psC[:, 0:T], ALU.mult).then_inc(l.hid_scaled, 1)

            def result(l, tt, q):
                wait(dve, l.out_stored, 16 * tt)
                for b in range(2):
                    dve.wait_ge(l.ytok_summed, 2 * tt + b + 1)
                    v = x2[:, 2 * b:2 * b + 2, :]
                    tt_(v, res[q][:, 2 * b:2 * b + 2, :],
                        psM[b][0:PT, :].rearrange("p (s d) -> p s d", s=2), ALU.add)\
                        .then_inc(l.out_ready, 1)
                if l.i == 0:
                    dve.wait_ge(l.out_ready, 2 * tt + 2)
                    ln_moments(x2, 1, s_ln2m)

            def result_normed(tt):
                dve.wait_ge(s_ln2s, tt + 1)
                wait(dve, s_x2Ts, 2 * tt)
                ln_apply(xn2, x2, 1, s_x2n)

            for l in L:
                general_windows(l)
                todo = stage_groups(0)
                for n, j in enumerate(todo):
                    onehots(l, 0, j)
                    if n:
                        add_window(l, 0, todo[n - 1])
                add_window(l, 0, todo[-1])
                take(l, 0)
                residual(l, 0, 0)
                normed(l, 0, 0)
                gate_max(l, 0)
                gate_weights(l, 0)

                def tile(t, q, first, last):
                    for n in range(l.M):
                        here = [] if last else stage_place(l, n)
                        if here:
                            onehots(l, t + 1, here[0])
                        scale(l, t, n)
                        if n and not last:
                            for j in stage_place(l, n - 1)[-1:]:
                                add_window(l, t + 1, j)
                        if len(here) == 2:
                            onehots(l, t + 1, here[1])
                            add_window(l, t + 1, here[0])
                        if n == 2 and not first:
                            result(l, t - 1, 1 - q)
                        if n == 4 and not first and l.i == 0:
                            result_normed(t - 1)
                        if last:
                            continue
                        if n == l.at_take:
                            take(l, t + 1)
                        if n == (l.at_lin + 1 if l.i == 0 else l.at_lin):
                            residual(l, t + 1, 1 - q)
                        if n == (l.at_norm - 1 if l.i == 0 else l.at_norm):
                            normed(l, t + 1, 1 - q)
                        if n == l.at_gate:
                            gate_max(l, t + 1)
                        if n == min(l.at_gate + 2, l.M - 1):
                            gate_weights(l, t + 1)

                iteration(l, tile, c, (90, 94)[l.i])
                result(l, NT - 1, 0)
                if l.i == 0:
                    result_normed(NT - 1)
                    link(dve.memset(acc[:, :, :], 0.0))

        @block.scalar
        def _(act):
            f = act.activation

            def root(i, then):
                f(sd[i][:, :], mv[i][:, :, 1], ACT.Sqrt, bias=eps_t[0:PT, :]).then_inc(then, 1)

            with act.Fori(0, NT) as t:
                act.wait_ge(s_t0m, t + 1)
                root(0, s_t0s)

            def copied(dst, k, ready, value, then):
                act.wait_ge(ready, value)
                f(dst, psM[k][:, 0:T], ACT.Copy).then_inc(then, 1)

            def take_root(l, u):
                act.wait_ge(l.agg_ready, u + 1)
                f(aggs[:, 1, :], aggs[:, 0, :], ACT.Sqrt).then_inc(l.agg_root, 1)

            def feat_copied(l, u):
                wait(act, l.lin_summed, 2 * u)
                for k in range(KD):
                    copied(featT[:, k, :], k, l.featT_summed, 2 * u + k + 1, l.featT_copied)

            def deviation(l, u):
                act.wait_ge(l.ln_stats, u + 1)
                root(0, l.ln_sd)

            def normed_copied(l, u, q):
                for k in range(KD):
                    copied(xnT[q][:, k, :], k, l.xnT_summed, 2 * u + k + 1, l.xnT_copied)

            def exponent(l, u):
                act.wait_ge(l.logits_taken, u + 1)
                f(ex[:, :, :], lgd[:, :, :], ACT.Exp).then_inc(l.exp_done, 1)

            def weights_copied(l, u, q):
                act.wait_ge(l.combT_summed, u + 1)
                f(cT[q][:, :].rearrange("k (s p) -> k s p", s=SUB), cps[0:CP * NX, 0:SUB, 0:PT], ACT.Copy)\
                    .then_inc(l.comb_ready, 1)

            def active(l, t, n):
                act.wait_ge(l.hid_summed, l.M * t + n + 1)
                wait(act, l.hid_scaled, l.M * t + n - 1)
                f(hid[n % 2][:, :], psH[n % 2][:, 0:T], (ACT.Relu, ACT.Gelu)[l.i],
                  bias=l.b1[:, n // l.HC, n % l.HC:n % l.HC + 1]).then_inc(l.hid_active, 1)

            def sum_copied(l, tt):
                act.wait_ge(l.hid_used, l.M * tt + l.M)
                wait(act, l.ytok_summed, 2 * tt)
                f(yT[:, 0, :], psY[0][:, 0:T], ACT.Copy)
                f(yT[:, 1, :], psY[1][:, 0:T], ACT.Copy).then_inc(l.y_copied, 1)

            def result_deviation(tt):
                act.wait_ge(s_ln2m, tt + 1)
                root(1, s_ln2s)

            def result_copied(tt):
                wait(act, s_hraw, tt)
                for k in range(KD):
                    copied(x2T[:, k, :], k, s_x2Ts, 2 * tt + k + 1, s_x2T)

            def projected(tt):
                act.wait_ge(s_hraw, tt + 1)
                wait(act, s_hTw, 16 * tt)
                wait(act, s_hps, tt)
                f(hT[:, :], psM[0][:, 0:T], ACT.Relu, bias=bp[:, :]).then_inc(s_hT, 1)

            def squared(tt):
                act.wait_ge(s_hps, tt + 1)
                wait(act, s_hpw, 16 * tt)
                f(hp[:, :, :].rearrange("p s d -> p (s d)"), psM[1][0:PT, :], ACT.Square)\
                    .then_inc(s_hp, 1)

            act.wait_ge(s_wl, 16 * (15 + 2 * CP))
            for l in L:
                if l.i == 0:
                    feat_copied(l, 0)
                else:
                    take_root(l, 0)
                deviation(l, 0)
                normed_copied(l, 0, 0)
                exponent(l, 0)
                weights_copied(l, 0, 0)

                def tile(t, q, first, last):
                    if not first:
                        sum_copied(l, t - 1)
                    for n in range(l.M):
                        active(l, t, n)
                        if l.i == 0 and not first:
                            if n == 4:
                                result_deviation(t - 1)
                            if n == 7:
                                result_copied(t - 1)
                            if n == 10:
                                projected(t - 1)
                            if n == 12:
                                squared(t - 1)
                        if last:
                            continue
                        if l.i == 0:
                            if n == l.at_feat + 1:
                                feat_copied(l, t + 1)
                            if n == l.at_lin + 1:
                                deviation(l, t + 1)
                            if n == l.at_norm + 1:
                                normed_copied(l, t + 1, 1 - q)
                            if n == l.at_gate + 1:
                                exponent(l, t + 1)
                            if n == l.M - 1:
                                weights_copied(l, t + 1, 1 - q)
                        else:
                            if n == l.at_take:
                                take_root(l, t + 1)
                            if n == l.at_lin:
                                deviation(l, t + 1)
                            if n == l.at_norm + 1:
                                normed_copied(l, t + 1, 1 - q)
                                exponent(l, t + 1)
                                weights_copied(l, t + 1, 1 - q)

                iteration(l, tile, Chain(act, s_act), 0)
                sum_copied(l, NT - 1)
                if l.i == 0:
                    result_deviation(NT - 1)
                    result_copied(NT - 1)
                    projected(NT - 1)
                    squared(NT - 1)


def laid_out(inputs, n_nodes, n_edges):
    NT, NG = shapes(n_nodes, n_edges)
    EP = NG * GE

    def arr(name):
        return np.ascontiguousarray(inputs[name])

    def edges(x, fill):
        x = np.concatenate([x.reshape(-1), np.full(EP - n_edges, fill, x.dtype)])
        return np.ascontiguousarray(x.reshape(NG * SUB, P).T)

    def chunks(w):
        return np.ascontiguousarray(w.reshape(-1, P, w.shape[1]).transpose(1, 0, 2))

    def experts(w):
        return np.ascontiguousarray(w.reshape(NX, -1, P, w.shape[2]).transpose(2, 0, 1, 3))

    def columns(b):
        return np.ascontiguousarray(b.reshape(NX, -1, P).transpose(2, 0, 1))

    f32 = np.float32
    spread = np.zeros((3, NX, NX, P), f32)
    partmask = np.zeros((3, 3 * NX, 3), f32)
    for e in range(NX):
        spread[:, e, e, :] = 1
    for j in range(3):
        partmask[j, :, j] = 1
    stage = [T * max(0, (g - LAG) // GPT) for g in range(NG)]
    return {
        "x": np.concatenate([arr("x"), np.zeros((NT * T - n_nodes, D), f32)]),
        "src": edges(arr("src"), 0), "dst": edges(arr("dst"), n_nodes),
        "w0": edges(arr("edge_weight1"), 0), "w1": edges(arr("edge_weight"), 0),
        "gnn0_w": chunks(arr("L0_gnn_W").T), "gnn0_b": arr("L0_gnn_b").reshape(1, D),
        "wg0": chunks(arr("L0_ffn_Wg")), "bg": arr("L0_ffn_bg").reshape(1, NX),
        "bias": arr("L0_ffn_bias").reshape(1, NX),
        "w1_0": experts(arr("L0_ffn_W1")), "b1_0": columns(arr("L0_ffn_b1")),
        "w2_0": experts(arr("L0_ffn_W2")), "b2_0": arr("L0_ffn_b2"),
        "wp": chunks(arr("L1_gnn_Wp").T), "bp": arr("L1_gnn_bp").reshape(P, 1),
        "gnn1_w": np.ascontiguousarray(np.stack([arr("L1_gnn_W1").T, arr("L1_gnn_W2").T], 1)),
        "gnn1_b1": arr("L1_gnn_b1").reshape(1, D), "gnn1_b2": arr("L1_gnn_b2").reshape(1, D),
        "wg1": chunks(arr("L1_ffn_router_w").T),
        "w1_1": experts(arr("L1_ffn_w1")), "b1_1": columns(arr("L1_ffn_b1")),
        "w2_1": experts(arr("L1_ffn_w2")), "b2_1": arr("L1_ffn_b2"),
        "ident": np.eye(P, dtype=f32),
        "iota": np.tile(np.arange(T, dtype=f32), (P, 1)),
        "lower": np.tile(np.tril(np.ones((NX, NX), f32), -1).reshape(1, -1), (P, 1)),
        "spread": spread.reshape(3 * NX, NX * P),
        "partmask": partmask.reshape(9 * NX, 3),
        "floor": np.tile(np.array(stage, f32), (P, 1)),
    }


def kernel(**inputs):
    import concourse.bacc as bacc
    from concourse.bass_utils import run_bass_kernel_spmd

    n_nodes, n_edges = inputs["x"].shape[0], inputs["src"].shape[0]
    arrays = laid_out(inputs, n_nodes, n_edges)
    nc = bacc.Bacc("TRN2", target_bir_lowering=False, num_devices=1)
    aps = {k: nc.dram_tensor(k + "_in", v.shape, mybir.dt.from_np(v.dtype), kind="ExternalInput").ap()
           for k, v in arrays.items()}
    aps["out"] = nc.dram_tensor("out_dram", (n_nodes, D), F32, kind="ExternalOutput").ap()
    build_program(nc, aps, n_nodes, n_edges)
    r = run_bass_kernel_spmd(nc, [{k + "_in": v for k, v in arrays.items()}], core_ids=[0])
    return r.results[0]["out_dram"]
```

```python
import numpy as np
import concourse.bass as bass
from concourse import mybir
from contextlib import ExitStack

F32 = mybir.dt.float32
BF16 = mybir.dt.bfloat16
F16 = mybir.dt.float16
I32 = mybir.dt.int32
ALU = mybir.AluOpType
ACT = mybir.ActivationFunctionType
AX = mybir.AxisListType.X
RMAX = bass.bass_isa.ReduceOp.max

P = 128
D = 256
KD = D // P
NX = 8
SUB = 4
PT = 121
T = SUB * PT
GE = SUB * P
W = 64
GPT = 16
LAG = 2
WACC = T + 256
HC0, HC1 = 4, 2
CP = 9
EPS = 1e-5
PARTS = ((0, 0), (0, 1), (1, 0))
XS = 2.0 ** 11
TINY = 2.0 ** -40
EXP_MASK = 0x7f800000
ONE_EXP = 1 << 23


def shapes(n, e):
    tiles = -(-n // T)
    groups = GPT * tiles + LAG
    assert tiles % 2 == 1 and groups * GE >= e and tiles >= 5
    return tiles, groups


def build_program(nc, a, n_nodes, n_edges):
    NT, NG = shapes(n_nodes, n_edges)
    NPAD = NT * T
    ET = NG * SUB

    table0 = nc.dram_tensor("table0", (NPAD, D), F32, kind="Internal").ap()
    table1 = nc.dram_tensor("table1", (NPAD, P), F32, kind="Internal").ap()
    x2_d = nc.dram_tensor("x2_d", (NPAD, D), F32, kind="Internal").ap()
    hT_d = nc.dram_tensor("hT_d", (NT, P, T), F32, kind="Internal").ap()
    seed0_d = nc.dram_tensor("seed0_d", (NT, P, 3 * T), F32, kind="Internal").ap()
    seed1_d = nc.dram_tensor("seed1_d", (NT, P, T), F32, kind="Internal").ap()

    def rows(dram, t):
        return dram[bass.ds(t * T, T), :].rearrange("(p s) d -> p (s d)", s=SUB)

    ctx = ExitStack()

    def sb(name, shape, dt=F32):
        return ctx.enter_context(nc.sbuf_tensor(name, shape, dt))

    def sem(name):
        return ctx.enter_context(nc.semaphore(name))

    def rep(x, axis, n):
        x = x.unsqueeze(axis)
        return x.broadcast_to([n if k == axis else d for k, d in enumerate(x.shape)])

    def wait(eng, s, value):
        if isinstance(value, int) and value <= 0:
            return
        eng.wait_ge(s, value)

    def hold(eng):
        eng.nop(nofuse=True)

    class Chain:

        def __init__(self, eng, s):
            self.eng, self.sem, self.base, self.n = eng, s, 0, 0

        def link(self, ins):
            self.n += 1
            ins.then_inc(self.sem, 1)
            self.eng.wait_ge(self.sem, self.base + self.n)

        def loop(self, i, per):
            self.start, self.per = self.base + self.n, per
            self.base, self.n = self.start + i * per, 0

        def looped(self, count):
            assert self.n == self.per, (self.n, self.per)
            self.base, self.n = self.start + count * self.per, 0

    with ctx:
        ident = sb("ident", [P, P])
        ident_b = sb("ident_b", [P, P], BF16)
        ones_b = sb("ones_b", [P, P], BF16)
        iota = sb("iota", [P, T])
        lower = sb("lower", [P, NX * NX])
        eps_t = sb("eps_t", [P, 1])
        spread = sb("spread", [3 * NX, NX, P], BF16)
        partmask = sb("partmask", [CP * NX, 3])
        gnn0_w = sb("gnn0_w", [P, 2 * KD, D])
        gnn0_b = sb("gnn0_b", [P, D])
        wg0 = sb("wg0", [P, KD, NX])
        gb0 = sb("gb0", [P, 2, NX])
        SLOT = (KD * HC0 * P, KD * HC1 * P)
        wbuf = sb("wbuf", [P, (2 * NX + 1) * SLOT[0]])
        wbuf_h = wbuf[:, :].bitcast(F16)
        b1_0 = sb("b1_0", [P, NX, HC0])
        wp = sb("wp", [P, KD, P])
        bp = sb("bp", [P, 1])
        gnn1_w = sb("gnn1_w", [P, 2, D])
        gnn1_b = sb("gnn1_b", [P, 2, D])
        wg1 = sb("wg1", [P, KD, NX])
        wgh = [sb(f"wgh{i}", [P, 2, KD, NX], F16) for i in range(2)]
        mag = [sb(f"mag{i}", [P, 4]) for i in range(2)]
        magr = [sb(f"magr{i}", [P, 4]) for i in range(2)]
        bits = sb("bits", [P, 4], I32)
        scl = [sb(f"scl{i}", [P, 8]) for i in range(2)]
        b1_1 = sb("b1_1", [P, NX, HC1])
        b2s = [sb(f"b2s{i}", [CP * NX, D], BF16) for i in range(2)]

        src_s = sb("src_s", [P, ET], I32)
        w_s = [sb(f"w_s{i}", [P, ET]) for i in range(2)]
        dst_f = sb("dst_f", [P, NG, SUB])
        drel = sb("drel", [P, NG, SUB])
        floor_s = sb("floor_s", [P, NG])
        rel = sb("rel", [P, NG])
        base_i = sb("base_i", [P, NG + 2], I32)
        flag_f = sb("flag_f", [P, 2])
        flag_i = sb("flag_i", [1, 1], I32)
        RING = [4, 8]
        ring = sb("ring", [P, RING[0] * SUB * D])
        ringv = [ring[:, :].rearrange("p (r k d) -> p r k d", r=RING[0], k=SUB),
                 ring[:, :].rearrange("p (r k d) -> p r k d", r=RING[1], k=SUB)]
        idx = sb("idx", [P, 8, SUB], I32)
        oh = sb("oh", [P, 4, SUB, W], BF16)
        ohw = sb("ohw", [P, 4, SUB, W])
        acc = sb("acc", [P, 3, WACC])
        cnt = sb("cnt", [P, 2, T])
        aggs = sb("aggs", [P, KD, T])

        xin = sb("xin", [PT, SUB, D])
        feat = sb("feat", [PT, SUB, D])
        featT = sb("featT", [P, KD, T])
        res = [sb(f"res{i}", [PT, SUB, D]) for i in range(2)]
        xn = sb("xn", [PT, SUB, D])
        xnT = [sb(f"xnT{i}", [P, 2, KD, T], F16) for i in range(2)]
        hid = [sb(f"hid{i}", [P, T]) for i in range(2)]
        hsc = [sb(f"hsc{i}", [P, 2, T], F16) for i in range(2)]
        yT = sb("yT", [P, KD, T])
        x2 = sb("x2", [PT, SUB, D])
        x2T = sb("x2T", [P, KD, T])
        hT = sb("hT", [P, T])
        hp = sb("hp", [PT, SUB, P])
        stats = [sb(f"stats{i}", [PT, SUB, 6]) for i in range(2)]
        mv = [sb(f"mv{i}", [PT, SUB, 2]) for i in range(2)]
        sd = [sb(f"sd{i}", [PT, SUB]) for i in range(2)]
        rs = [sb(f"rs{i}", [PT, SUB]) for i in range(2)]
        lg = sb("lg", [PT, SUB, NX])
        lgd = sb("lgd", [PT, SUB, NX])
        ex = sb("ex", [PT, SUB, NX])
        pr = sb("pr", [PT, SUB, NX])
        m4 = sb("m4", [PT, 4, SUB])
        gt = sb("gt", [PT, SUB, NX, NX])
        eq = sb("eq", [PT, SUB, NX, NX])
        mask = sb("mask", [PT, SUB, NX])
        comb = sb("comb", [PT, SUB, NX])
        crem = sb("crem", [PT, SUB, NX])
        c72 = sb("c72", [PT, SUB, CP * NX], BF16)
        xn2 = xn
        hTl = featT[:, 0, :]
        spread_f = x2[0:3 * NX, :, :].rearrange("p s d -> p (s d)")
        dst_s = ring[:, 0:ET].bitcast(I32)
        ext = x2T[:, :, :].rearrange("p k n -> p (k n)")[:, 0:2 * NG]
        extr = yT[:, :, :].rearrange("p k n -> p (k n)")[:, 0:2 * NG]
        chk = aggs[:, :, :].rearrange("p k n -> p (k n)")[:, 0:3 * NG].rearrange("p (a g) -> p a g", a=3)
        b2f = featT[0:CP * NX, 1, 0:D]
        b2p = [yT[:, :, :].rearrange("p k n -> p (k n)")[0:CP * NX, k * D:(k + 1) * D] for k in range(3)]
        fb_oh = sb("fb_oh", [P, T], BF16)
        fb_d = sb("fb_d", [P, 1])
        fb_off = sb("fb_off", [P, 1])
        cT = [sb(f"cT{i}", [CP * NX, T], BF16) for i in range(2)]

        psH = [ctx.enter_context(nc.psum_tensor(f"psH{i}", [P, 512], F32)) for i in range(2)]
        psY = [ctx.enter_context(nc.psum_tensor(f"psY{i}", [P, 512], F32)) for i in range(2)]
        psC = ctx.enter_context(nc.psum_tensor("psC", [P, 512], F32))
        psE = ctx.enter_context(nc.psum_tensor("psE", [P, 512], F32))
        psM = [ctx.enter_context(nc.psum_tensor(f"psM{i}", [P, 512], F32)) for i in range(2)]

        cps = psM[1][:, :].bitcast(BF16).rearrange("p (s n) -> p s n", s=2 * SUB)

        s_const = sem("const_loaded")
        s_edge = sem("edges_loaded")
        s_wl = sem("weights_loaded")
        s_ext = sem("extremes_ready")
        s_extr = sem("extremes_reduced")
        s_flag = sem("flag_ready")
        s_ready = sem("constants_made")
        s_dve = sem("dve_chain")
        s_act = sem("act_chain")
        s_idx = [sem(f"idx_staged{i}") for i in range(2)]
        s_t0x = [sem(f"t0_x_loaded{i}") for i in range(2)]
        s_t0m = sem("t0_stats")
        s_t0s = sem("t0_sd")
        s_t0n = sem("t0_normed")
        s_t0w = [sem(f"t0_stored{i}") for i in range(2)]

        class Layer:

            def __init__(self, i):
                def s(name):
                    return sem(f"l{i}_{name}")

                self.onehot_ready = s("onehot_ready")
                self.group_summed = s("group_summed")
                self.window_added = s("window_added")
                self.agg_ready = s("agg_ready")
                self.agg_root = s("agg_root")
                self.feat_loaded = s("feat_loaded")
                self.xin_loaded = s("xin_loaded")
                self.featT_summed = s("featT_summed")
                self.featT_copied = s("featT_copied")
                self.lin_summed = s("lin_summed")
                self.res_ready = s("res_ready")
                self.ln_stats = s("ln_stats")
                self.ln_sd = s("ln_sd")
                self.xn_ready = s("xn_ready")
                self.xnT_summed = s("xnT_summed")
                self.xnT_copied = s("xnT_copied")
                self.xnT_ready = s("xnT_ready")
                self.logits_summed = s("logits_summed")
                self.logits_taken = s("logits_taken")
                self.exp_done = s("exp_done")
                self.comb_split = s("comb_split")
                self.combT_summed = s("combT_summed")
                self.comb_ready = s("comb_ready")
                self.spread_ready = s("spread_ready")
                self.hid_summed = s("hid_summed")
                self.hid_active = s("hid_active")
                self.hid_scaled = s("hid_scaled")
                self.hid_hi = s("hid_hi")
                self.hid_lo = s("hid_lo")
                self.experts_loaded = s("experts_loaded")
                self.mags_ready = s("mags_ready")
                self.mags_reduced = s("mags_reduced")
                self.scales_ready = s("scales_ready")
                self.w_hi = s("w_hi")
                self.w_lo = s("w_lo")
                self.hid_used = s("hid_used")
                self.ffn_summed = s("ffn_summed")
                self.y_copied = s("y_copied")
                self.ytok_summed = s("ytok_summed")
                self.out_ready = s("out_ready")
                self.out_stored = s("out_stored")
                self.fb_idx = s("fb_idx")
                self.fb_gathered = s("fb_gathered")
                self.fb_onehot = s("fb_onehot")
                self.fb_summed = s("fb_summed")
                self.fb_used = s("fb_used")
                self.fb_chain = s("fb_chain")
                self.fb_tile = s("fb_tile")
                self.fb_stored = s("fb_stored")
                self.seed_loaded = s("seed_loaded")
                self.seed_wanted = s("seed_wanted")
                self.i, self.HC = i, (HC0, HC1)[i]
                self.M = NX * self.HC
                self.R = RING[i]
                self.ring = ringv[i]
                self.gathered = [s(f"gathered{r}") for r in range(self.R)]
                self.b1, self.wg, self.wgh, self.w = (b1_0, b1_1)[i], (wg0, wg1)[i], wgh[i], w_s[i]
                self.slot, self.mag, self.magr = SLOT[i], mag[i], magr[i]
                c = [scl[i][:, k:k + 1] for k in range(8)]
                self.s_w1, self.s_w2, self.s_h, self.s_wg, self.un_up, self.un_y, self.un_h, self.un_g = c
                self.scales = scl[i]
                self.table, self.seed_d = (table0, table1)[i], (seed0_d, seed1_d)[i]
                self.parts = (3, 1)[i]
                self.at_take, self.at_lin, self.at_norm, self.at_gate, self.at_comb = (
                    (17, 18, 21, 23, 27), (8, 9, 11, 12, 13))[i]
                self.at_feat = 14
                self.per_step = (1, 2)[i]

            def raw(self, k, n=1):
                return wbuf[:, (k + 1) * self.slot:(k + 1 + n) * self.slot]

            def part(self, k, j):
                return wbuf_h[:, (2 * k + j) * self.slot:(2 * k + j + 1) * self.slot]

            def w1(self, e, j, k, c):
                o = (k * self.HC + c) * P
                return self.part(e, j)[:, o:o + P]

            def w2(self, e, j, c, d):
                o = c * D + d * P
                return self.part(NX + e, j)[:, o:o + P]

        L = [Layer(0), Layer(1)]
        s_ln2m, s_ln2s, s_x2n = sem("ln2_stats"), sem("ln2_sd"), sem("x2n_ready")
        s_x2Ts, s_x2T = sem("x2T_summed"), sem("x2T_copied")
        s_hraw, s_hT = sem("hT_summed"), sem("hT_ready")
        s_hps, s_hp = sem("hp_summed"), sem("hp_ready")
        s_hTw, s_hpw = sem("hT_stored"), sem("hp_stored")

        block = ctx.enter_context(nc.Block())

        LASTG = LAG + GPT

        def first_batches(l):
            return [list(range(g, g + l.per_step)) for g in range(0, LASTG, l.per_step)]

        def batch(l, n):
            first = l.per_step * (n - 1)
            return [LAG + first + k for k in range(l.per_step)] if 0 <= first < GPT else []

        def split_at(l, n):
            per, start = (1, 2)[l.i], (2, 1)[l.i]
            return range(max(0, per * (n - start)), max(0, per * (n - start + 1)))

        def iteration(l, emit, chain, per):
            emit(0, 0, True, False)
            emit(1, 1, False, False)
            with chain.eng.Fori(0, (NT - 3) // 2) as i:
                chain.loop(i, per)
                emit(2 * i + 2, 0, False, False)
                emit(2 * i + 3, 1, False, False)
            chain.looped((NT - 3) // 2)
            emit(NT - 1, 0, False, True)

        @block.sync
        def _(sp):
            for dst, s in ((ident, "ident"), (iota, "iota"), (lower, "lower"),
                           (partmask, "partmask"), (x2, "spread"), (floor_s, "floor")):
                dst = spread_f if s == "spread" else dst[:, :]
                sp.dma_start(dst, a[s]).then_inc(s_const, 16)
            for dst, s in ((src_s, "src"), (None, "dst"), (w_s[0], "w0"), (w_s[1], "w1")):
                sp.dma_start(dst_s if s == "dst" else dst[:, :], a[s]).then_inc(s_edge, 16)

            def t0_load(t, q):
                if not isinstance(t, int) or t >= 2:
                    sp.wait_ge(s_t0n, t - 1)
                sp.dma_start((xin, feat)[q][:, :, :].rearrange("p s d -> p (s d)"),
                             rows(a["x"], t)).then_inc(s_t0x[q], 16)

            def t0_store(t, q):
                sp.wait_ge(s_t0n, t + 1)
                sp.dma_start(rows(table0, t),
                             res[q][:, :, :].rearrange("p s d -> p (s d)")).then_inc(s_t0w[q], 16)

            t0_load(0, 0)
            t0_load(1, 1)
            with sp.Fori(0, (NT - 3) // 2) as i:
                t0_store(2 * i, 0)
                t0_load(2 * i + 2, 0)
                t0_store(2 * i + 1, 1)
                t0_load(2 * i + 3, 1)
            t0_store(NT - 3, 0)
            t0_load(NT - 1, 0)
            t0_store(NT - 2, 1)
            t0_store(NT - 1, 0)

            for dst, s in (
                (gnn0_w, "gnn0_w"), (wg0, "wg0"), (b1_0, "b1_0"),
                (wp, "wp"), (gnn1_w, "gnn1_w"), (wg1, "wg1"),
                (b1_1, "b1_1"),
            ):
                sp.dma_start(dst[:, :, :], a[s]).then_inc(s_wl, 16)
            sp.dma_start(bp[:, :], a["bp"]).then_inc(s_wl, 16)
            sp.dma_start(gnn0_b[:, :], a["gnn0_b"].broadcast_to((P, a["gnn0_b"].shape[1]))).then_inc(s_wl, 16)
            sp.dma_start(gnn1_b[:, 0, :], a["gnn1_b1"].broadcast_to((P, a["gnn1_b1"].shape[1]))).then_inc(s_wl, 16)
            sp.dma_start(gnn1_b[:, 1, :], a["gnn1_b2"].broadcast_to((P, a["gnn1_b2"].shape[1]))).then_inc(s_wl, 16)
            sp.dma_start(gb0[:, 0, :], a["bg"].broadcast_to((P, a["bg"].shape[1]))).then_inc(s_wl, 16)
            sp.dma_start(gb0[:, 1, :], a["bias"].broadcast_to((P, a["bias"].shape[1]))).then_inc(s_wl, 16)

            def experts_load(l):
                sp.dma_start(l.raw(0, NX), a[("w1_0", "w1_1")[l.i]]).then_inc(l.experts_loaded, 16)
                sp.dma_start(l.raw(NX, NX), a[("w2_0", "w2_1")[l.i]]).then_inc(l.experts_loaded, 16)
                for k in range(CP):
                    sp.dma_start(b2f[k * NX:(k + 1) * NX, :], a[("b2_0", "b2_1")[l.i]])\
                      .then_inc(l.experts_loaded, 16)

            experts_load(L[0])
            sp.wait_ge(s_flag, 1)
            flag = sp.value_load(flag_i[0:1, 0:1], min_val=0, max_val=1)

            def general_store(l):
                with sp.If(flag):
                    with sp.Fori(0, NT) as u:
                        sp.wait_ge(l.fb_tile, u + 1)
                        sp.dma_start(l.seed_d[bass.ds(u, 1), :, :].rearrange(
                            "o p (k n) -> (o p) k n", k=l.parts),
                            acc[:, 0:l.parts, 0:T]).then_inc(l.fb_stored, 16)

            def seed_load(l, u):
                with sp.If(flag):
                    sp.wait_ge(l.seed_wanted, u + 1)
                    sp.dma_start(acc[:, 0:l.parts, 0:T], l.seed_d[bass.ds(u, 1), :, :].rearrange(
                        "o p (k n) -> (o p) k n", k=l.parts)).then_inc(l.seed_loaded, 16)

            def inputs(l, u):
                if l.i == 0:
                    wait(sp, l.featT_summed, 2 * u)
                    sp.dma_start(feat[:, :, :].rearrange("p s d -> p (s d)"), rows(table0, u))\
                      .then_inc(l.feat_loaded, 16)
                    src = a["x"]
                else:
                    wait(sp, l.lin_summed, 2 * u)
                    sp.dma_start(hTl, hT_d[bass.ds(u, 1), :, :].rearrange(
                        "o p n -> (o p) n")).then_inc(l.feat_loaded, 16)
                    src = x2_d
                wait(sp, l.res_ready, u)
                sp.dma_start(xin[:, :, :].rearrange("p s d -> p (s d)"), rows(src, u))\
                  .then_inc(l.xin_loaded, 16)

            def results0(tt):
                sp.wait_ge(L[0].out_ready, 2 * tt + 2)
                sp.dma_start(rows(x2_d, tt), x2[:, :, :].rearrange("p s d -> p (s d)"))\
                  .then_inc(L[0].out_stored, 16)
                sp.wait_ge(s_hT, tt + 1)
                sp.dma_start(hT_d[bass.ds(tt, 1), :, :].rearrange("o p n -> (o p) n"), hT[:, :])\
                  .then_inc(s_hTw, 16)
                sp.wait_ge(s_hp, tt + 1)
                sp.dma_start(rows(table1, tt), hp[:, :, :].rearrange("p s d -> p (s d)"))\
                  .then_inc(s_hpw, 16)

            def results1(tt, last=False):
                sp.wait_ge(L[1].out_ready, 2 * tt + 2)
                if not last:
                    sp.dma_start(rows(a["out"], tt), x2[:, :, :].rearrange("p s d -> p (s d)"))\
                      .then_inc(L[1].out_stored, 16)
                    return
                left = n_nodes - tt * T
                full, rest = left // SUB, left % SUB
                sp.dma_start(a["out"][tt * T:tt * T + full * SUB, :].rearrange(
                    "(p s) d -> p (s d)", s=SUB),
                    x2[0:full, :, :].rearrange("p s d -> p (s d)")).then_inc(L[1].out_stored, 16)
                if rest:
                    sp.dma_start(a["out"][tt * T + full * SUB:n_nodes, :].rearrange(
                        "(o s) d -> o (s d)", o=1),
                        x2[full:full + 1, 0:rest, :].rearrange("p s d -> p (s d)"))\
                      .then_inc(L[1].out_stored, 16)

            for q in range(2):
                sp.wait_ge(s_t0w[q], 16 * ((NT + 1 - q) // 2))
            general_store(L[0])
            ends = Chain(sp, s_act)
            for l, results in ((L[0], results0), (L[1], results1)):
                if l.i == 1:
                    sp.wait_ge(L[0].hid_used, L[0].M * NT)
                    experts_load(l)
                    general_store(l)
                    sp.wait_ge(L[0].out_stored, 16 * NT)
                    sp.wait_ge(s_hTw, 16 * NT)
                inputs(l, 0)
                seed_load(l, 0)

                def tile(t, q, first, last):
                    if not first:
                        results(t - 1)
                    if not last:
                        inputs(l, t + 1)
                        seed_load(l, t + 1)

                iteration(l, tile, ends, 0)
                if l.i == 0:
                    results(NT - 1)
                else:
                    results(NT - 1, last=True)
            stores = NT + (1 if (n_nodes - (NT - 1) * T) % SUB else 0)
            sp.wait_ge(L[1].out_stored, 16 * stores)
            sp.wait_ge(s_hpw, 16 * NT)

        @block.gpsimd
        def _(pool):
            pool.wait_ge(s_ext, 1)
            pool.partition_all_reduce(extr, ext, P, RMAX).then_inc(s_extr, 1)
            pool.wait_ge(s_edge, 64)
            pool.wait_ge(s_flag, 1)
            flag = pool.value_load(flag_i[0:1, 0:1], min_val=0, max_val=1)

            def general_gather(l):
                with pool.If(flag):
                    with pool.Fori(0, NT) as u:
                        with pool.Fori(0, ET) as j:
                            n = u * ET + j
                            pool.wait_ge(l.fb_used, n + 1)
                            pool.tensor_copy(idx[:, 0, 0:1], src_s[:, bass.ds(j, 1)])\
                                .then_inc(l.fb_idx, 1)
                            pool.wait_ge(l.fb_idx, n + 1)
                            hold(pool)
                            pool.indirect_dma_start(
                                out=l.ring[:, 0, 0, :], out_offset=None, in_=l.table,
                                in_offset=bass.IndirectOffsetOnAxis(ap=idx[:, 0, 0:1], axis=0))\
                                .then_inc(l.fb_gathered, 16)
                    pool.wait_ge(l.fb_used, NT * ET + 1)

            def gather_group(l, it, g8):
                g = 8 * it + g8
                wait(pool, l.group_summed, g - l.R + 1)
                pool.tensor_copy(idx[:, g8, :], src_s[:, bass.ds(g * SUB, SUB)])\
                    .then_inc(s_idx[l.i], 1)
                pool.wait_ge(s_idx[l.i], g + 1)
                hold(pool)
                for k in range(SUB):
                    pool.indirect_dma_start(
                        out=l.ring[:, g8 % l.R, k, :], out_offset=None, in_=l.table,
                        in_offset=bass.IndirectOffsetOnAxis(ap=idx[:, g8, k:k + 1], axis=0))\
                        .then_inc(l.gathered[g8 % l.R], 16)

            for l in L:
                if l.i == 0:
                    for q in range(2):
                        pool.wait_ge(s_t0w[q], 16 * ((NT + 1 - q) // 2))
                else:
                    pool.wait_ge(L[0].group_summed, NG)
                    pool.wait_ge(s_hpw, 16 * NT)
                general_gather(l)
                for g8 in range(8):
                    if g8 == 4:
                        pool.wait_ge(l.mags_ready, 1)
                        pool.partition_all_reduce(l.magr[:, :], l.mag[:, :], P, RMAX)\
                            .then_inc(l.mags_reduced, 1)
                    gather_group(l, 0, g8)
                with pool.Fori(1, NG // 8) as it:
                    for g8 in range(8):
                        gather_group(l, it, g8)
                for g8 in range(NG % 8):
                    gather_group(l, NG // 8, g8)

        @block.tensor
        def _(pe):
            pe.wait_ge(s_ready, 1)
            pe.wait_ge(s_wl, 16 * 13)
            flag = pe.value_load(flag_i[0:1, 0:1], min_val=0, max_val=1)
            mm = pe.matmul

            def general_sums(l):
                with pe.If(flag):
                    with pe.Fori(0, NT) as u:
                        with pe.Fori(0, ET) as j:
                            n = u * ET + j
                            pe.wait_ge(l.fb_onehot, n + 1)
                            pe.wait_ge(l.fb_gathered, 16 * n + 16)
                            if l.i == 0:
                                mm(psH[0][:, 0:T], l.ring[:, 0, 0, 0:P], hid[0][:, :], start=True, stop=True)
                                mm(psH[1][:, 0:T], l.ring[:, 0, 0, P:D], hid[0][:, :], start=True, stop=True)
                                mm(psC[:, 0:T], ones_b[:, :], fb_oh[:, :], start=True, stop=True)\
                                    .then_inc(l.fb_summed, 1)
                            else:
                                mm(psC[:, 0:T], l.ring[:, 0, 0, :], hid[0][:, :], start=True, stop=True)\
                                    .then_inc(l.fb_summed, 1)

            def sum_groups(l, u, js):
                pe.wait_ge(l.onehot_ready, GPT * u + js[-1] + 1)
                wait(pe, l.window_added, GPT * u + js[0])
                for i, j in enumerate(js):
                    r, q = j % l.R, j % 4
                    pe.wait_ge(l.gathered[r], 16 * SUB * ((GPT // l.R) * u + j // l.R + 1))
                    o = i * l.parts * W
                    for h in range(KD if l.i == 0 else 1):
                        for k in range(SUB):
                            last = mm(psE[:, o + h * W:o + (h + 1) * W], l.ring[:, r, k, h * P:(h + 1) * P],
                                      ohw[:, q, k, :], start=(k == 0), stop=(k == SUB - 1))
                    if l.i == 0:
                        for k in range(SUB):
                            last = mm(psE[:, o + 2 * W:o + 3 * W], ones_b[:, :], oh[:, q, k, :],
                                      start=(k == 0), stop=(k == SUB - 1))
                    last.then_inc(l.group_summed, 1)

            def up(l, t, q, n):
                e, c = n // l.HC, n % l.HC
                wait(pe, l.hid_active, l.M * t + n - 1)
                for k in range(KD):
                    for m, (i, j) in enumerate(PARTS):
                        last = mm(psH[n % 2][:, 0:T], l.w1(e, i, k, c), xnT[q][:, j, k, :],
                                  start=(k == 0 and m == 0), stop=(k == KD - 1 and m == 2))
                last.then_inc(l.hid_summed, 1)

            def spread_weights(l, t, q, e):
                wait(pe, l.hid_scaled, l.M * t + l.HC * e)
                mm(psC[:, 0:T], spread[:, e, :], cT[q][0:3 * NX, :], start=True, stop=True)\
                    .then_inc(l.spread_ready, 1)

            def down(l, t, q, n):
                e, c = n // l.HC, n % l.HC
                if n == 0:
                    wait(pe, l.y_copied, t)
                    for d in range(KD):
                        mm(psY[d][:, 0:T], b2s[l.i][:, d * P:(d + 1) * P], cT[q][:, :],
                           start=True, stop=False)
                pe.wait_ge(l.hid_lo, l.M * t + n + 1)
                for d in range(KD):
                    for m, (i, j) in enumerate(PARTS):
                        last = mm(psY[d][:, 0:T], l.w2(e, i, c, d), hsc[n % 2][:, j, :],
                                  start=False, stop=(n == l.M - 1 and m == 2))
                last.then_inc(l.hid_used, 1)

            def back_to_tokens(l, tt):
                pe.wait_ge(l.y_copied, tt + 1)
                for b in range(2):
                    for s in (2 * b, 2 * b + 1):
                        for k in range(KD):
                            last = pe.transpose(psM[b][0:PT, (s % 2) * D + k * P:(s % 2) * D + (k + 1) * P],
                                                yT[:, k, s * PT:(s + 1) * PT], ident[:, :])
                    last.then_inc(l.ytok_summed, 1)

            def to_features(src, b, k, then):
                for s in range(SUB):
                    last = pe.transpose(psM[b][:, s * PT:(s + 1) * PT], src[:, s, k * P:(k + 1) * P],
                                        ident[0:PT, 0:PT])
                last.then_inc(then, 1)

            def project(tt):
                pe.wait_ge(s_x2T, 2 * tt + 2)
                for k in range(KD):
                    last = mm(psM[0][:, 0:T], wp[:, k, :], x2T[:, k, :], start=(k == 0), stop=(k == KD - 1))
                last.then_inc(s_hraw, 1)

            def project_tokens(tt):
                pe.wait_ge(s_hT, tt + 1)
                for s in range(SUB):
                    last = pe.transpose(psM[1][0:PT, s * P:(s + 1) * P], hT[:, s * PT:(s + 1) * PT],
                                        ident[:, :])
                last.then_inc(s_hps, 1)

            def feat_transposed(l, u):
                pe.wait_ge(l.feat_loaded, 16 * u + 16)
                wait(pe, s_hT, u - 1)
                wait(pe, l.logits_taken, u)
                to_features(feat, 0, 0, l.featT_summed)
                wait(pe, s_hp, u - 1)
                wait(pe, l.comb_ready, u)
                to_features(feat, 1, 1, l.featT_summed)

            def linear(l, u):
                if l.i == 0:
                    pe.wait_ge(l.featT_copied, 2 * u + 2)
                    pe.wait_ge(l.agg_ready, u + 1)
                    parts = [(aggs[:, k, :], gnn0_w[:, k, :]) for k in range(KD)]
                    parts += [(featT[:, k, :], gnn0_w[:, KD + k, :]) for k in range(KD)]
                else:
                    wait(pe, l.out_ready, 2 * u - 2)
                    wait(pe, l.logits_taken, u)
                    wait(pe, l.comb_ready, u)
                    pe.wait_ge(l.feat_loaded, 16 * u + 16)
                    pe.wait_ge(l.agg_root, u + 1)
                    parts = [(hTl, gnn1_w[:, 0, :]), (aggs[:, 1, :], gnn1_w[:, 1, :])]
                for b in range(2):
                    for s in (2 * b, 2 * b + 1):
                        for m, (x, w) in enumerate(parts):
                            last = mm(psM[b][0:PT, (s % 2) * D:(s % 2 + 1) * D],
                                      x[:, s * PT:(s + 1) * PT], w, start=(m == 0), stop=(m == len(parts) - 1))
                    last.then_inc(l.lin_summed, 1)

            def normed_transposed(l, u):
                pe.wait_ge(l.xn_ready, u + 1)
                for k in range(KD):
                    to_features(xn, k, k, l.xnT_summed)

            def logits(l, u, q):
                pe.wait_ge(l.xnT_ready, 2 * u + 2)
                for s in range(SUB):
                    for k in range(KD):
                        for m, (i, j) in enumerate(PARTS):
                            last = mm(psM[0][0:PT, s * NX:(s + 1) * NX],
                                      xnT[q][:, j, k, s * PT:(s + 1) * PT], l.wgh[:, i, k, :],
                                      start=(k == 0 and m == 0), stop=(k == KD - 1 and m == 2))
                last.then_inc(l.logits_summed, 1)

            def weights_transposed(l, u):
                pe.wait_ge(l.comb_split, u + 1)
                for s in range(SUB):
                    last = pe.transpose(cps[0:CP * NX, s, 0:PT], c72[:, s, :], ident_b[0:PT, 0:PT])
                last.then_inc(l.combT_summed, 1)

            for l in L:
                general_sums(l)
                for js in first_batches(l):
                    sum_groups(l, 0, js)
                pe.wait_ge(l.scales_ready, 1)
                if l.i == 0:
                    feat_transposed(l, 0)
                linear(l, 0)
                normed_transposed(l, 0)
                logits(l, 0, 0)
                weights_transposed(l, 0)
                pe.wait_ge(l.w_lo, 2 * NX)
                pe.wait_ge(l.comb_ready, 1)
                up(l, 0, 0, 0)
                spread_weights(l, 0, 0, 0)
                up(l, 0, 0, 1)

                def tile(t, q, first, last):
                    for n in range(l.M):
                        if n + 2 < l.M:
                            up(l, t, q, n + 2)
                        elif not last:
                            if n + 2 == l.M:
                                pe.wait_ge(l.comb_ready, t + 2)
                            up(l, t + 1, 1 - q, n + 2 - l.M)
                        if n + 2 < l.M and (n + 2) % l.HC == 0:
                            spread_weights(l, t, q, (n + 2) // l.HC)
                        if n + 2 == l.M and not last:
                            spread_weights(l, t + 1, 1 - q, 0)
                        down(l, t, q, n)
                        if n == 1 and not first:
                            back_to_tokens(l, t - 1)
                        if l.i == 0 and not first:
                            if n == 6:
                                pe.wait_ge(s_x2n, t)
                                to_features(xn2, 0, 0, s_x2Ts)
                                to_features(xn2, 1, 1, s_x2Ts)
                            if n == 9:
                                project(t - 1)
                            if n == 11:
                                project_tokens(t - 1)
                        if last:
                            continue
                        if batch(l, n):
                            sum_groups(l, t + 1, batch(l, n))
                        if n == l.at_feat and l.i == 0:
                            feat_transposed(l, t + 1)
                        if n == l.at_lin:
                            linear(l, t + 1)
                        if n == l.at_norm:
                            normed_transposed(l, t + 1)
                        if n == l.at_gate:
                            logits(l, t + 1, 1 - q)
                        if n == l.at_comb:
                            weights_transposed(l, t + 1)

                iteration(l, tile, Chain(pe, s_act), 0)
                pe.wait_ge(s_hp, NT - 1) if l.i == 0 else pe.wait_ge(l.out_ready, 2 * NT - 2)
                back_to_tokens(l, NT - 1)
                if l.i == 0:
                    pe.wait_ge(s_x2n, NT)
                    to_features(xn2, 0, 0, s_x2Ts)
                    to_features(xn2, 1, 1, s_x2Ts)
                    project(NT - 1)
                    project_tokens(NT - 1)

        @block.vector
        def _(dve):
            c = Chain(dve, s_dve)
            link = c.link
            tt_, ts_ = dve.tensor_tensor, dve.tensor_scalar

            dve.wait_ge(s_const, 16 * 6)
            dve.memset(ones_b[:, :], 1.0)
            dve.memset(eps_t[:, :], EPS)
            dve.memset(acc[:, :, :], 0.0)
            dve.memset(base_i[:, :], 0)
            dve.tensor_copy(ident_b[:, :], ident[:, :])
            link(dve.tensor_copy(spread[:, :, :].rearrange("k e p -> k (e p)"), spread_f))

            dve.wait_ge(s_edge, 64)
            link(dve.tensor_copy(dst_f[:, :, :].rearrange("p g k -> p (g k)"), dst_s))
            link(ts_(drel[:, :, :], dst_f[:, :, :], -1.0, None, ALU.mult))
            dve.reduce_max(ext[:, 0:NG], dst_f[:, :, :], AX)
            dve.reduce_max(ext[:, NG:2 * NG], drel[:, :, :], AX).then_inc(s_ext, 1)
            dve.wait_ge(s_extr, 1)
            hi, neg = extr[:, 0:NG], extr[:, NG:2 * NG]
            link(tt_(rel[:, :], neg, floor_s[:, :], ALU.add))
            link(ts_(rel[:, :], rel[:, :], -1.0, None, ALU.mult))
            link(tt_(chk[:, 2, :], hi, neg, ALU.add))
            ts_(chk[:, 0, :], rel[:, :], 0.0, None, ALU.is_lt)
            ts_(chk[:, 1, :], rel[:, :], float(WACC - W), None, ALU.is_gt)
            link(ts_(chk[:, 2, :], chk[:, 2, :], float(W - 1), None, ALU.is_gt))
            link(dve.reduce_max(flag_f[:, 0:1], chk.rearrange("p a g -> p (a g)"), AX))
            link(ts_(flag_f[:, 1:2], flag_f[:, 0:1], -1.0, 1.0, ALU.mult, ALU.add))
            link(ts_(rel[:, :], rel[:, :], 0.0, float(WACC - W), ALU.max, ALU.min))
            dve.tensor_copy(base_i[:, 2:NG + 2], rel[:, :])
            link(tt_(drel[:, :, :], dst_f[:, :, :], rep(neg, 2, SUB), ALU.add))
            link(ts_(drel[:, :, :], drel[:, :, :], flag_f[:, 1:2], flag_f[:, 0:1], ALU.mult, ALU.subtract))
            link(dve.tensor_copy(flag_i[:, :], flag_f[0:1, 0:1]))
            dve.sem_inc(s_flag, 1)

            def ln_moments(x, i, then):
                for s in range(SUB):
                    last = dve.bn_stats(stats[i][:, s, :], x[:, s, :])
                link(last)
                hold(dve)
                for s in range(SUB):
                    last = dve.bn_aggr(mv[i][:, s, :], stats[i][:, s, :])
                last.then_inc(then, 1)

            def ln_apply(out, x, i, then):
                link(dve.reciprocal(rs[i][:, :], sd[i][:, :]))
                for s in range(SUB):
                    last = ts_(out[:, s, :], x[:, s, :], mv[i][:, s, 0:1], rs[i][:, s:s + 1],
                               ALU.subtract, ALU.mult)
                last.then_inc(then, 1)

            def table_tile(t, q, k):
                dve.wait_ge(s_t0x[q], 16 * k + 16)
                x = (xin, feat)[q]
                if not isinstance(t, int) or t >= 2:
                    dve.wait_ge(s_t0w[q], 16 * k)
                ln_moments(x, 0, s_t0m)
                dve.wait_ge(s_t0s, t + 1)
                ln_apply(res[q], x, 0, s_t0n)
                dve.wait_ge(s_t0n, t + 1)
                hold(dve)

            table_tile(0, 0, 0)
            table_tile(1, 1, 0)
            with dve.Fori(1, (NT - 1) // 2) as i:
                c.loop(i - 1, 4)
                table_tile(2 * i, 0, i)
                table_tile(2 * i + 1, 1, i)
            c.looped((NT - 1) // 2 - 1)
            table_tile(NT - 1, 0, (NT - 1) // 2)

            dve.sem_inc(s_ready, 1)
            dve.wait_ge(s_wl, 16 * 13)

            def magnitudes(l):
                dve.wait_ge(l.experts_loaded, 16 * (2 + CP))

                def largest(k, x):
                    return dve.tensor_reduce(l.mag[:, k:k + 1], x, AX, ALU.max,
                                             apply_absolute_value=True)

                largest(0, l.raw(0, NX))
                largest(1, l.raw(NX, NX))
                largest(2, l.b1[:, :, :].rearrange("p e c -> p (e c)"))
                largest(3, l.wg[:, :, :].rearrange("p k e -> p (k e)")).then_inc(l.mags_ready, 1)

            def scales(l):
                dve.wait_ge(l.mags_reduced, 1)
                m, up, un = l.magr[:, :], l.scales[:, 0:4], l.scales[:, 4:8]
                link(dve.scalar_tensor_tensor(m[:, 2:3], m[:, 0:1], float(D), m[:, 2:3],
                                              ALU.mult, ALU.add))
                link(ts_(m, m, TINY, None, ALU.max))
                link(ts_(bits[:, :], m.bitcast(I32), EXP_MASK, None, ALU.bitwise_and))
                link(ts_(bits[:, :], bits[:, :], -1.0, float(268 * ONE_EXP), ALU.mult, ALU.add))
                link(dve.tensor_copy(up.bitcast(I32), bits[:, :]))
                link(ts_(bits[:, :], bits[:, :], -1.0, float(254 * ONE_EXP), ALU.mult, ALU.add))
                link(dve.tensor_copy(un.bitcast(I32), bits[:, :]))
                ts_(l.un_up, l.un_up, 1.0 / XS, None, ALU.mult)
                ts_(l.un_g, l.un_g, 1.0 / XS, None, ALU.mult)
                link(tt_(l.un_y, l.un_y, l.un_h, ALU.mult))
                link(ts_(l.wgh[:, 0, :, :], l.wg[:, :, :], l.s_wg, None, ALU.mult))
                dve.scalar_tensor_tensor(l.wgh[:, 1, :, :], l.wg[:, :, :], l.s_wg, l.wgh[:, 0, :, :],
                                         ALU.mult, ALU.subtract)
                bb, n = b2s[l.i][:, :], CP * NX
                link(ts_(b2f, b2f, l.s_w2[0:n, :], None, ALU.mult))
                for k in range(3):
                    link(dve.tensor_copy(bb, b2f))
                    link(dve.tensor_copy(b2p[k], bb))
                    link(tt_(b2f, b2f, b2p[k], ALU.subtract))
                link(ts_(b2p[0], b2p[0], partmask[:, 0:1], None, ALU.mult))
                link(dve.scalar_tensor_tensor(b2p[0], b2p[1], partmask[:, 1:2], b2p[0], ALU.mult, ALU.add))
                link(dve.scalar_tensor_tensor(bb, b2p[2], partmask[:, 2:3], b2p[0], ALU.mult, ALU.add))
                dve.sem_inc(l.scales_ready, 1)

            def matrix_low(l, k):
                dve.wait_ge(l.w_hi, k + 1)
                dve.scalar_tensor_tensor(l.part(k, 1), l.raw(k), l.s_w1 if k < NX else l.s_w2,
                                         l.part(k, 0), ALU.mult, ALU.subtract).then_inc(l.w_lo, 1)

            flag = dve.value_load(flag_i[0:1, 0:1], min_val=0, max_val=1)

            def general_windows(l):
                per = ET + 2
                d2 = dst_f[:, :, :].rearrange("p g k -> p (g k)")
                with dve.If(flag):
                    dve.memset(fb_off[:, :], 0.0).then_inc(l.fb_chain, 1)
                    dve.sem_inc(l.fb_used, 1)
                    with dve.Fori(0, NT) as u:
                        dve.wait_ge(l.fb_chain, u * per + 1)
                        dve.memset(acc[:, 0:l.parts, 0:T], 0.0).then_inc(l.fb_chain, 1)
                        with dve.Fori(0, ET) as j:
                            n = u * ET + j
                            dve.wait_ge(l.fb_chain, u * per + j + 2)
                            tt_(fb_d[:, :], d2[:, bass.ds(j, 1)], fb_off[:, :], ALU.subtract)\
                                .then_inc(l.fb_chain, 1)
                            dve.wait_ge(l.fb_chain, u * per + j + 3)
                            hold(dve)
                            ts_(fb_oh[:, :], iota[:, :], fb_d[:, 0:1], None, ALU.is_equal)
                            ts_(hid[0][:, :], iota[:, :], fb_d[:, 0:1], l.w[:, bass.ds(j, 1)],
                                ALU.is_equal, ALU.mult).then_inc(l.fb_onehot, 1)
                            dve.wait_ge(l.fb_summed, n + 1)
                            for k in range(l.parts):
                                ps = (psH[0], psH[1], psC)[k] if l.i == 0 else psC
                                last = tt_(acc[:, k, 0:T], acc[:, k, 0:T], ps[:, 0:T], ALU.add)
                            last.then_inc(l.fb_used, 1)
                            dve.wait_ge(l.fb_used, n + 2)
                            hold(dve)
                        dve.wait_ge(l.fb_chain, u * per + ET + 2)
                        ts_(fb_off[:, :], fb_off[:, :], float(T), None, ALU.add).then_inc(l.fb_chain, 1)
                        dve.sem_inc(l.fb_tile, 1)
                        dve.wait_ge(l.fb_stored, 16 * u + 16)
                        hold(dve)
                    dve.memset(acc[:, :, :], 0.0).then_inc(l.fb_chain, 1)
                    dve.wait_ge(l.fb_chain, NT * per + 2)

            def onehots(l, u, j):
                g, q = GPT * u + j, j % 4
                wait(dve, l.group_summed, g - 3)
                ohw_e, oh_e = ohw[:, q, :, :], oh[:, q, :, :]
                d = rep(drel[:, bass.ds(g, 1), :].rearrange("p g k -> p (g k)"), 2, W)
                w = rep(l.w[:, bass.ds(g * SUB, SUB)], 2, W)
                i = rep(iota[:, 0:W], 1, SUB)
                link(tt_(oh_e, i, d, ALU.is_equal))
                tt_(ohw_e, oh_e, w, ALU.mult).then_inc(l.onehot_ready, 1)

            regs = {}

            def window_columns(l, u, j):
                n = 2 if j == 0 else 4
                cols = base_i[0:1, bass.ds(GPT * u + j + 2, n)]
                _, vals = nc.values_load_multi_w_load_instructions(
                    cols, engines=[mybir.EngineType.DVE], min_val=0, max_val=WACC - W,
                    skip_runtime_bounds_check_because="clamped to the range above")
                for k in range(n):
                    regs[j + k] = vals[k]

            def add_windows(l, u, js):
                dve.wait_ge(l.group_summed, GPT * u + js[-1] + 1)
                for i, j in enumerate(js):
                    if j == 0 or (j - LAG) % 4 == 0:
                        window_columns(l, u, j)
                    wait(dve, l.window_added, GPT * u + j)
                    v = acc[:, 0:l.parts, bass.ds(regs[j], W)]
                    ps = psE[:, i * l.parts * W:(i + 1) * l.parts * W].rearrange("p (k n) -> p k n", k=l.parts)
                    tt_(v, v, ps, ALU.add).then_inc(l.window_added, 1)

            def take(l, u):
                dve.wait_ge(l.window_added, GPT * u + LASTG)
                hold(dve)
                with dve.If(flag):
                    dve.sem_inc(l.seed_wanted, 1)
                    dve.wait_ge(l.seed_loaded, 16 * u + 16)
                    hold(dve)
                wait(dve, l.lin_summed, 2 * u)

                def perm(x):
                    return x.rearrange("c (q s) -> c q s", s=SUB)

                def placed(x):
                    return x.rearrange("c (s q) -> c q s", s=SUB)

                if l.i == 0:
                    link(ts_(cnt[:, 0, :], acc[:, 2, 0:T], 1.0, None, ALU.max))
                    link(dve.reciprocal(cnt[:, 1, :], cnt[:, 0, :]))
                    for k in range(KD):
                        last = tt_(placed(aggs[:, k, :]), perm(acc[:, k, 0:T]), perm(cnt[:, 1, :]), ALU.mult)
                    last.then_inc(l.agg_ready, 1)
                else:
                    dve.tensor_copy(placed(aggs[:, 0, :]), perm(acc[:, 0, 0:T])).then_inc(l.agg_ready, 1)
                dve.wait_ge(l.agg_ready, u + 1)
                link(dve.tensor_copy(acc[:, 0:l.parts, 0:WACC - T], acc[:, 0:l.parts, T:WACC]))
                link(dve.memset(acc[:, 0:l.parts, WACC - T:WACC], 0.0))

            def flat(x):
                return x.rearrange("p s d -> p (s d)")

            def residual(l, u, q):
                wait(dve, l.out_ready, 2 * u - 2)
                dve.wait_ge(l.xin_loaded, 16 * u + 16)
                for b in range(2):
                    dve.wait_ge(l.lin_summed, 2 * u + b + 1)
                    r = res[q][:, 2 * b:2 * b + 2, :]
                    p = psM[b][0:PT, :].rearrange("p (s d) -> p s d", s=2)
                    bias = rep((gnn0_b[0:PT, :] if l.i == 0 else gnn1_b[0:PT, 0, :]), 1, 2)
                    link(tt_(r, p, bias, ALU.add))
                    if l.i == 1:
                        bias2 = rep(gnn1_b[0:PT, 1, :], 1, 2)
                        link(tt_(r, r, bias2, ALU.add))
                    link(tt_(r, r, xin[:, 2 * b:2 * b + 2, :], ALU.add))
                dve.sem_inc(l.res_ready, 1)
                ln_moments(res[q], 0, l.ln_stats)

            def normed(l, u, q):
                dve.wait_ge(l.ln_sd, u + 1)
                wait(dve, l.xnT_summed, 2 * u)
                if l.i == 0:
                    wait(dve, s_x2Ts, 2 * u - 2)
                ln_apply(xn, res[q], 0, l.xn_ready)
                if l.i == 1:
                    dve.wait_ge(l.xn_ready, u + 1)
                    link(tt_(flat(res[q][:, :, :]), flat(res[q][:, :, :]), flat(xn[:, :, :]), ALU.add))

            def gate_max(l, u):
                dve.wait_ge(l.logits_summed, u + 1)
                ps = psM[0][0:PT, 0:SUB * NX].rearrange("p (s e) -> p s e", s=SUB)
                un = l.un_g[0:PT, :]
                if l.i == 0:
                    link(dve.scalar_tensor_tensor(lg[:, :, :], ps, un, rep(gb0[0:PT, 0, :], 1, SUB),
                                                  ALU.mult, ALU.add))
                    link(tt_(lg[:, :, :], lg[:, :, :], rep(gb0[0:PT, 1, :], 1, SUB), ALU.add))
                else:
                    link(ts_(lg[:, :, :], ps, un, None, ALU.mult))
                link(dve.reduce_max(m4[:, 0, :], lg[:, :, :], AX))
                tt_(lgd[:, :, :], lg[:, :, :], rep(m4[:, 0, :], 2, NX), ALU.subtract)\
                    .then_inc(l.logits_taken, 1)

            def gate_weights(l, u):
                dve.wait_ge(l.exp_done, u + 1)
                if l.i == 0:
                    key = lg
                else:
                    key = pr
                    link(dve.reduce_sum(m4[:, 1, :], ex[:, :, :], AX))
                    link(dve.reciprocal(m4[:, 2, :], m4[:, 1, :]))
                    link(tt_(pr[:, :, :], ex[:, :, :], rep(m4[:, 2, :], 2, NX), ALU.mult))
                other = rep(key[:, :, :], 2, NX)
                own = rep(key[:, :, :], 3, NX)
                tt_(gt[:, :, :, :], other, own, ALU.is_gt)
                link(tt_(eq[:, :, :, :], other, own, ALU.is_equal))
                low = rep(lower[0:PT, :], 1, SUB)
                e3 = eq[:, :, :, :].rearrange("p s e j -> p s (e j)")
                link(tt_(e3, e3, low, ALU.mult))
                link(tt_(gt[:, :, :, :], gt[:, :, :, :], eq[:, :, :, :], ALU.add))
                link(dve.reduce_sum(mask[:, :, :], gt[:, :, :, :], AX))
                link(ts_(mask[:, :, :], mask[:, :, :], 1.5, None, ALU.is_lt))
                link(tt_(comb[:, :, :], mask[:, :, :], (ex if l.i == 0 else pr)[:, :, :], ALU.mult))
                link(dve.reduce_sum(m4[:, 1, :], comb[:, :, :], AX))
                if l.i == 1:
                    link(ts_(m4[:, 1, :], m4[:, 1, :], 1e-12, None, ALU.max))
                link(dve.reciprocal(m4[:, 2, :], m4[:, 1, :]))
                link(ts_(m4[:, 2, :], m4[:, 2, :], l.s_h[0:PT, :], None, ALU.mult))
                link(tt_(crem[:, :, :], comb[:, :, :], rep(m4[:, 2, :], 2, NX), ALU.mult))
                wait(dve, l.combT_summed, u)
                for k in range(3):
                    c4 = c72[:, :, :].rearrange("p s (j i e) -> p s j i e", j=3, i=3)
                    link(dve.tensor_copy(c4[:, :, :, k, :], rep(crem[:, :, :], 2, 3)))
                    if k < 2:
                        link(tt_(crem[:, :, :], crem[:, :, :], c4[:, :, 0, k, :], ALU.subtract))
                dve.sem_inc(l.comb_split, 1)

            def normed_low(l, u, q):
                for k in range(KD):
                    dve.wait_ge(l.xnT_copied, 2 * u + k + 1)
                    dve.scalar_tensor_tensor(xnT[q][:, 1, k, :], psM[k][:, 0:T], XS, xnT[q][:, 0, k, :],
                                             ALU.mult, ALU.subtract).then_inc(l.xnT_ready, 1)

            def scale(l, t, n):
                dve.wait_ge(l.hid_active, l.M * t + n + 1)
                if n % l.HC == 0:
                    dve.wait_ge(l.spread_ready, NX * t + n // l.HC + 1)
                h = hid[n % 2][:, :]
                tt_(h, h, psC[:, 0:T], ALU.mult).then_inc(l.hid_scaled, 1)

            def hidden_low(l, t, n):
                dve.wait_ge(l.hid_hi, l.M * t + n + 1)
                tt_(hsc[n % 2][:, 1, :], hid[n % 2][:, :], hsc[n % 2][:, 0, :], ALU.subtract)\
                    .then_inc(l.hid_lo, 1)

            def result(l, tt, q):
                wait(dve, l.out_stored, 16 * tt)
                for b in range(2):
                    dve.wait_ge(l.ytok_summed, 2 * tt + b + 1)
                    v = x2[:, 2 * b:2 * b + 2, :]
                    tt_(v, res[q][:, 2 * b:2 * b + 2, :],
                        psM[b][0:PT, :].rearrange("p (s d) -> p s d", s=2), ALU.add)\
                        .then_inc(l.out_ready, 1)
                if l.i == 0:
                    dve.wait_ge(l.out_ready, 2 * tt + 2)
                    ln_moments(x2, 1, s_ln2m)

            def result_normed(tt, final=False):
                dve.wait_ge(s_ln2s, tt + 1)
                dve.wait_ge(L[0].xnT_summed, 2 * NT if final else 2 * tt + 4)
                ln_apply(xn2, x2, 1, s_x2n)

            for l in L:
                general_windows(l)
                magnitudes(l)
                todo = first_batches(l)
                for n, js in enumerate(todo):
                    for j in js:
                        onehots(l, 0, j)
                    if n:
                        add_windows(l, 0, todo[n - 1])
                    if n == (2, 1)[l.i]:
                        scales(l)
                    for k in split_at(l, n):
                        matrix_low(l, k)
                add_windows(l, 0, todo[-1])
                take(l, 0)
                residual(l, 0, 0)
                normed(l, 0, 0)
                normed_low(l, 0, 0)
                gate_max(l, 0)
                gate_weights(l, 0)
                scale(l, 0, 0)

                def tile(t, q, first, last):
                    for n in range(l.M):
                        if n + 1 < l.M:
                            scale(l, t, n + 1)
                        elif not last:
                            scale(l, t + 1, 0)
                        hidden_low(l, t, n)
                        if n and not last and batch(l, n - 1) and not (l.i == 1 and n - 1 == l.at_take):
                            add_windows(l, t + 1, batch(l, n - 1))
                        if not last:
                            for j in batch(l, n + 1):
                                onehots(l, t + 1, j)
                        if n == 2 and not first:
                            result(l, t - 1, 1 - q)
                        if n == 4 and not first and l.i == 0:
                            result_normed(t - 1)
                        if last:
                            continue
                        if n == l.at_take:
                            if l.i == 1:
                                add_windows(l, t + 1, batch(l, n))
                            take(l, t + 1)
                        if n == l.at_lin + 1:
                            residual(l, t + 1, 1 - q)
                        if n == (l.at_norm - 1):
                            normed(l, t + 1, 1 - q)
                        if n == l.at_norm + (1, 0)[l.i]:
                            normed_low(l, t + 1, 1 - q)
                        if n == l.at_gate + (1, 0)[l.i]:
                            gate_max(l, t + 1)
                        if n == l.at_gate + (2, 0)[l.i]:
                            gate_weights(l, t + 1)

                iteration(l, tile, c, (92, 96)[l.i])
                result(l, NT - 1, 0)
                if l.i == 0:
                    result_normed(NT - 1, final=True)
                    link(dve.memset(acc[:, :, :], 0.0))

        @block.scalar
        def _(act):
            f = act.activation

            def root(i, then):
                f(sd[i][:, :], mv[i][:, :, 1], ACT.Sqrt, bias=eps_t[0:PT, :]).then_inc(then, 1)

            with act.Fori(0, NT) as t:
                act.wait_ge(s_t0m, t + 1)
                root(0, s_t0s)

            def copied(dst, k, ready, value, then):
                act.wait_ge(ready, value)
                f(dst, psM[k][:, 0:T], ACT.Copy).then_inc(then, 1)

            def take_root(l, u):
                act.wait_ge(l.agg_ready, u + 1)
                f(aggs[:, 1, :], aggs[:, 0, :], ACT.Sqrt).then_inc(l.agg_root, 1)

            def feat_copied(l, u):
                wait(act, l.lin_summed, 2 * u)
                for k in range(KD):
                    copied(featT[:, k, :], k, l.featT_summed, 2 * u + k + 1, l.featT_copied)

            def deviation(l, u):
                act.wait_ge(l.ln_stats, u + 1)
                root(0, l.ln_sd)

            def normed_copied(l, u, q):
                for k in range(KD):
                    act.wait_ge(l.xnT_summed, 2 * u + k + 1)
                    f(xnT[q][:, 0, k, :], psM[k][:, 0:T], ACT.Copy, scale=XS).then_inc(l.xnT_copied, 1)

            def exponent(l, u):
                act.wait_ge(l.logits_taken, u + 1)
                f(ex[:, :, :], lgd[:, :, :], ACT.Exp).then_inc(l.exp_done, 1)

            def weights_copied(l, u, q):
                act.wait_ge(l.combT_summed, u + 1)
                f(cT[q][:, :].rearrange("k (s p) -> k s p", s=SUB), cps[0:CP * NX, 0:SUB, 0:PT], ACT.Copy)\
                    .then_inc(l.comb_ready, 1)

            def active(l, t, n):
                act.wait_ge(l.hid_summed, l.M * t + n + 1)
                wait(act, l.hid_lo, l.M * t + n - 1)
                f(hid[n % 2][:, :], psH[n % 2][:, 0:T], (ACT.Relu, ACT.Gelu)[l.i], scale=l.un_up,
                  bias=l.b1[:, n // l.HC, n % l.HC:n % l.HC + 1]).then_inc(l.hid_active, 1)

            def hidden_high(l, t, n):
                act.wait_ge(l.hid_scaled, l.M * t + n + 1)
                wait(act, l.hid_used, l.M * t + n - 1)
                f(hsc[n % 2][:, 0, :], hid[n % 2][:, :], ACT.Copy).then_inc(l.hid_hi, 1)

            def matrix_high(l, k):
                wait(act, l.w_lo, k)
                f(l.part(k, 0), l.raw(k), ACT.Copy, scale=l.s_w1 if k < NX else l.s_w2)\
                    .then_inc(l.w_hi, 1)

            def sum_copied(l, tt):
                act.wait_ge(l.hid_used, l.M * tt + l.M)
                wait(act, l.ytok_summed, 2 * tt)
                f(yT[:, 0, :], psY[0][:, 0:T], ACT.Copy, scale=l.un_y)
                f(yT[:, 1, :], psY[1][:, 0:T], ACT.Copy, scale=l.un_y).then_inc(l.y_copied, 1)

            def result_deviation(tt):
                act.wait_ge(s_ln2m, tt + 1)
                root(1, s_ln2s)

            def result_copied(tt):
                wait(act, s_hraw, tt)
                for k in range(KD):
                    copied(x2T[:, k, :], k, s_x2Ts, 2 * tt + k + 1, s_x2T)

            def projected(tt):
                act.wait_ge(s_hraw, tt + 1)
                wait(act, s_hTw, 16 * tt)
                wait(act, s_hps, tt)
                f(hT[:, :], psM[0][:, 0:T], ACT.Relu, bias=bp[:, :]).then_inc(s_hT, 1)

            def squared(tt):
                act.wait_ge(s_hps, tt + 1)
                wait(act, s_hpw, 16 * tt)
                f(hp[:, :, :].rearrange("p s d -> p (s d)"), psM[1][0:PT, :], ACT.Square)\
                    .then_inc(s_hp, 1)

            act.wait_ge(s_wl, 16 * 13)
            for l in L:
                act.wait_ge(l.scales_ready, 1)
                for k in range(2 * NX):
                    matrix_high(l, k)
                if l.i == 0:
                    feat_copied(l, 0)
                else:
                    take_root(l, 0)
                deviation(l, 0)
                normed_copied(l, 0, 0)
                exponent(l, 0)
                weights_copied(l, 0, 0)
                active(l, 0, 0)

                def tile(t, q, first, last):
                    if not first:
                        sum_copied(l, t - 1)
                    for n in range(l.M):
                        if n + 1 < l.M:
                            active(l, t, n + 1)
                        elif not last:
                            active(l, t + 1, 0)
                        hidden_high(l, t, n)
                        if l.i == 0 and not first:
                            if n == 4:
                                result_deviation(t - 1)
                            if n == 7:
                                result_copied(t - 1)
                            if n == 10:
                                projected(t - 1)
                            if n == 12:
                                squared(t - 1)
                        if last:
                            continue
                        if n == l.at_feat + 1 and l.i == 0:
                            feat_copied(l, t + 1)
                        if n == l.at_take and l.i == 1:
                            take_root(l, t + 1)
                        if n == l.at_lin + 1:
                            deviation(l, t + 1)
                        if n == l.at_norm + (1, 0)[l.i]:
                            normed_copied(l, t + 1, 1 - q)
                        if n == l.at_gate + (1, 0)[l.i]:
                            exponent(l, t + 1)
                        if n == l.at_comb + (1, 0)[l.i]:
                            weights_copied(l, t + 1, 1 - q)

                iteration(l, tile, Chain(act, s_act), 0)
                sum_copied(l, NT - 1)
                if l.i == 0:
                    result_deviation(NT - 1)
                    result_copied(NT - 1)
                    projected(NT - 1)
                    squared(NT - 1)


def laid_out(inputs, n_nodes, n_edges):
    NT, NG = shapes(n_nodes, n_edges)
    EP = NG * GE

    def arr(name):
        return np.ascontiguousarray(inputs[name])

    def edges(x, fill):
        x = np.concatenate([x.reshape(-1), np.full(EP - n_edges, fill, x.dtype)])
        return np.ascontiguousarray(x.reshape(NG * SUB, P).T)

    def chunks(w):
        return np.ascontiguousarray(w.reshape(-1, P, w.shape[1]).transpose(1, 0, 2))

    def experts(w):
        return np.ascontiguousarray(w.reshape(NX, -1, P, w.shape[2]).transpose(2, 0, 1, 3))

    def columns(b):
        return np.ascontiguousarray(b.reshape(NX, -1, P).transpose(2, 0, 1))

    f32 = np.float32
    spread = np.zeros((3, NX, NX, P), f32)
    partmask = np.zeros((3, 3 * NX, 3), f32)
    for e in range(NX):
        spread[:, e, e, :] = 1
    for j in range(3):
        partmask[j, :, j] = 1
    stage = [T * max(0, (g - LAG) // GPT) for g in range(NG)]
    return {
        "x": np.concatenate([arr("x"), np.zeros((NT * T - n_nodes, D), f32)]),
        "src": edges(arr("src"), 0), "dst": edges(arr("dst"), n_nodes),
        "w0": edges(arr("edge_weight1"), 0), "w1": edges(arr("edge_weight"), 0),
        "gnn0_w": chunks(arr("L0_gnn_W").T), "gnn0_b": arr("L0_gnn_b").reshape(1, D),
        "wg0": chunks(arr("L0_ffn_Wg")), "bg": arr("L0_ffn_bg").reshape(1, NX),
        "bias": arr("L0_ffn_bias").reshape(1, NX),
        "w1_0": experts(arr("L0_ffn_W1")), "b1_0": columns(arr("L0_ffn_b1")),
        "w2_0": experts(arr("L0_ffn_W2")), "b2_0": arr("L0_ffn_b2"),
        "wp": chunks(arr("L1_gnn_Wp").T), "bp": arr("L1_gnn_bp").reshape(P, 1),
        "gnn1_w": np.ascontiguousarray(np.stack([arr("L1_gnn_W1").T, arr("L1_gnn_W2").T], 1)),
        "gnn1_b1": arr("L1_gnn_b1").reshape(1, D), "gnn1_b2": arr("L1_gnn_b2").reshape(1, D),
        "wg1": chunks(arr("L1_ffn_router_w").T),
        "w1_1": experts(arr("L1_ffn_w1")), "b1_1": columns(arr("L1_ffn_b1")),
        "w2_1": experts(arr("L1_ffn_w2")), "b2_1": arr("L1_ffn_b2"),
        "ident": np.eye(P, dtype=f32),
        "iota": np.tile(np.arange(T, dtype=f32), (P, 1)),
        "lower": np.tile(np.tril(np.ones((NX, NX), f32), -1).reshape(1, -1), (P, 1)),
        "spread": spread.reshape(3 * NX, NX * P),
        "partmask": partmask.reshape(9 * NX, 3),
        "floor": np.tile(np.array(stage, f32), (P, 1)),
    }


def kernel(**inputs):
    import concourse.bacc as bacc
    from concourse.bass_utils import run_bass_kernel_spmd

    n_nodes, n_edges = inputs["x"].shape[0], inputs["src"].shape[0]
    arrays = laid_out(inputs, n_nodes, n_edges)
    nc = bacc.Bacc("TRN2", target_bir_lowering=False, num_devices=1)
    aps = {k: nc.dram_tensor(k + "_in", v.shape, mybir.dt.from_np(v.dtype), kind="ExternalInput").ap()
           for k, v in arrays.items()}
    aps["out"] = nc.dram_tensor("out_dram", (n_nodes, D), F32, kind="ExternalOutput").ap()
    build_program(nc, aps, n_nodes, n_edges)
    r = run_bass_kernel_spmd(nc, [{k + "_in": v for k, v in arrays.items()}], core_ids=[0])
    return r.results[0]["out_dram"]
```

```python
import numpy as np
import concourse.bass as bass
from concourse import mybir
from contextlib import ExitStack

F32 = mybir.dt.float32
BF16 = mybir.dt.bfloat16
F16 = mybir.dt.float16
I32 = mybir.dt.int32
ALU = mybir.AluOpType
ACT = mybir.ActivationFunctionType
AX = mybir.AxisListType.X
RMAX = bass.bass_isa.ReduceOp.max

P = 128
D = 256
KD = D // P
NX = 8
SUB = 4
PT = 121
T = SUB * PT
GE = SUB * P
W = 40
GPT = 16
SMALL = 13
LAG = 2
WACC = T + 256
HC0, HC1 = 4, 2
CP = 9
EPS = 1e-5
PARTS = ((0, 0), (0, 1), (1, 0))
XS = 2.0 ** 11
TINY = 2.0 ** -40
EXP_MASK = 0x7f800000
ONE_EXP = 1 << 23


def shapes(n, e):
    tiles = -(-n // T)
    groups = GPT * tiles + LAG
    assert tiles % 2 == 1 and groups * GE >= e and tiles >= 7
    return tiles, groups


def build_program(nc, a, n_nodes, n_edges):
    NT, NG = shapes(n_nodes, n_edges)
    NPAD = NT * T
    ET = NG * SUB

    table0 = nc.dram_tensor("table0", (NPAD, D), F32, kind="Internal").ap()
    table1 = nc.dram_tensor("table1", (NPAD, P), F32, kind="Internal").ap()
    x2_d = nc.dram_tensor("x2_d", (NPAD, D), F32, kind="Internal").ap()
    hT_d = nc.dram_tensor("hT_d", (NT, P, T), F32, kind="Internal").ap()
    seed0_d = nc.dram_tensor("seed0_d", (NT, P, 3 * T), F32, kind="Internal").ap()
    seed1_d = nc.dram_tensor("seed1_d", (NT, P, T), F32, kind="Internal").ap()

    def rows(dram, t):
        return dram[bass.ds(t * T, T), :].rearrange("(p s) d -> p (s d)", s=SUB)

    ctx = ExitStack()

    def sb(name, shape, dt=F32):
        return ctx.enter_context(nc.sbuf_tensor(name, shape, dt))

    def sem(name):
        return ctx.enter_context(nc.semaphore(name))

    def rep(x, axis, n):
        x = x.unsqueeze(axis)
        return x.broadcast_to([n if k == axis else d for k, d in enumerate(x.shape)])

    def wait(eng, s, value):
        if isinstance(value, int) and value <= 0:
            return
        eng.wait_ge(s, value)

    def hold(eng):
        eng.nop(nofuse=True)

    class Chain:

        def __init__(self, eng, s):
            self.eng, self.sem, self.base, self.n = eng, s, 0, 0

        def link(self, ins):
            self.n += 1
            ins.then_inc(self.sem, 1)
            self.eng.wait_ge(self.sem, self.base + self.n)

        def loop(self, i, per):
            self.start, self.per = self.base + self.n, per
            self.base, self.n = self.start + i * per, 0

        def looped(self, count):
            assert self.n == self.per, (self.n, self.per)
            self.base, self.n = self.start + count * self.per, 0

    with ctx:
        ident = sb("ident", [P, P])
        ident_b = sb("ident_b", [P, P], BF16)
        ones_b = sb("ones_b", [P, P], BF16)
        iota = sb("iota", [P, T])
        lower = sb("lower", [P, NX * NX])
        eps_t = sb("eps_t", [P, 1])
        spread = sb("spread", [3 * NX, NX, P], BF16)
        partmask = sb("partmask", [CP * NX, 3])
        gnn0_w = sb("gnn0_w", [P, 2 * KD, D])
        gnn0_b = sb("gnn0_b", [P, D])
        wg0 = sb("wg0", [P, KD, NX])
        gb0 = sb("gb0", [P, 2, NX])
        SLOT = (KD * HC0 * P, KD * HC1 * P)
        wbuf = sb("wbuf", [P, (2 * NX + 1) * SLOT[0]])
        wbuf_h = wbuf[:, :].bitcast(F16)
        b1_0 = sb("b1_0", [P, NX, HC0])
        wp = sb("wp", [P, KD, P])
        bp = sb("bp", [P, 1])
        gnn1_w = sb("gnn1_w", [P, 2, D])
        gnn1_b = sb("gnn1_b", [P, 2, D])
        wg1 = sb("wg1", [P, KD, NX])
        wgh = [sb(f"wgh{i}", [P, 2, KD, NX], F16) for i in range(2)]
        mag = [sb(f"mag{i}", [P, 6]) for i in range(2)]
        magr = [sb(f"magr{i}", [P, 6]) for i in range(2)]
        bits = sb("bits", [P, 4], I32)
        scl = [sb(f"scl{i}", [P, 8]) for i in range(2)]
        b1_1 = sb("b1_1", [P, NX, HC1])
        b2s = [sb(f"b2s{i}", [CP * NX, D], BF16) for i in range(2)]

        src_s = sb("src_s", [P, ET], I32)
        w_s = [sb(f"w_s{i}", [P, ET]) for i in range(2)]
        dst_f = sb("dst_f", [P, NG, SUB])
        drel = sb("drel", [P, NG, SUB])
        floor_s = sb("floor_s", [P, NG])
        rel = sb("rel", [P, NG])
        base_i = sb("base_i", [P, NG + 2], I32)
        flag_f = sb("flag_f", [P, 2])
        flag_i = sb("flag_i", [1, 1], I32)
        RING = [4, 8]
        ring = sb("ring", [P, RING[0] * SUB * D])
        ringv = [ring[:, :].rearrange("p (r k d) -> p r k d", r=RING[0], k=SUB),
                 ring[:, :].rearrange("p (r k d) -> p r k d", r=RING[1], k=SUB)]
        idx = sb("idx", [P, GPT, SUB], I32)
        oh = sb("oh", [P, 4, SUB, W], BF16)
        ohw = sb("ohw", [P, 8, SUB, W])
        acc = sb("acc", [P, 3, WACC])
        aggs = sb("aggs", [P, KD, T])

        xin = sb("xin", [PT, SUB, D])
        feat = sb("feat", [PT, SUB, D])
        featT = sb("featT", [P, KD, T])
        res = [sb(f"res{i}", [PT, SUB, D]) for i in range(2)]
        xn = sb("xn", [PT, SUB, D])
        xnT = [sb(f"xnT{i}", [P, 2, KD, T], F16) for i in range(2)]
        hid = [sb(f"hid{i}", [P, T]) for i in range(4)]
        hsc = [sb(f"hsc{i}", [P, 2, T], F16) for i in range(2)]
        yT = sb("yT", [P, KD, T])
        x2 = sb("x2", [PT, SUB, D])
        x2T = featT
        hT = sb("hT", [P, T])
        hp = sb("hp", [PT, SUB, P])
        stats = [sb(f"stats{i}", [PT, SUB, 6]) for i in range(2)]
        mv = [sb(f"mv{i}", [PT, SUB, 2]) for i in range(2)]
        sd = [sb(f"sd{i}", [PT, SUB]) for i in range(2)]
        rs = [sb(f"rs{i}", [PT, SUB]) for i in range(2)]
        lg = sb("lg", [PT, SUB, NX])
        lgd = sb("lgd", [PT, SUB, NX])
        ex = sb("ex", [PT, SUB, NX])
        pr = sb("pr", [PT, SUB, NX])
        m4 = sb("m4", [PT, 4, SUB])
        gt = sb("gt", [PT, SUB, NX, NX])
        eq = sb("eq", [PT, SUB, NX, NX])
        mask = sb("mask", [PT, SUB, NX])
        comb = sb("comb", [PT, SUB, NX])
        crem = sb("crem", [PT, SUB, NX])
        c72 = sb("c72", [PT, SUB, CP * NX], BF16)
        xn2 = xn
        hTl = featT[:, 0, :]
        spread_f = x2[0:3 * NX, :, :].rearrange("p s d -> p (s d)")
        dst_s = ring[:, 0:ET].bitcast(I32)
        ext = hT[:, 0:2 * NG]
        extr = yT[:, :, :].rearrange("p k n -> p (k n)")[:, 0:2 * NG]
        chk = aggs[:, :, :].rearrange("p k n -> p (k n)")[:, 0:3 * NG].rearrange("p (a g) -> p a g", a=3)
        b2f = featT[0:CP * NX, 1, 0:D]
        b2p = [yT[:, :, :].rearrange("p k n -> p (k n)")[0:CP * NX, k * D:(k + 1) * D] for k in range(3)]
        fb_oh = sb("fb_oh", [P, T], BF16)
        fb_d = sb("fb_d", [P, 1])
        fb_off = sb("fb_off", [P, 1])
        cT = [sb(f"cT{i}", [CP * NX, T], BF16) for i in range(2)]

        psH = [ctx.enter_context(nc.psum_tensor(f"psH{i}", [P, 512], F32)) for i in range(2)]
        psY = [ctx.enter_context(nc.psum_tensor(f"psY{i}", [P, 512], F32)) for i in range(2)]
        psC = ctx.enter_context(nc.psum_tensor("psC", [P, 512], F32))
        psE = ctx.enter_context(nc.psum_tensor("psE", [P, 512], F32))
        psM = [ctx.enter_context(nc.psum_tensor(f"psM{i}", [P, 512], F32)) for i in range(2)]

        cps = psM[1][:, :].bitcast(BF16).rearrange("p (s n) -> p s n", s=2 * SUB)

        s_const = sem("const_loaded")
        s_edge = sem("edges_loaded")
        s_wl = sem("weights_loaded")
        s_ext = sem("extremes_ready")
        s_extr = sem("extremes_reduced")
        s_flag = sem("flag_ready")
        s_ready = sem("constants_made")
        s_dve = sem("dve_chain")
        s_act = sem("act_chain")
        s_idx = [sem(f"idx_staged{i}") for i in range(2)]
        s_t0x = [sem(f"t0_x_loaded{i}") for i in range(2)]
        s_t0m = sem("t0_stats")
        s_t0s = sem("t0_sd")
        s_t0n = sem("t0_normed")
        s_t0w = [sem(f"t0_stored{i}") for i in range(2)]

        class Layer:

            def __init__(self, i):
                def s(name):
                    return sem(f"l{i}_{name}")

                self.onehot_ready = s("onehot_ready")
                self.group_summed = s("group_summed")
                self.window_added = s("window_added")
                self.agg_ready = s("agg_ready")
                self.agg_root = s("agg_root")
                self.feat_loaded = s("feat_loaded")
                self.xin_loaded = s("xin_loaded")
                self.featT_summed = s("featT_summed")
                self.featT_copied = s("featT_copied")
                self.lin_summed = s("lin_summed")
                self.res_ready = s("res_ready")
                self.ln_stats = s("ln_stats")
                self.ln_sd = s("ln_sd")
                self.xn_ready = s("xn_ready")
                self.xnT_summed = s("xnT_summed")
                self.xnT_copied = s("xnT_copied")
                self.xnT_ready = s("xnT_ready")
                self.logits_summed = s("logits_summed")
                self.logits_taken = s("logits_taken")
                self.exp_done = s("exp_done")
                self.comb_split = s("comb_split")
                self.combT_summed = s("combT_summed")
                self.comb_ready = s("comb_ready")
                self.spread_ready = s("spread_ready")
                self.hid_summed = s("hid_summed")
                self.hid_active = s("hid_active")
                self.hid_scaled = s("hid_scaled")
                self.hid_hi = s("hid_hi")
                self.hid_lo = s("hid_lo")
                self.w1_loaded = s("w1_loaded")
                self.w2_loaded = s("w2_loaded")
                self.b2_loaded = s("b2_loaded")
                self.mags_ready = s("mags_ready")
                self.mags_reduced = s("mags_reduced")
                self.scales_ready = s("scales_ready")
                self.w_hi = s("w_hi")
                self.w_lo = s("w_lo")
                self.hid_used = s("hid_used")
                self.y_copied = s("y_copied")
                self.ytok_summed = s("ytok_summed")
                self.out_ready = s("out_ready")
                self.out_stored = s("out_stored")
                self.fb_idx = s("fb_idx")
                self.fb_gathered = s("fb_gathered")
                self.fb_onehot = s("fb_onehot")
                self.fb_summed = s("fb_summed")
                self.fb_used = s("fb_used")
                self.fb_chain = s("fb_chain")
                self.fb_tile = s("fb_tile")
                self.fb_stored = s("fb_stored")
                self.seed_loaded = s("seed_loaded")
                self.seed_wanted = s("seed_wanted")
                self.i, self.HC = i, (HC0, HC1)[i]
                self.M = NX * self.HC
                self.R = RING[i]
                self.ring = ringv[i]
                self.gathered = [s(f"gathered{r}") for r in range(self.R)]
                self.b1, self.wg, self.wgh, self.w = (b1_0, b1_1)[i], (wg0, wg1)[i], wgh[i], w_s[i]
                self.slot, self.mag, self.magr = SLOT[i], mag[i], magr[i]
                c = [scl[i][:, k:k + 1] for k in range(8)]
                self.s_w1, self.s_w2, self.s_h, self.s_wg, self.un_up, self.un_y, self.un_h, self.un_g = c
                self.scales = scl[i]
                self.table, self.seed_d = (table0, table1)[i], (seed0_d, seed1_d)[i]
                self.parts = (3, 1)[i]
                self.at_take, self.at_lin, self.at_norm, self.at_gate, self.at_comb = (
                    (13, 18, 22, 24, 29), (1, 3, 7, 9, 13))[i]
                self.at_feat = 13
                self.at_scales = (4, 3)[i]
                self.at_bias = (12, 2)[i]
                self.turn = (28, 1)[i]
                self.ahead = self.M - self.turn
                self.first_batch = (1, 2)[i]

            def raw(self, k, n=1):
                return wbuf[:, (k + 1) * self.slot:(k + 1 + n) * self.slot]

            def part(self, k, j):
                return wbuf_h[:, (2 * k + j) * self.slot:(2 * k + j + 1) * self.slot]

            def w1(self, e, j, k, c):
                o = (k * self.HC + c) * P
                return self.part(e, j)[:, o:o + P]

            def w2(self, e, j, c, d):
                o = c * D + d * P
                return self.part(NX + e, j)[:, o:o + P]

        L = [Layer(0), Layer(1)]
        s_ln2m, s_ln2s, s_x2n = sem("ln2_stats"), sem("ln2_sd"), sem("x2n_ready")
        s_x2Ts, s_x2T = sem("x2T_summed"), sem("x2T_copied")
        s_hraw, s_hT = sem("hT_summed"), sem("hT_ready")
        s_hps, s_hp = sem("hp_summed"), sem("hp_ready")
        s_hTw, s_hpw = sem("hT_stored"), sem("hp_stored")

        block = ctx.enter_context(nc.Block())

        LASTG = LAG + GPT

        def first_batches(l):
            return [list(range(g, g + l.first_batch)) for g in range(0, LASTG, l.first_batch)]

        def batch(l, t, n, last, more):
            if n == l.M:
                return t + 2, [LAG + l.ahead] if more else []
            if n >= l.turn:
                return t + 2, [LAG + n - l.turn] if more else []
            if n < 0:
                return t + 1, [LAG + l.ahead - 1] if not last else []
            return t + 1, [LAG + l.ahead + n] if n < GPT - l.ahead and not last else []

        def begun(l):
            n = l.ahead
            return [list(range(LAG + n * k // 4, LAG + n * (k + 1) // 4)) for k in range(4)]

        def split_at(l, n):
            start = l.at_scales + 1
            per = 2 * NX / (len(first_batches(l)) - start)
            return range(max(0, int(per * (n - start))), max(0, int(per * (n - start + 1))))

        def iteration(l, emit, chain, per):
            emit(0, 0, True, False, True)
            emit(1, 1, False, False, True)
            with chain.eng.Fori(0, (NT - 5) // 2) as i:
                chain.loop(i, per)
                emit(2 * i + 2, 0, False, False, True)
                emit(2 * i + 3, 1, False, False, True)
            chain.looped((NT - 5) // 2)
            emit(NT - 3, 0, False, False, True)
            emit(NT - 2, 1, False, False, False)
            emit(NT - 1, 0, False, True, False)

        @block.sync
        def _(sp):
            for dst, s in ((ident, "ident"), (iota, "iota"), (lower, "lower"),
                           (partmask, "partmask"), (x2, "spread"), (floor_s, "floor")):
                dst = spread_f if s == "spread" else dst[:, :]
                sp.dma_start(dst, a[s]).then_inc(s_const, 16)
            for dst, s in ((src_s, "src"), (None, "dst"), (w_s[0], "w0"), (w_s[1], "w1")):
                sp.dma_start(dst_s if s == "dst" else dst[:, :], a[s]).then_inc(s_edge, 16)

            def t0_load(t, q):
                if not isinstance(t, int) or t >= 2:
                    sp.wait_ge(s_t0n, t - 1)
                sp.dma_start((xin, feat)[q][:, :, :].rearrange("p s d -> p (s d)"),
                             rows(a["x"], t)).then_inc(s_t0x[q], 16)

            def t0_store(t, q):
                sp.wait_ge(s_t0n, t + 1)
                sp.dma_start(rows(table0, t),
                             res[q][:, :, :].rearrange("p s d -> p (s d)")).then_inc(s_t0w[q], 16)

            t0_load(0, 0)
            t0_load(1, 1)
            sp.dma_start(L[0].raw(0, NX), a["w1_0"]).then_inc(L[0].w1_loaded, 16)
            sp.dma_start(L[0].raw(NX, NX // 2), a["w2_0"][:, 0:NX // 2])\
              .then_inc(L[0].w2_loaded, 16)
            for dst, s in (
                (gnn0_w, "gnn0_w"), (wg0, "wg0"), (b1_0, "b1_0"),
                (wp, "wp"), (gnn1_w, "gnn1_w"), (wg1, "wg1"),
                (b1_1, "b1_1"),
            ):
                sp.dma_start(dst[:, :, :], a[s]).then_inc(s_wl, 16)
            sp.dma_start(bp[:, :], a["bp"]).then_inc(s_wl, 16)
            sp.dma_start(gnn0_b[:, :], a["gnn0_b"].broadcast_to((P, a["gnn0_b"].shape[1]))).then_inc(s_wl, 16)
            sp.dma_start(gnn1_b[:, 0, :], a["gnn1_b1"].broadcast_to((P, a["gnn1_b1"].shape[1]))).then_inc(s_wl, 16)
            sp.dma_start(gnn1_b[:, 1, :], a["gnn1_b2"].broadcast_to((P, a["gnn1_b2"].shape[1]))).then_inc(s_wl, 16)
            sp.dma_start(gb0[:, 0, :], a["bg"].broadcast_to((P, a["bg"].shape[1]))).then_inc(s_wl, 16)
            sp.dma_start(gb0[:, 1, :], a["bias"].broadcast_to((P, a["bias"].shape[1]))).then_inc(s_wl, 16)

            def b2_load(l):
                for k in range(CP):
                    sp.dma_start(b2f[k * NX:(k + 1) * NX, :], a[("b2_0", "b2_1")[l.i]])\
                      .then_inc(l.b2_loaded, 16)

            b2_load(L[0])
            with sp.Fori(0, (NT - 3) // 2) as i:
                t0_store(2 * i, 0)
                t0_load(2 * i + 2, 0)
                t0_store(2 * i + 1, 1)
                t0_load(2 * i + 3, 1)
            t0_store(NT - 3, 0)
            t0_load(NT - 1, 0)
            sp.dma_start(L[0].raw(NX + NX // 2, NX // 2), a["w2_0"][:, NX // 2:NX])\
              .then_inc(L[0].w2_loaded, 16)
            t0_store(NT - 2, 1)
            t0_store(NT - 1, 0)

            sp.wait_ge(s_flag, 1)
            flag = sp.value_load(flag_i[0:1, 0:1], min_val=0, max_val=1)

            def general_store(l):
                with sp.If(flag):
                    with sp.Fori(0, NT) as u:
                        sp.wait_ge(l.fb_tile, u + 1)
                        sp.dma_start(l.seed_d[bass.ds(u, 1), :, :].rearrange(
                            "o p (k n) -> (o p) k n", k=l.parts),
                            acc[:, 0:l.parts, 0:T]).then_inc(l.fb_stored, 16)

            def seed_load(l, u):
                with sp.If(flag):
                    sp.wait_ge(l.seed_wanted, u + 1)
                    sp.dma_start(acc[:, 0:l.parts, 0:T], l.seed_d[bass.ds(u, 1), :, :].rearrange(
                        "o p (k n) -> (o p) k n", k=l.parts)).then_inc(l.seed_loaded, 16)

            def inputs(l, u):
                if l.i == 0:
                    wait(sp, l.featT_summed, 2 * u)
                    sp.dma_start(feat[:, :, :].rearrange("p s d -> p (s d)"), rows(table0, u))\
                      .then_inc(l.feat_loaded, 16)
                    src = a["x"]
                else:
                    wait(sp, l.lin_summed, 2 * u)
                    sp.dma_start(hTl, hT_d[bass.ds(u, 1), :, :].rearrange(
                        "o p n -> (o p) n")).then_inc(l.feat_loaded, 16)
                    src = x2_d
                wait(sp, l.res_ready, u)
                sp.dma_start(xin[:, :, :].rearrange("p s d -> p (s d)"), rows(src, u))\
                  .then_inc(l.xin_loaded, 16)

            def results0(tt):
                sp.wait_ge(L[0].out_ready, 2 * tt + 2)
                sp.dma_start(rows(x2_d, tt), x2[:, :, :].rearrange("p s d -> p (s d)"))\
                  .then_inc(L[0].out_stored, 16)
                sp.wait_ge(s_hT, tt + 1)
                sp.dma_start(hT_d[bass.ds(tt, 1), :, :].rearrange("o p n -> (o p) n"), hT[:, :])\
                  .then_inc(s_hTw, 16)
                sp.wait_ge(s_hp, tt + 1)
                sp.dma_start(rows(table1, tt), hp[:, :, :].rearrange("p s d -> p (s d)"))\
                  .then_inc(s_hpw, 16)

            def results1(tt, last=False):
                sp.wait_ge(L[1].out_ready, 2 * tt + 2)
                if not last:
                    sp.dma_start(rows(a["out"], tt), x2[:, :, :].rearrange("p s d -> p (s d)"))\
                      .then_inc(L[1].out_stored, 16)
                    return
                left = n_nodes - tt * T
                full, rest = left // SUB, left % SUB
                sp.dma_start(a["out"][tt * T:tt * T + full * SUB, :].rearrange(
                    "(p s) d -> p (s d)", s=SUB),
                    x2[0:full, :, :].rearrange("p s d -> p (s d)")).then_inc(L[1].out_stored, 16)
                if rest:
                    sp.dma_start(a["out"][tt * T + full * SUB:n_nodes, :].rearrange(
                        "(o s) d -> o (s d)", o=1),
                        x2[full:full + 1, 0:rest, :].rearrange("p s d -> p (s d)"))\
                      .then_inc(L[1].out_stored, 16)

            for q in range(2):
                sp.wait_ge(s_t0w[q], 16 * ((NT + 1 - q) // 2))
            general_store(L[0])
            ends = Chain(sp, s_act)
            for l, results in ((L[0], results0), (L[1], results1)):
                if l.i == 1:
                    b2_load(l)
                    general_store(l)
                    sp.wait_ge(L[0].out_stored, 16 * NT)
                    sp.wait_ge(s_hTw, 16 * NT)
                inputs(l, 0)
                seed_load(l, 0)

                def tile(t, q, first, last, more):
                    if not last:
                        inputs(l, t + 1)
                    if l.i == 1 and not last:
                        seed_load(l, t + 1)
                    if not first:
                        results(t - 1)
                    if l.i == 0 and not last:
                        seed_load(l, t + 1)

                iteration(l, tile, ends, 0)
                if l.i == 0:
                    sp.wait_ge(l.hid_used, l.M * NT)
                    sp.dma_start(L[1].raw(0, NX), a["w1_1"]).then_inc(L[1].w1_loaded, 16)
                    sp.dma_start(L[1].raw(NX, NX), a["w2_1"]).then_inc(L[1].w2_loaded, 16)
                    results(NT - 1)
                else:
                    results(NT - 1, last=True)
            stores = NT + (1 if (n_nodes - (NT - 1) * T) % SUB else 0)
            sp.wait_ge(L[1].out_stored, 16 * stores)
            sp.wait_ge(s_hpw, 16 * NT)

        @block.gpsimd
        def _(pool):
            pool.wait_ge(s_ext, 1)
            pool.partition_all_reduce(extr, ext, P, RMAX).then_inc(s_extr, 1)
            pool.wait_ge(s_edge, 64)
            pool.wait_ge(s_flag, 1)
            flag = pool.value_load(flag_i[0:1, 0:1], min_val=0, max_val=1)

            def general_gather(l):
                with pool.If(flag):
                    with pool.Fori(0, NT) as u:
                        with pool.Fori(0, ET) as j:
                            n = u * ET + j
                            pool.wait_ge(l.fb_used, n + 1)
                            pool.tensor_copy(idx[:, 0, 0:1], src_s[:, bass.ds(j, 1)])\
                                .then_inc(l.fb_idx, 1)
                            pool.wait_ge(l.fb_idx, n + 1)
                            hold(pool)
                            pool.indirect_dma_start(
                                out=l.ring[:, 0, 0, :], out_offset=None, in_=l.table,
                                in_offset=bass.IndirectOffsetOnAxis(ap=idx[:, 0, 0:1], axis=0))\
                                .then_inc(l.fb_gathered, 16)
                    pool.wait_ge(l.fb_used, NT * ET + 1)

            def gather_group(l, it, k16, staged=4):
                g, per = GPT * it + k16, GPT // 4
                wait(pool, l.group_summed, g - l.R + 1)
                if k16 % 4 == 0:
                    pool.tensor_copy(idx[:, k16:k16 + staged, :].rearrange("p g k -> p (g k)"),
                                     src_s[:, bass.ds(g * SUB, staged * SUB)]).then_inc(s_idx[l.i], 1)
                    pool.wait_ge(s_idx[l.i], per * it + k16 // 4 + 1)
                hold(pool)
                for k in range(SUB):
                    pool.indirect_dma_start(
                        out=l.ring[:, k16 % l.R, k, :], out_offset=None, in_=l.table,
                        in_offset=bass.IndirectOffsetOnAxis(ap=idx[:, k16, k:k + 1], axis=0))\
                        .then_inc(l.gathered[k16 % l.R], 16)

            for l in L:
                if l.i == 0:
                    for q in range(2):
                        pool.wait_ge(s_t0w[q], 16 * ((NT + 1 - q) // 2))
                else:
                    pool.wait_ge(L[0].group_summed, NG)
                    pool.wait_ge(s_hpw, 16 * NT)
                general_gather(l)
                for k in range(GPT):
                    if k == 5:
                        pool.wait_ge(l.mags_ready, 1)
                        pool.partition_all_reduce(l.magr[:, :], l.mag[:, :], P, RMAX)\
                            .then_inc(l.mags_reduced, 1)
                    gather_group(l, 0, k)
                with pool.Fori(1, NT) as it:
                    for k in range(GPT):
                        gather_group(l, it, k)
                for k in range(LAG):
                    gather_group(l, NT, k, LAG)

        @block.tensor
        def _(pe):
            pe.wait_ge(s_ready, 1)
            pe.wait_ge(s_wl, 16 * SMALL)
            flag = pe.value_load(flag_i[0:1, 0:1], min_val=0, max_val=1)
            mm = pe.matmul

            def general_sums(l):
                with pe.If(flag):
                    with pe.Fori(0, NT) as u:
                        with pe.Fori(0, ET) as j:
                            n = u * ET + j
                            pe.wait_ge(l.fb_onehot, n + 1)
                            pe.wait_ge(l.fb_gathered, 16 * n + 16)
                            if l.i == 0:
                                mm(psH[0][:, 0:T], l.ring[:, 0, 0, 0:P], hid[0][:, :], start=True, stop=True)
                                mm(psH[1][:, 0:T], l.ring[:, 0, 0, P:D], hid[0][:, :], start=True, stop=True)
                                mm(psC[:, 0:T], ones_b[:, :], fb_oh[:, :], start=True, stop=True)\
                                    .then_inc(l.fb_summed, 1)
                            else:
                                mm(psC[:, 0:T], l.ring[:, 0, 0, :], hid[0][:, :], start=True, stop=True)\
                                    .then_inc(l.fb_summed, 1)

            def sum_groups(l, u, js):
                if not js:
                    return
                pe.wait_ge(l.onehot_ready, GPT * u + js[-1] + 1)
                wait(pe, l.window_added, GPT * u + js[0])
                for i, j in enumerate(js):
                    r, q = j % l.R, j % 8
                    pe.wait_ge(l.gathered[r], 16 * SUB * ((GPT // l.R) * u + j // l.R + 1))
                    o = i * l.parts * W
                    for h in range(KD if l.i == 0 else 1):
                        for k in range(SUB):
                            last = mm(psE[:, o + h * W:o + (h + 1) * W], l.ring[:, r, k, h * P:(h + 1) * P],
                                      ohw[:, q, k, :], start=(k == 0), stop=(k == SUB - 1))
                    if l.i == 0:
                        for k in range(SUB):
                            last = mm(psE[:, o + 2 * W:o + 3 * W], ones_b[:, :], oh[:, q % 4, k, :],
                                      start=(k == 0), stop=(k == SUB - 1))
                    last.then_inc(l.group_summed, 1)

            def up(l, t, q, n):
                e, c = n // l.HC, n % l.HC
                wait(pe, l.hid_active, l.M * t + n - 1)
                for k in range(KD):
                    for m, (i, j) in enumerate(PARTS):
                        last = mm(psH[n % 2][:, 0:T], l.w1(e, i, k, c), xnT[q][:, j, k, :],
                                  start=(k == 0 and m == 0), stop=(k == KD - 1 and m == 2))
                last.then_inc(l.hid_summed, 1)

            def spread_weights(l, t, q, e):
                wait(pe, l.hid_scaled, l.M * t + l.HC * e)
                mm(psC[:, 0:T], spread[:, e, :], cT[q][0:3 * NX, :], start=True, stop=True)\
                    .then_inc(l.spread_ready, 1)

            def down(l, t, q, n):
                e, c = n // l.HC, n % l.HC
                if n == 0:
                    wait(pe, l.y_copied, t)
                    for d in range(KD):
                        mm(psY[d][:, 0:T], b2s[l.i][:, d * P:(d + 1) * P], cT[q][:, :],
                           start=True, stop=False)
                pe.wait_ge(l.hid_lo, l.M * t + n + 1)
                for d in range(KD):
                    for m, (i, j) in enumerate(PARTS):
                        last = mm(psY[d][:, 0:T], l.w2(e, i, c, d), hsc[n % 2][:, j, :],
                                  start=False, stop=(n == l.M - 1 and m == 2))
                last.then_inc(l.hid_used, 1)

            def back_to_tokens(l, tt):
                pe.wait_ge(l.y_copied, tt + 1)
                for b in range(2):
                    for s in (2 * b, 2 * b + 1):
                        for k in range(KD):
                            last = pe.transpose(psM[b][0:PT, (s % 2) * D + k * P:(s % 2) * D + (k + 1) * P],
                                                yT[:, k, s * PT:(s + 1) * PT], ident[:, :])
                    last.then_inc(l.ytok_summed, 1)

            def to_features(src, b, k, then):
                for s in range(SUB):
                    last = pe.transpose(psM[b][:, s * PT:(s + 1) * PT], src[:, s, k * P:(k + 1) * P],
                                        ident[0:PT, 0:PT])
                last.then_inc(then, 1)

            def project(tt):
                pe.wait_ge(s_x2T, 2 * tt + 2)
                for k in range(KD):
                    last = mm(psM[0][:, 0:T], wp[:, k, :], x2T[:, k, :], start=(k == 0), stop=(k == KD - 1))
                last.then_inc(s_hraw, 1)

            def project_tokens(tt):
                pe.wait_ge(s_hT, tt + 1)
                for s in range(SUB):
                    last = pe.transpose(psM[1][0:PT, s * P:(s + 1) * P], hT[:, s * PT:(s + 1) * PT],
                                        ident[:, :])
                last.then_inc(s_hps, 1)

            def feat_transposed(l, u):
                pe.wait_ge(l.feat_loaded, 16 * u + 16)
                wait(pe, s_hT, u - 1)
                wait(pe, l.logits_taken, u)
                to_features(feat, 0, 0, l.featT_summed)
                wait(pe, s_hp, u - 1)
                wait(pe, l.comb_ready, u)
                to_features(feat, 1, 1, l.featT_summed)

            def linear(l, u):
                if l.i == 0:
                    pe.wait_ge(l.featT_copied, 2 * u + 2)
                    pe.wait_ge(l.agg_ready, u + 1)
                    parts = [(aggs[:, k, :], gnn0_w[:, k, :]) for k in range(KD)]
                    parts += [(featT[:, k, :], gnn0_w[:, KD + k, :]) for k in range(KD)]
                else:
                    wait(pe, l.out_ready, 2 * u - 2)
                    wait(pe, l.logits_taken, u)
                    wait(pe, l.comb_ready, u)
                    pe.wait_ge(l.feat_loaded, 16 * u + 16)
                    pe.wait_ge(l.agg_root, u + 1)
                    parts = [(hTl, gnn1_w[:, 0, :]), (aggs[:, 1, :], gnn1_w[:, 1, :])]
                for b in range(2):
                    if b:
                        yield
                    for s in (2 * b, 2 * b + 1):
                        for m, (x, w) in enumerate(parts):
                            last = mm(psM[b][0:PT, (s % 2) * D:(s % 2 + 1) * D],
                                      x[:, s * PT:(s + 1) * PT], w, start=(m == 0), stop=(m == len(parts) - 1))
                    last.then_inc(l.lin_summed, 1)

            def normed_transposed(l, u):
                pe.wait_ge(l.xn_ready, u + 1)
                for k in range(KD):
                    to_features(xn, k, k, l.xnT_summed)

            def logits(l, u, q):
                pe.wait_ge(l.xnT_ready, 2 * u + 2)
                for s in range(SUB):
                    for k in range(KD):
                        for m, (i, j) in enumerate(PARTS):
                            last = mm(psM[0][0:PT, s * NX:(s + 1) * NX],
                                      xnT[q][:, j, k, s * PT:(s + 1) * PT], l.wgh[:, i, k, :],
                                      start=(k == 0 and m == 0), stop=(k == KD - 1 and m == 2))
                last.then_inc(l.logits_summed, 1)

            def weights_transposed(l, u):
                pe.wait_ge(l.comb_split, u + 1)
                for s in range(SUB):
                    last = pe.transpose(cps[0:CP * NX, s, 0:PT], c72[:, s, :], ident_b[0:PT, 0:PT])
                last.then_inc(l.combT_summed, 1)

            for l in L:
                general_sums(l)
                for js in first_batches(l):
                    sum_groups(l, 0, js)
                pe.wait_ge(l.scales_ready, 1)
                if l.i == 0:
                    feat_transposed(l, 0)
                for _ in linear(l, 0):
                    pass
                sum_groups(l, 1, begun(l)[0])
                normed_transposed(l, 0)
                sum_groups(l, 1, begun(l)[1])
                logits(l, 0, 0)
                sum_groups(l, 1, begun(l)[2])
                weights_transposed(l, 0)
                sum_groups(l, 1, begun(l)[3])
                pe.wait_ge(l.w_lo, 2 * NX)
                pe.wait_ge(l.comb_ready, 1)
                up(l, 0, 0, 0)
                spread_weights(l, 0, 0, 0)
                up(l, 0, 0, 1)

                def tile(t, q, first, last, more):
                    for n in range(l.M):
                        if n + 2 < l.M:
                            up(l, t, q, n + 2)
                        elif not last:
                            up(l, t + 1, 1 - q, n + 2 - l.M)
                        if n + 2 < l.M and (n + 2) % l.HC == 0:
                            spread_weights(l, t, q, (n + 2) // l.HC)
                        down(l, t, q, n)
                        if n + 2 == l.M and not last:
                            pe.wait_ge(l.comb_ready, t + 2)
                            spread_weights(l, t + 1, 1 - q, 0)
                        if n == 1 and not first:
                            back_to_tokens(l, t - 1)
                        if l.i == 0 and not first:
                            if n == 6:
                                pe.wait_ge(s_x2n, t)
                                to_features(xn2, 0, 0, s_x2Ts)
                                to_features(xn2, 1, 1, s_x2Ts)
                            if n == 9:
                                project(t - 1)
                            if n == 11:
                                project_tokens(t - 1)
                        sum_groups(l, *batch(l, t, n, last, more))
                        if last:
                            continue
                        if n == l.at_feat and l.i == 0:
                            feat_transposed(l, t + 1)
                        if n == l.at_lin:
                            products = linear(l, t + 1)
                            next(products)
                        if n == l.at_lin + 1:
                            next(products, None)
                        if n == l.at_norm:
                            normed_transposed(l, t + 1)
                        if n == l.at_gate:
                            logits(l, t + 1, 1 - q)
                        if n == l.at_comb:
                            weights_transposed(l, t + 1)

                iteration(l, tile, Chain(pe, s_act), 0)
                pe.wait_ge(s_hp, NT - 1) if l.i == 0 else pe.wait_ge(l.out_ready, 2 * NT - 2)
                back_to_tokens(l, NT - 1)
                if l.i == 0:
                    pe.wait_ge(s_x2n, NT)
                    to_features(xn2, 0, 0, s_x2Ts)
                    to_features(xn2, 1, 1, s_x2Ts)
                    project(NT - 1)
                    project_tokens(NT - 1)

        @block.vector
        def _(dve):
            c = Chain(dve, s_dve)
            link = c.link
            tt_, ts_ = dve.tensor_tensor, dve.tensor_scalar

            dve.wait_ge(s_const, 16 * 6)
            dve.memset(ones_b[:, :], 1.0)
            dve.memset(eps_t[:, :], EPS)
            dve.memset(acc[:, :, :], 0.0)
            dve.memset(base_i[:, :], 0)
            dve.tensor_copy(ident_b[:, :], ident[:, :])
            link(dve.tensor_copy(spread[:, :, :].rearrange("k e p -> k (e p)"), spread_f))

            dve.wait_ge(s_edge, 64)
            link(dve.tensor_copy(dst_f[:, :, :].rearrange("p g k -> p (g k)"), dst_s))
            link(ts_(drel[:, :, :], dst_f[:, :, :], -1.0, None, ALU.mult))
            dve.reduce_max(ext[:, 0:NG], dst_f[:, :, :], AX)
            dve.reduce_max(ext[:, NG:2 * NG], drel[:, :, :], AX).then_inc(s_ext, 1)
            dve.wait_ge(s_extr, 1)
            hi, neg = extr[:, 0:NG], extr[:, NG:2 * NG]
            link(tt_(rel[:, :], neg, floor_s[:, :], ALU.add))
            link(ts_(rel[:, :], rel[:, :], -1.0, None, ALU.mult))
            link(tt_(chk[:, 2, :], hi, neg, ALU.add))
            ts_(chk[:, 0, :], rel[:, :], 0.0, None, ALU.is_lt)
            ts_(chk[:, 1, :], rel[:, :], float(WACC - W), None, ALU.is_gt)
            link(ts_(chk[:, 2, :], chk[:, 2, :], float(W - 1), None, ALU.is_gt))
            link(dve.reduce_max(flag_f[:, 0:1], chk.rearrange("p a g -> p (a g)"), AX))
            link(ts_(flag_f[:, 1:2], flag_f[:, 0:1], -1.0, 1.0, ALU.mult, ALU.add))
            link(ts_(rel[:, :], rel[:, :], 0.0, float(WACC - W), ALU.max, ALU.min))
            dve.tensor_copy(base_i[:, 2:NG + 2], rel[:, :])
            link(tt_(drel[:, :, :], dst_f[:, :, :], rep(neg, 2, SUB), ALU.add))
            link(ts_(drel[:, :, :], drel[:, :, :], flag_f[:, 1:2], flag_f[:, 0:1], ALU.mult, ALU.subtract))
            link(dve.tensor_copy(flag_i[:, :], flag_f[0:1, 0:1]))
            dve.sem_inc(s_flag, 1)

            def ln_moments(x, i, then):
                for s in range(SUB):
                    last = dve.bn_stats(stats[i][:, s, :], x[:, s, :])
                link(last)
                moments_joined(i, then)

            def moments_joined(i, then):
                hold(dve)
                for s in range(SUB):
                    last = dve.bn_aggr(mv[i][:, s, :], stats[i][:, s, :])
                last.then_inc(then, 1)

            def ln_apply(out, x, i, then):
                link(dve.reciprocal(rs[i][:, :], sd[i][:, :]))
                for s in range(SUB):
                    last = ts_(out[:, s, :], x[:, s, :], mv[i][:, s, 0:1], rs[i][:, s:s + 1],
                               ALU.subtract, ALU.mult)
                last.then_inc(then, 1)

            def table_tile(t, q, k):
                dve.wait_ge(s_t0x[q], 16 * k + 16)
                x = (xin, feat)[q]
                if not isinstance(t, int) or t >= 2:
                    dve.wait_ge(s_t0w[q], 16 * k)
                ln_moments(x, 0, s_t0m)
                dve.wait_ge(s_t0s, t + 1)
                ln_apply(res[q], x, 0, s_t0n)
                dve.wait_ge(s_t0n, t + 1)
                hold(dve)

            table_tile(0, 0, 0)
            table_tile(1, 1, 0)
            with dve.Fori(1, (NT - 1) // 2) as i:
                c.loop(i - 1, 4)
                table_tile(2 * i, 0, i)
                table_tile(2 * i + 1, 1, i)
            c.looped((NT - 1) // 2 - 1)
            table_tile(NT - 1, 0, (NT - 1) // 2)

            dve.sem_inc(s_ready, 1)
            dve.wait_ge(s_wl, 16 * SMALL)
            link(tt_(gnn1_b[:, 0, :], gnn1_b[:, 0, :], gnn1_b[:, 1, :], ALU.add))

            def magnitudes(l, k):

                def largest(k, x):
                    return dve.tensor_reduce(l.mag[:, k:k + 1], x, AX, ALU.max,
                                             apply_absolute_value=True)

                if k == 0:
                    dve.wait_ge(l.w1_loaded, 16)
                if k == 2:
                    dve.wait_ge(l.w2_loaded, (32, 16)[l.i])
                largest((0, 4, 1, 5)[k], l.raw(k * NX // 2, NX // 2))
                if k == 3:
                    largest(2, l.b1[:, :, :].rearrange("p e c -> p (e c)"))
                    largest(3, l.wg[:, :, :].rearrange("p k e -> p (k e)")).then_inc(l.mags_ready, 1)

            def scales(l):
                dve.wait_ge(l.mags_reduced, 1)
                link(tt_(l.magr[:, 0:2], l.magr[:, 0:2], l.magr[:, 4:6], ALU.max))
                m, up, un = l.magr[:, 0:4], l.scales[:, 0:4], l.scales[:, 4:8]
                link(dve.scalar_tensor_tensor(m[:, 2:3], m[:, 0:1], float(D), m[:, 2:3],
                                              ALU.mult, ALU.add))
                link(ts_(m, m, TINY, None, ALU.max))
                link(ts_(bits[:, :], m.bitcast(I32), EXP_MASK, None, ALU.bitwise_and))
                link(ts_(bits[:, :], bits[:, :], -1.0, float(268 * ONE_EXP), ALU.mult, ALU.add))
                link(dve.tensor_copy(up.bitcast(I32), bits[:, :]))
                link(ts_(bits[:, :], bits[:, :], -1.0, float(254 * ONE_EXP), ALU.mult, ALU.add))
                link(dve.tensor_copy(un.bitcast(I32), bits[:, :]))
                ts_(l.un_up, l.un_up, 1.0 / XS, None, ALU.mult)
                ts_(l.un_g, l.un_g, 1.0 / XS, None, ALU.mult)
                link(tt_(l.un_y, l.un_y, l.un_h, ALU.mult))
                link(ts_(l.wgh[:, 0, :, :], l.wg[:, :, :], l.s_wg, None, ALU.mult))
                dve.scalar_tensor_tensor(l.wgh[:, 1, :, :], l.wg[:, :, :], l.s_wg, l.wgh[:, 0, :, :],
                                         ALU.mult, ALU.subtract)
                dve.wait_ge(l.b2_loaded, 16 * CP)
                bb, n = b2s[l.i][:, :], CP * NX
                link(ts_(b2f, b2f, l.s_w2[0:n, :], None, ALU.mult))
                for k in range(3):
                    link(dve.tensor_copy(bb, b2f))
                    link(dve.tensor_copy(b2p[k], bb))
                    link(tt_(b2f, b2f, b2p[k], ALU.subtract))
                link(ts_(b2p[0], b2p[0], partmask[:, 0:1], None, ALU.mult))
                link(dve.scalar_tensor_tensor(b2p[0], b2p[1], partmask[:, 1:2], b2p[0], ALU.mult, ALU.add))
                link(dve.scalar_tensor_tensor(bb, b2p[2], partmask[:, 2:3], b2p[0], ALU.mult, ALU.add))
                dve.sem_inc(l.scales_ready, 1)

            def matrix_low(l, k):
                dve.wait_ge(l.w_hi, k + 1)
                dve.scalar_tensor_tensor(l.part(k, 1), l.raw(k), l.s_w1 if k < NX else l.s_w2,
                                         l.part(k, 0), ALU.mult, ALU.subtract).then_inc(l.w_lo, 1)

            flag = dve.value_load(flag_i[0:1, 0:1], min_val=0, max_val=1)

            def general_windows(l):
                per = ET + 2
                d2 = dst_f[:, :, :].rearrange("p g k -> p (g k)")
                with dve.If(flag):
                    dve.memset(fb_off[:, :], 0.0).then_inc(l.fb_chain, 1)
                    dve.sem_inc(l.fb_used, 1)
                    with dve.Fori(0, NT) as u:
                        dve.wait_ge(l.fb_chain, u * per + 1)
                        dve.memset(acc[:, 0:l.parts, 0:T], 0.0).then_inc(l.fb_chain, 1)
                        with dve.Fori(0, ET) as j:
                            n = u * ET + j
                            dve.wait_ge(l.fb_chain, u * per + j + 2)
                            tt_(fb_d[:, :], d2[:, bass.ds(j, 1)], fb_off[:, :], ALU.subtract)\
                                .then_inc(l.fb_chain, 1)
                            dve.wait_ge(l.fb_chain, u * per + j + 3)
                            hold(dve)
                            ts_(fb_oh[:, :], iota[:, :], fb_d[:, 0:1], None, ALU.is_equal)
                            ts_(hid[0][:, :], iota[:, :], fb_d[:, 0:1], l.w[:, bass.ds(j, 1)],
                                ALU.is_equal, ALU.mult).then_inc(l.fb_onehot, 1)
                            dve.wait_ge(l.fb_summed, n + 1)
                            for k in range(l.parts):
                                ps = (psH[0], psH[1], psC)[k] if l.i == 0 else psC
                                last = tt_(acc[:, k, 0:T], acc[:, k, 0:T], ps[:, 0:T], ALU.add)
                            last.then_inc(l.fb_used, 1)
                            dve.wait_ge(l.fb_used, n + 2)
                            hold(dve)
                        dve.wait_ge(l.fb_chain, u * per + ET + 2)
                        ts_(fb_off[:, :], fb_off[:, :], float(T), None, ALU.add).then_inc(l.fb_chain, 1)
                        dve.sem_inc(l.fb_tile, 1)
                        dve.wait_ge(l.fb_stored, 16 * u + 16)
                        hold(dve)
                    dve.memset(acc[:, :, :], 0.0).then_inc(l.fb_chain, 1)
                    dve.wait_ge(l.fb_chain, NT * per + 2)

            def onehots(l, u, j):
                g, q = GPT * u + j, j % 8
                wait(dve, l.group_summed, g - (3, 7)[l.i])
                ohw_e = ohw[:, q, :, :]
                oh_e = oh[:, q % 4, :, :] if l.i == 0 else ohw_e
                d = rep(drel[:, bass.ds(g, 1), :].rearrange("p g k -> p (g k)"), 2, W)
                w = rep(l.w[:, bass.ds(g * SUB, SUB)], 2, W)
                i = rep(iota[:, 0:W], 1, SUB)
                link(tt_(oh_e, i, d, ALU.is_equal))
                tt_(ohw_e, oh_e, w, ALU.mult).then_inc(l.onehot_ready, 1)

            regs = {}
            COLUMNS = [{0: 2, LAG: 3, LAG + 3: 1, LAG + 4: 4, LAG + 8: 4, LAG + 12: 4},
                       {0: 2, LAG: 4, LAG + 4: 4, LAG + 8: 4, LAG + 12: 2, LAG + 14: 2}]

            def window_columns(l, u, j):
                n = COLUMNS[l.i][j]
                cols = base_i[0:1, bass.ds(GPT * u + j + 2, n)]
                _, vals = nc.values_load_multi_w_load_instructions(
                    cols, engines=[mybir.EngineType.DVE], min_val=0, max_val=WACC - W,
                    skip_runtime_bounds_check_because="clamped to the range above")
                for k in range(n):
                    regs[j + k] = vals[k]

            def add_windows(l, u, js):
                if not js:
                    return
                dve.wait_ge(l.group_summed, GPT * u + js[-1] + 1)
                for i, j in enumerate(js):
                    if j in COLUMNS[l.i]:
                        window_columns(l, u, j)
                    wait(dve, l.window_added, GPT * u + j)
                    v = acc[:, 0:l.parts, bass.ds(regs[j], W)]
                    ps = psE[:, i * l.parts * W:(i + 1) * l.parts * W].rearrange("p (k n) -> p k n", k=l.parts)
                    tt_(v, v, ps, ALU.add).then_inc(l.window_added, 1)

            def take(l, u):
                dve.wait_ge(l.window_added, GPT * u + LASTG)
                hold(dve)
                with dve.If(flag):
                    dve.sem_inc(l.seed_wanted, 1)
                    dve.wait_ge(l.seed_loaded, 16 * u + 16)
                    hold(dve)
                wait(dve, l.lin_summed, 2 * u)

                def perm(x):
                    return x.rearrange("c (q s) -> c q s", s=SUB)

                def placed(x):
                    return x.rearrange("c (s q) -> c q s", s=SUB)

                if l.i == 0:
                    deg = acc[:, 2, 0:T]
                    link(ts_(deg, deg, 1.0, None, ALU.max))
                    for k in range(SUB):
                        part = deg[:, k * PT:(k + 1) * PT]
                        link(dve.reciprocal(part, part))
                        yield
                    for k in range(KD):
                        last = tt_(placed(aggs[:, k, :]), perm(acc[:, k, 0:T]), perm(deg), ALU.mult)
                    last.then_inc(l.agg_ready, 1)
                else:
                    dve.tensor_copy(placed(aggs[:, 0, :]), perm(acc[:, 0, 0:T])).then_inc(l.agg_ready, 1)
                dve.wait_ge(l.agg_ready, u + 1)
                link(dve.tensor_copy(acc[:, 0:l.parts, 0:WACC - T], acc[:, 0:l.parts, T:WACC]))
                if l.i == 0:
                    yield
                link(dve.memset(acc[:, 0:l.parts, WACC - T:WACC], 0.0))

            def flat(x):
                return x.rearrange("p s d -> p (s d)")

            def biased(l, u):
                dve.wait_ge(l.xin_loaded, 16 * u + 16)
                bias = rep((gnn0_b[0:PT, :] if l.i == 0 else gnn1_b[0:PT, 0, :]), 1, SUB)
                link(tt_(xin[:, :, :], xin[:, :, :], bias, ALU.add))

            def residual(l, u, q):
                wait(dve, l.out_ready, 2 * u - 2)
                for b in range(2):
                    dve.wait_ge(l.lin_summed, 2 * u + b + 1)
                    p = psM[b][0:PT, :].rearrange("p (s d) -> p s d", s=2)
                    v = slice(2 * b, 2 * b + 2)
                    link(tt_(res[q][:, v, :], p, xin[:, v, :], ALU.add))
                    for s in range(2 * b, 2 * b + 2):
                        last = dve.bn_stats(stats[0][:, s, :], res[q][:, s, :])
                    link(last)
                    if b == 0:
                        yield
                dve.sem_inc(l.res_ready, 1)
                moments_joined(0, l.ln_stats)

            def normed(l, u, q):
                dve.wait_ge(l.ln_sd, u + 1)
                wait(dve, l.xnT_summed, 2 * u)
                if l.i == 0:
                    wait(dve, s_x2Ts, 2 * u - 2)
                ln_apply(xn, res[q], 0, l.xn_ready)
                if l.i == 1:
                    dve.wait_ge(l.xn_ready, u + 1)
                    link(tt_(flat(res[q][:, :, :]), flat(res[q][:, :, :]), flat(xn[:, :, :]), ALU.add))

            def gate_max(l, u):
                dve.wait_ge(l.logits_summed, u + 1)
                ps = psM[0][0:PT, 0:SUB * NX].rearrange("p (s e) -> p s e", s=SUB)
                un = l.un_g[0:PT, :]
                if l.i == 0:
                    link(dve.scalar_tensor_tensor(lg[:, :, :], ps, un, rep(gb0[0:PT, 0, :], 1, SUB),
                                                  ALU.mult, ALU.add))
                    link(tt_(lg[:, :, :], lg[:, :, :], rep(gb0[0:PT, 1, :], 1, SUB), ALU.add))
                else:
                    link(ts_(lg[:, :, :], ps, un, None, ALU.mult))
                link(dve.reduce_max(m4[:, 0, :], lg[:, :, :], AX))
                tt_(lgd[:, :, :], lg[:, :, :], rep(m4[:, 0, :], 2, NX), ALU.subtract)\
                    .then_inc(l.logits_taken, 1)

            def gate_weights(l, u):
                dve.wait_ge(l.exp_done, u + 1)
                if l.i == 0:
                    key = lg
                else:
                    key = pr
                    link(dve.reduce_sum(m4[:, 1, :], ex[:, :, :], AX))
                    link(dve.reciprocal(m4[:, 2, :], m4[:, 1, :]))
                    link(tt_(pr[:, :, :], ex[:, :, :], rep(m4[:, 2, :], 2, NX), ALU.mult))
                other = rep(key[:, :, :], 2, NX)
                own = rep(key[:, :, :], 3, NX)
                tt_(gt[:, :, :, :], other, own, ALU.is_gt)
                link(tt_(eq[:, :, :, :], other, own, ALU.is_equal))
                low = rep(lower[0:PT, :], 1, SUB)
                e3 = eq[:, :, :, :].rearrange("p s e j -> p s (e j)")
                link(tt_(e3, e3, low, ALU.mult))
                yield
                link(tt_(gt[:, :, :, :], gt[:, :, :, :], eq[:, :, :, :], ALU.add))
                link(dve.reduce_sum(mask[:, :, :], gt[:, :, :, :], AX))
                link(ts_(mask[:, :, :], mask[:, :, :], 1.5, None, ALU.is_lt))
                if l.i == 0:
                    yield
                link(tt_(comb[:, :, :], mask[:, :, :], (ex if l.i == 0 else pr)[:, :, :], ALU.mult))
                link(dve.reduce_sum(m4[:, 1, :], comb[:, :, :], AX))
                if l.i == 1:
                    link(ts_(m4[:, 1, :], m4[:, 1, :], 1e-12, None, ALU.max))
                link(dve.reciprocal(m4[:, 2, :], m4[:, 1, :]))
                link(ts_(m4[:, 2, :], m4[:, 2, :], l.s_h[0:PT, :], None, ALU.mult))
                link(tt_(crem[:, :, :], comb[:, :, :], rep(m4[:, 2, :], 2, NX), ALU.mult))
                yield
                wait(dve, l.combT_summed, u)
                for k in range(3):
                    c4 = c72[:, :, :].rearrange("p s (j i e) -> p s j i e", j=3, i=3)
                    link(dve.tensor_copy(c4[:, :, :, k, :], rep(crem[:, :, :], 2, 3)))
                    if k < 2:
                        link(tt_(crem[:, :, :], crem[:, :, :], c4[:, :, 0, k, :], ALU.subtract))
                dve.sem_inc(l.comb_split, 1)

            def normed_low(l, u, q):
                for k in range(KD):
                    dve.wait_ge(l.xnT_copied, 2 * u + k + 1)
                    dve.scalar_tensor_tensor(xnT[q][:, 1, k, :], psM[k][:, 0:T], XS, xnT[q][:, 0, k, :],
                                             ALU.mult, ALU.subtract).then_inc(l.xnT_ready, 1)

            def scale(l, t, n):
                dve.wait_ge(l.hid_active, l.M * t + n + 1)
                if n % l.HC == 0:
                    dve.wait_ge(l.spread_ready, NX * t + n // l.HC + 1)
                h = hid[n % 4][:, :]
                tt_(h, h, psC[:, 0:T], ALU.mult).then_inc(l.hid_scaled, 1)

            def hidden_low(l, t, n):
                dve.wait_ge(l.hid_hi, l.M * t + n + 1)
                tt_(hsc[n % 2][:, 1, :], hid[n % 4][:, :], hsc[n % 2][:, 0, :], ALU.subtract)\
                    .then_inc(l.hid_lo, 1)

            def result(l, tt, q):
                wait(dve, l.out_stored, 16 * tt)
                for b in range(2):
                    dve.wait_ge(l.ytok_summed, 2 * tt + b + 1)
                    v = x2[:, 2 * b:2 * b + 2, :]
                    tt_(v, res[q][:, 2 * b:2 * b + 2, :],
                        psM[b][0:PT, :].rearrange("p (s d) -> p s d", s=2), ALU.add)\
                        .then_inc(l.out_ready, 1)
                if l.i == 0:
                    dve.wait_ge(l.out_ready, 2 * tt + 2)
                    ln_moments(x2, 1, s_ln2m)

            def result_normed(tt, final=False):
                dve.wait_ge(s_ln2s, tt + 1)
                dve.wait_ge(L[0].xnT_summed, 2 * NT if final else 2 * tt + 4)
                ln_apply(xn2, x2, 1, s_x2n)

            for l in L:
                general_windows(l)
                magnitudes(l, 0)
                magnitudes(l, 1)
                todo = first_batches(l)
                for n, js in enumerate(todo):
                    for j in js:
                        onehots(l, 0, j)
                    if n:
                        add_windows(l, 0, todo[n - 1])
                    if n < 2:
                        magnitudes(l, n + 2)
                    if n == l.at_scales:
                        scales(l)
                    for k in split_at(l, n):
                        matrix_low(l, k)
                add_windows(l, 0, todo[-1])
                for _ in take(l, 0):
                    pass

                def begin(k):
                    for j in begun(l)[k] if k < 4 else []:
                        onehots(l, 1, j)
                    if k:
                        add_windows(l, 1, begun(l)[k - 1])

                begin(0)
                biased(l, 0)
                for _ in residual(l, 0, 0):
                    pass
                begin(1)
                normed(l, 0, 0)
                normed_low(l, 0, 0)
                begin(2)
                gate_max(l, 0)
                begin(3)
                for _ in gate_weights(l, 0):
                    pass
                begin(4)
                for j in batch(l, -1, l.M, False, True)[1]:
                    onehots(l, 1, j)
                scale(l, 0, 0)

                def tile(t, q, first, last, more):
                    taking = adding = weighing = None
                    for n in range(l.M):
                        if n + 1 < l.M:
                            scale(l, t, n + 1)
                        elif not last:
                            scale(l, t + 1, 0)
                        hidden_low(l, t, n)
                        if n or not first:
                            add_windows(l, *batch(l, t, n - 1, last, more))
                        u, js = batch(l, t, n + 1, last, more)
                        for j in js:
                            onehots(l, u, j)
                        if n == 2 and not first:
                            result(l, t - 1, 1 - q)
                        if n == 4 and not first and l.i == 0:
                            result_normed(t - 1)
                        if last:
                            continue
                        if n == l.at_take:
                            taking = take(l, t + 1)
                        if n >= l.at_take:
                            next(taking, None)
                        if n == l.at_bias:
                            biased(l, t + 1)
                        if n == l.at_lin + 1:
                            adding = residual(l, t + 1, 1 - q)
                            next(adding)
                        if n == l.at_lin + 2:
                            next(adding, None)
                        if n == (l.at_norm - 1):
                            normed(l, t + 1, 1 - q)
                        if n == l.at_norm + 1:
                            normed_low(l, t + 1, 1 - q)
                        if n == l.at_gate + 1:
                            gate_max(l, t + 1)
                        if n == l.at_gate + 2:
                            weighing = gate_weights(l, t + 1)
                        if n >= l.at_gate + 2:
                            next(weighing, None)

                iteration(l, tile, c, (98, 92)[l.i])
                result(l, NT - 1, 0)
                if l.i == 0:
                    result_normed(NT - 1, final=True)
                    link(dve.memset(acc[:, :, :], 0.0))

        @block.scalar
        def _(act):
            f = act.activation

            def root(i, then):
                f(sd[i][:, :], mv[i][:, :, 1], ACT.Sqrt, bias=eps_t[0:PT, :]).then_inc(then, 1)

            with act.Fori(0, NT) as t:
                act.wait_ge(s_t0m, t + 1)
                root(0, s_t0s)

            def copied(dst, k, ready, value, then):
                act.wait_ge(ready, value)
                f(dst, psM[k][:, 0:T], ACT.Copy).then_inc(then, 1)

            def take_root(l, u):
                act.wait_ge(l.agg_ready, u + 1)
                f(aggs[:, 1, :], aggs[:, 0, :], ACT.Sqrt).then_inc(l.agg_root, 1)

            def feat_copied(l, u):
                wait(act, l.lin_summed, 2 * u)
                wait(act, s_hraw, u - 1)
                for k in range(KD):
                    copied(featT[:, k, :], k, l.featT_summed, 2 * u + k + 1, l.featT_copied)

            def deviation(l, u):
                act.wait_ge(l.ln_stats, u + 1)
                root(0, l.ln_sd)

            def normed_copied(l, u, q):
                for k in range(KD):
                    act.wait_ge(l.xnT_summed, 2 * u + k + 1)
                    f(xnT[q][:, 0, k, :], psM[k][:, 0:T], ACT.Copy, scale=XS).then_inc(l.xnT_copied, 1)

            def exponent(l, u):
                act.wait_ge(l.logits_taken, u + 1)
                f(ex[:, :, :], lgd[:, :, :], ACT.Exp).then_inc(l.exp_done, 1)

            def weights_copied(l, u, q):
                act.wait_ge(l.combT_summed, u + 1)
                f(cT[q][:, :].rearrange("k (s p) -> k s p", s=SUB), cps[0:CP * NX, 0:SUB, 0:PT], ACT.Copy)\
                    .then_inc(l.comb_ready, 1)

            def active(l, t, n):
                act.wait_ge(l.hid_summed, l.M * t + n + 1)
                wait(act, l.hid_lo, l.M * t + n - 3)
                f(hid[n % 4][:, :], psH[n % 2][:, 0:T], (ACT.Relu, ACT.Gelu)[l.i], scale=l.un_up,
                  bias=l.b1[:, n // l.HC, n % l.HC:n % l.HC + 1]).then_inc(l.hid_active, 1)

            def hidden_high(l, t, n):
                act.wait_ge(l.hid_scaled, l.M * t + n + 1)
                wait(act, l.hid_used, l.M * t + n - 1)
                f(hsc[n % 2][:, 0, :], hid[n % 4][:, :], ACT.Copy).then_inc(l.hid_hi, 1)

            def matrix_high(l, k):
                wait(act, l.w_lo, k)
                f(l.part(k, 0), l.raw(k), ACT.Copy, scale=l.s_w1 if k < NX else l.s_w2)\
                    .then_inc(l.w_hi, 1)

            def sum_copied(l, tt):
                act.wait_ge(l.hid_used, l.M * tt + l.M)
                wait(act, l.ytok_summed, 2 * tt)
                f(yT[:, 0, :], psY[0][:, 0:T], ACT.Copy, scale=l.un_y)
                f(yT[:, 1, :], psY[1][:, 0:T], ACT.Copy, scale=l.un_y).then_inc(l.y_copied, 1)

            def result_deviation(tt):
                act.wait_ge(s_ln2m, tt + 1)
                root(1, s_ln2s)

            def result_copied(tt, final=False):
                act.wait_ge(L[0].lin_summed, 2 * NT if final else 2 * tt + 4)
                for k in range(KD):
                    copied(x2T[:, k, :], k, s_x2Ts, 2 * tt + k + 1, s_x2T)

            def projected(tt):
                act.wait_ge(s_hraw, tt + 1)
                wait(act, s_hTw, 16 * tt)
                wait(act, s_hps, tt)
                f(hT[:, :], psM[0][:, 0:T], ACT.Relu, bias=bp[:, :]).then_inc(s_hT, 1)

            def squared(tt):
                act.wait_ge(s_hps, tt + 1)
                wait(act, s_hpw, 16 * tt)
                f(hp[:, :, :].rearrange("p s d -> p (s d)"), psM[1][0:PT, :], ACT.Square)\
                    .then_inc(s_hp, 1)

            act.wait_ge(s_wl, 16 * SMALL)
            for l in L:
                act.wait_ge(l.scales_ready, 1)
                for k in range(2 * NX):
                    matrix_high(l, k)
                if l.i == 0:
                    feat_copied(l, 0)
                else:
                    take_root(l, 0)
                deviation(l, 0)
                normed_copied(l, 0, 0)
                exponent(l, 0)
                weights_copied(l, 0, 0)
                active(l, 0, 0)

                def tile(t, q, first, last, more):
                    for n in range(l.M):
                        if n + 1 < l.M:
                            active(l, t, n + 1)
                        elif not last:
                            active(l, t + 1, 0)
                        hidden_high(l, t, n)
                        if n == 0 and not first:
                            sum_copied(l, t - 1)
                        if l.i == 0 and not first:
                            if n == 4:
                                result_deviation(t - 1)
                            if n == 7:
                                result_copied(t - 1)
                            if n == 10:
                                projected(t - 1)
                            if n == 12:
                                squared(t - 1)
                        if last:
                            continue
                        if n == l.at_feat + 1 and l.i == 0:
                            feat_copied(l, t + 1)
                        if n == l.at_take + 1 and l.i == 1:
                            take_root(l, t + 1)
                        if n == l.at_lin + 2:
                            deviation(l, t + 1)
                        if n == l.at_norm + 1:
                            normed_copied(l, t + 1, 1 - q)
                        if n == l.at_gate + 1:
                            exponent(l, t + 1)
                        if n == l.at_comb + 1:
                            weights_copied(l, t + 1, 1 - q)

                iteration(l, tile, Chain(act, s_act), 0)
                sum_copied(l, NT - 1)
                if l.i == 0:
                    result_deviation(NT - 1)
                    result_copied(NT - 1, final=True)
                    projected(NT - 1)
                    squared(NT - 1)


def laid_out(inputs, n_nodes, n_edges):
    NT, NG = shapes(n_nodes, n_edges)
    EP = NG * GE

    def arr(name):
        return np.ascontiguousarray(inputs[name])

    def edges(x, fill):
        x = np.concatenate([x.reshape(-1), np.full(EP - n_edges, fill, x.dtype)])
        return np.ascontiguousarray(x.reshape(NG * SUB, P).T)

    def chunks(w):
        return np.ascontiguousarray(w.reshape(-1, P, w.shape[1]).transpose(1, 0, 2))

    def experts(w):
        return np.ascontiguousarray(w.reshape(NX, -1, P, w.shape[2]).transpose(2, 0, 1, 3))

    def columns(b):
        return np.ascontiguousarray(b.reshape(NX, -1, P).transpose(2, 0, 1))

    f32 = np.float32
    spread = np.zeros((3, NX, NX, P), f32)
    partmask = np.zeros((3, 3 * NX, 3), f32)
    for e in range(NX):
        spread[:, e, e, :] = 1
    for j in range(3):
        partmask[j, :, j] = 1
    stage = [T * max(0, (g - LAG) // GPT) for g in range(NG)]
    return {
        "x": np.concatenate([arr("x"), np.zeros((NT * T - n_nodes, D), f32)]),
        "src": edges(arr("src"), 0), "dst": edges(arr("dst"), n_nodes),
        "w0": edges(arr("edge_weight1"), 0), "w1": edges(arr("edge_weight"), 0),
        "gnn0_w": chunks(arr("L0_gnn_W").T), "gnn0_b": arr("L0_gnn_b").reshape(1, D),
        "wg0": chunks(arr("L0_ffn_Wg")), "bg": arr("L0_ffn_bg").reshape(1, NX),
        "bias": arr("L0_ffn_bias").reshape(1, NX),
        "w1_0": experts(arr("L0_ffn_W1")), "b1_0": columns(arr("L0_ffn_b1")),
        "w2_0": experts(arr("L0_ffn_W2")), "b2_0": arr("L0_ffn_b2"),
        "wp": chunks(arr("L1_gnn_Wp").T), "bp": arr("L1_gnn_bp").reshape(P, 1),
        "gnn1_w": np.ascontiguousarray(np.stack([arr("L1_gnn_W1").T, arr("L1_gnn_W2").T], 1)),
        "gnn1_b1": arr("L1_gnn_b1").reshape(1, D), "gnn1_b2": arr("L1_gnn_b2").reshape(1, D),
        "wg1": chunks(arr("L1_ffn_router_w").T),
        "w1_1": experts(arr("L1_ffn_w1")), "b1_1": columns(arr("L1_ffn_b1")),
        "w2_1": experts(arr("L1_ffn_w2")), "b2_1": arr("L1_ffn_b2"),
        "ident": np.eye(P, dtype=f32),
        "iota": np.tile(np.arange(T, dtype=f32), (P, 1)),
        "lower": np.tile(np.tril(np.ones((NX, NX), f32), -1).reshape(1, -1), (P, 1)),
        "spread": spread.reshape(3 * NX, NX * P),
        "partmask": partmask.reshape(9 * NX, 3),
        "floor": np.tile(np.array(stage, f32), (P, 1)),
    }


def kernel(**inputs):
    import concourse.bacc as bacc
    from concourse.bass_utils import run_bass_kernel_spmd

    n_nodes, n_edges = inputs["x"].shape[0], inputs["src"].shape[0]
    arrays = laid_out(inputs, n_nodes, n_edges)
    nc = bacc.Bacc("TRN2", target_bir_lowering=False, num_devices=1)
    aps = {k: nc.dram_tensor(k + "_in", v.shape, mybir.dt.from_np(v.dtype), kind="ExternalInput").ap()
           for k, v in arrays.items()}
    aps["out"] = nc.dram_tensor("out_dram", (n_nodes, D), F32, kind="ExternalOutput").ap()
    build_program(nc, aps, n_nodes, n_edges)
    r = run_bass_kernel_spmd(nc, [{k + "_in": v for k, v in arrays.items()}], core_ids=[0])
    return r.results[0]["out_dram"]
```
